# Optimizing a Trainium2 kernel written in Bass

```python
import numpy as np
import jax
import jax.numpy as jnp

def _softmax(x, axis=-1):
    return jax.nn.softmax(x, axis=axis)

def _gelu(x):
    return jax.nn.gelu(x, approximate=True)

def _silu(x):
    return jax.nn.silu(x)

def _sigmoid(x):
    return jax.nn.sigmoid(x)

def _layernorm(x, axis=-1, eps=1e-05):
    m = jnp.mean(x, axis=axis, keepdims=True)
    v = jnp.var(x, axis=axis, keepdims=True)
    return (x - m) / jnp.sqrt(v + eps)

def _scatter_add(tgt, idx, src, axis=0):
    return tgt.at[idx].add(src)

def _segment_sum(src, seg, n):
    return jax.ops.segment_sum(src, seg, n)
kernel_name = 'mk_xattn_ffn_d4_seqx_r4_b1e87c'

def setup_inputs(seed: int=0):
    np.random.seed(seed)
    _w = jnp.asarray

    def _rec_inputs():
        import jax
        import jax.numpy as jnp
        _rk = jax.random.key(seed)
        x = -0.0002928 + 1 * jax.random.normal(jax.random.fold_in(_rk, 1), (16, 256, 256), jnp.float32)
        _lenS = 256 - jax.random.randint(jax.random.fold_in(_rk, 7), (16,), 0, max(1, 256 // 4) + 1, jnp.int32)
        _lenS2 = 77 - jax.random.randint(jax.random.fold_in(_rk, 8), (16,), 0, max(1, 77 // 4) + 1, jnp.int32)
        _ctx_1024P = jax.random.normal(jax.random.fold_in(_rk, 11), (16, 16, 256), jnp.float32)
        _ctx_1024c = jax.random.dirichlet(jax.random.fold_in(_rk, 511), 0.3 * jnp.ones((16,), jnp.float32), (16, 77))
        _ctx_1024t = jnp.einsum('bsk,bkd->bsd', _ctx_1024c, _ctx_1024P)
        _ctx_1024t = _ctx_1024t * jax.lax.rsqrt(jnp.mean(jnp.square(_ctx_1024t)) + 1e-12) * 0.953939
        ctx_1024 = -1.39393e-06 + 0.999914 * (_ctx_1024t + 0.3 * jax.random.normal(jax.random.fold_in(_rk, 611), (16, 77, 256), jnp.float32))
        _validS = jnp.arange(256)[None, :] < _lenS[:, None]
        _validS2 = jnp.arange(77)[None, :] < _lenS2[:, None]
        _causal = jnp.tril(jnp.ones((256, 256), dtype=bool))
        mask_1x1xSxS2_bk0 = jnp.logical_not(jnp.broadcast_to(_validS2[0:1, None, None, :], (1, 1, 256, 77)))
        return (x, ctx_1024, mask_1x1xSxS2_bk0)
    x, ctx_1024, mask_1x1xSxS2_bk0 = _rec_inputs()

    def _L0_xattn_setup():
        import jax, jax.numpy as jnp
        import numpy as np
        EMB = 256
        HEADS = 16
        HEAD_DIM = EMB // HEADS
        B, S = (2, 512)
        key = jax.random.key(seed)
        ks = jax.random.split(key, 11)
        scale = 1.0 / np.sqrt(EMB)
        inp = {'query': jax.random.normal(ks[0], (B, S, EMB), jnp.float32), 'key': jax.random.normal(ks[1], (B, S, EMB), jnp.float32), 'value': jax.random.normal(ks[2], (B, S, EMB), jnp.float32), 'Wq': jax.random.normal(ks[3], (EMB, EMB), jnp.float32) * scale, 'bq': jnp.zeros((EMB,), jnp.float32), 'Wk': jax.random.normal(ks[4], (EMB, EMB), jnp.float32) * scale, 'bk': jnp.zeros((EMB,), jnp.float32), 'Wv': jax.random.normal(ks[5], (EMB, EMB), jnp.float32) * scale, 'bv': jnp.zeros((EMB,), jnp.float32), 'Wo': jax.random.normal(ks[6], (EMB, EMB), jnp.float32) * scale, 'bo': jnp.zeros((EMB,), jnp.float32)}
        return inp
    _L0_xattn_all = _L0_xattn_setup()
    _L0_xattn_in = {k: v for k, v in _L0_xattn_all.items() if k in ('Wq', 'bq', 'Wk', 'bk', 'Wv', 'bv', 'Wo', 'bo')}
    del _L0_xattn_all

    def _L0_ffn_setup():
        import jax, jax.numpy as jnp
        import numpy as np
        B, T, D = (2, 512, 256)
        DCD = 1024
        RET = 128
        NEXP = 1024
        NKEYS = 64
        H = 4
        KPH = 8
        key = jax.random.key(seed)
        ks = jax.random.split(key, 10)
        s = lambda k, shape, scale: jax.random.normal(k, shape, jnp.float32) * scale
        return {'hidden_states': jax.random.normal(ks[0], (B, T, D), jnp.float32), 'Wg': s(ks[1], (D, DCD), 0.02), 'bg': jnp.zeros((DCD,), jnp.float32), 'Wu': s(ks[2], (D, DCD), 0.02), 'bu': jnp.zeros((DCD,), jnp.float32), 'Wd': s(ks[3], (DCD, D), 0.02), 'bd': jnp.zeros((D,), jnp.float32), 'Wq': s(ks[4], (D, RET * H), 0.02), 'keys': s(ks[5], (H, NKEYS, 2, RET // 2), 0.02), 'down_embed': s(ks[6], (NEXP, D), 0.02), 'up_embed': s(ks[7], (NEXP, D), 0.02)}
    _L0_ffn_all = _L0_ffn_setup()
    _L0_ffn_in = {k: v for k, v in _L0_ffn_all.items() if k in ('Wg', 'bg', 'Wu', 'bu', 'Wd', 'bd', 'Wq', 'keys', 'down_embed', 'up_embed')}
    del _L0_ffn_all

    def _L1_xattn_setup():
        import jax, jax.numpy as jnp
        import numpy as np
        EMBED = 256
        B, S = (4, 1024)
        INV_SCALE = float(EMBED ** 0.5)
        key = jax.random.key(seed)
        ks = jax.random.split(key, 6)
        std = 1.0 / np.sqrt(EMBED)
        return {'query': jax.random.normal(ks[0], (B, S, EMBED), jnp.float32), 'key': jax.random.normal(ks[1], (B, S, EMBED), jnp.float32), 'value': jax.random.normal(ks[2], (B, S, EMBED), jnp.float32), 'Wq': jax.random.normal(ks[3], (EMBED, EMBED), jnp.float32) * std, 'bq': jnp.zeros((EMBED,), jnp.float32), 'Wk': jax.random.normal(ks[4], (EMBED, EMBED), jnp.float32) * std, 'bk': jnp.zeros((EMBED,), jnp.float32), 'Wv': jax.random.normal(ks[5], (EMBED, EMBED), jnp.float32) * std, 'bv': jnp.zeros((EMBED,), jnp.float32)}
    _L1_xattn_all = _L1_xattn_setup()
    _L1_xattn_in = {k: v for k, v in _L1_xattn_all.items() if k in ('Wq', 'bq', 'Wk', 'bk', 'Wv', 'bv')}
    del _L1_xattn_all

    def _L1_ffn_setup():
        import jax, jax.numpy as jnp
        import numpy as np
        DIM = 256
        DEPTH = 2
        HEADS = 8
        DIM_HEAD = 64
        WINDOW = 128
        INNER = HEADS * DIM_HEAD
        HID = int(DIM * 4 * 2 / 3)
        B, N = (2, 2048)
        QK_SCALE = 8.0

        def shift_token(t):
            t1, t2 = jnp.split(t, 2, axis=-1)
            t2 = jnp.pad(t2, ((0, 0), (1, 0), (0, 0)))[:, :-1]
            return jnp.concatenate([t1, t2], axis=-1)

        def l2norm(t):
            return t / jnp.clip(jnp.linalg.norm(t, axis=-1, keepdims=True), 1e-12)

        def rotate_half(x):
            x1, x2 = jnp.split(x, 2, axis=-1)
            return jnp.concatenate([-x2, x1], axis=-1)

        def rotary_xpos(q, k):
            n = q.shape[-2]
            half_idx = jnp.arange(0, DIM_HEAD, 2, dtype=jnp.float32)
            inv_freq = 1.0 / 10000.0 ** (half_idx / DIM_HEAD)
            t = jnp.arange(n, dtype=jnp.float32)
            freqs = t[:, None] * inv_freq[None, :]
            freqs = jnp.concatenate([freqs, freqs], axis=-1)
            base = (half_idx + 0.4 * DIM_HEAD) / (1.4 * DIM_HEAD)
            power = (t - n // 2) / float(WINDOW // 2)
            scale = base[None, :] ** power[:, None]
            scale = jnp.concatenate([scale, scale], axis=-1)
            cos, sin = (jnp.cos(freqs), jnp.sin(freqs))
            q = q * cos * scale + rotate_half(q) * sin * scale
            k = k * cos / scale + rotate_half(k) * sin / scale
            return (q, k)

        def local_attention(q, k, v):
            b, h, n, d = q.shape
            w = n // WINDOW
            bq = q.reshape(b, h, w, WINDOW, d) * QK_SCALE
            bk = k.reshape(b, h, w, WINDOW, d)
            bv = v.reshape(b, h, w, WINDOW, d)

            def look_around(t):
                p = jnp.pad(t, ((0, 0), (0, 0), (1, 0), (0, 0), (0, 0)))
                return jnp.concatenate([p[:, :, :w], p[:, :, 1:]], axis=3)
            bk, bv = (look_around(bk), look_around(bv))
            bt = jnp.arange(n).reshape(w, WINDOW)
            btp = jnp.pad(bt, ((1, 0), (0, 0)), constant_values=-1)
            btk = jnp.concatenate([btp[:w], btp[1:]], axis=1)
            sim = jnp.einsum('bhwid,bhwjd->bhwij', bq, bk)
            i = bt[:, :, None]
            j = btk[:, None, :]
            mask = (i < j) | (i > j + WINDOW) | (j == -1)
            sim = jnp.where(mask, -jnp.finfo(sim.dtype).max, sim)
            attn = jax.nn.softmax(sim, axis=-1)
            out = jnp.einsum('bhwij,bhwjd->bhwid', attn, bv)
            return out.reshape(b, h, n, d)

        def _layer(x, wqkv, qs, ksc, wo, lg, lb, w1, b1, w2, b2):
            b, n, _ = x.shape
            h = shift_token(x)
            qkv = h @ wqkv
            q, k, v = jnp.split(qkv, 3, axis=-1)
            to_heads = lambda t: t.reshape(b, n, HEADS, DIM_HEAD).transpose(0, 2, 1, 3)
            q, k, v = (to_heads(q), to_heads(k), to_heads(v))
            q = l2norm(q) * qs
            k = l2norm(k) * ksc
            q, k = rotary_xpos(q, k)
            o = local_attention(q, k, v)
            o = o.transpose(0, 2, 1, 3).reshape(b, n, INNER)
            x = x + o @ wo
            h = shift_token(x)
            mu = h.mean(-1, keepdims=True)
            var = h.var(-1, keepdims=True)
            h = (h - mu) / jnp.sqrt(var + 1e-05) * lg + lb
            h = h @ w1 + b1
            a, g = jnp.split(h, 2, axis=-1)
            h = a * jax.nn.gelu(g, approximate=False)
            x = x + h @ w2 + b2
            return x
        key = jax.random.key(seed)
        ks = jax.random.split(key, 6)
        return {'x': jax.random.normal(ks[0], (B, N, DIM), jnp.float32), 'wqkv': jax.random.normal(ks[1], (DEPTH, DIM, 3 * INNER), jnp.float32) * 0.02, 'q_scale': jnp.ones((DEPTH, DIM_HEAD), jnp.float32), 'k_scale': jnp.ones((DEPTH, DIM_HEAD), jnp.float32), 'wo': jax.random.normal(ks[2], (DEPTH, INNER, DIM), jnp.float32) * 0.02, 'ln_g': jnp.ones((DEPTH, DIM), jnp.float32), 'ln_b': jnp.zeros((DEPTH, DIM), jnp.float32), 'w1': jax.random.normal(ks[3], (DEPTH, DIM, 2 * HID), jnp.float32) * 0.02, 'b1': jnp.zeros((DEPTH, 2 * HID), jnp.float32), 'w2': jax.random.normal(ks[4], (DEPTH, HID, DIM), jnp.float32) * 0.02, 'b2': jnp.zeros((DEPTH, DIM), jnp.float32)}
    _L1_ffn_all = _L1_ffn_setup()
    _L1_ffn_in = {k: v for k, v in _L1_ffn_all.items() if k in ('wqkv', 'q_scale', 'k_scale', 'wo', 'ln_g', 'ln_b', 'w1', 'b1', 'w2', 'b2')}
    del _L1_ffn_all

    def _L2_xattn_setup():
        import jax, jax.numpy as jnp
        import numpy as np
        B, S, D, H = (4, 512, 256, 16)
        DK = D // H
        key = jax.random.key(seed)
        ks = jax.random.split(key, 8)
        scale = 1.0 / np.sqrt(D)
        q = jax.random.normal(ks[0], (B, S, D), dtype=jnp.float32)
        k = jax.random.normal(ks[1], (B, S, D), dtype=jnp.float32)
        v = jax.random.normal(ks[2], (B, S, D), dtype=jnp.float32)
        W_q = jax.random.normal(ks[3], (D, D), dtype=jnp.float32) * scale
        W_k = jax.random.normal(ks[4], (D, D), dtype=jnp.float32) * scale
        W_v = jax.random.normal(ks[5], (D, D), dtype=jnp.float32) * scale
        W_o = jax.random.normal(ks[6], (D, D), dtype=jnp.float32) * scale
        mask = jnp.tril(jnp.ones((S, S), dtype=bool))[None, None]
        return {'q': q, 'k': k, 'v': v, 'W_q': W_q, 'W_k': W_k, 'W_v': W_v, 'W_o': W_o, 'mask': mask}
    _L2_xattn_all = _L2_xattn_setup()
    _L2_xattn_in = {k: v for k, v in _L2_xattn_all.items() if k in ('W_q', 'W_k', 'W_v', 'W_o')}
    del _L2_xattn_all

    def _L2_ffn_setup():
        import jax, jax.numpy as jnp
        import numpy as np
        EPS = 1e-06
        LN_EPS = 1e-05

        def _absmean_core(W):
            gamma = jnp.mean(jnp.abs(W)) + EPS
            Ws = W / gamma
            Wq = jnp.sign(Ws) * jnp.minimum(jnp.round(jnp.abs(Ws)), 1.0)
            return (Wq, gamma)

        @jax.custom_vjp
        def absmean(W):
            return _absmean_core(W)[0]

        def _absmean_fwd(W):
            Wq, gamma = _absmean_core(W)
            return (Wq, gamma)

        def _absmean_bwd(gamma, g):
            return (g / gamma,)
        absmean.defvjp(_absmean_fwd, _absmean_bwd)

        def layernorm(x, w, b, eps=LN_EPS):
            mu = jnp.mean(x, axis=-1, keepdims=True)
            var = jnp.mean((x - mu) ** 2, axis=-1, keepdims=True)
            return (x - mu) * jax.lax.rsqrt(var + eps) * w + b
        key = jax.random.key(seed)
        k1, k2, k3 = jax.random.split(key, 3)
        d, h = (256, 1024)
        B, T = (8, 512)
        return {'x': jax.random.normal(k1, (B, T, d), jnp.float32), 'W_fc': jax.random.normal(k2, (h, d), jnp.float32), 'ln_w': jnp.ones((h,), jnp.float32), 'ln_b': jnp.zeros((h,), jnp.float32), 'W_proj': jax.random.normal(k3, (d, h), jnp.float32)}
    _L2_ffn_all = _L2_ffn_setup()
    _L2_ffn_in = {k: v for k, v in _L2_ffn_all.items() if k in ('W_fc', 'ln_w', 'ln_b', 'W_proj')}
    del _L2_ffn_all

    def _L3_xattn_setup():
        import jax, jax.numpy as jnp
        import numpy as np
        D_MODEL = 256
        NUM_HEADS = 16
        HEAD_DIM = D_MODEL // NUM_HEADS

        def _split_heads(x, B):
            return x.reshape(B, -1, NUM_HEADS, HEAD_DIM).transpose(0, 2, 1, 3)
        key = jax.random.key(seed)
        ks = jax.random.split(key, 11)
        B, S = (2, 512)
        s = 1.0 / np.sqrt(D_MODEL)
        inp = {'q': jax.random.normal(ks[0], (B, S, D_MODEL), jnp.float32), 'k': jax.random.normal(ks[1], (B, S, D_MODEL), jnp.float32), 'v': jax.random.normal(ks[2], (B, S, D_MODEL), jnp.float32), 'wq': jax.random.normal(ks[3], (D_MODEL, D_MODEL), jnp.float32) * s, 'bq': jnp.zeros((D_MODEL,), jnp.float32), 'wk': jax.random.normal(ks[4], (D_MODEL, D_MODEL), jnp.float32) * s, 'bk': jnp.zeros((D_MODEL,), jnp.float32), 'wv': jax.random.normal(ks[5], (D_MODEL, D_MODEL), jnp.float32) * s, 'bv': jnp.zeros((D_MODEL,), jnp.float32), 'wo': jax.random.normal(ks[6], (D_MODEL, D_MODEL), jnp.float32) * s, 'bo': jnp.zeros((D_MODEL,), jnp.float32)}
        return inp
    _L3_xattn_all = _L3_xattn_setup()
    _L3_xattn_in = {k: v for k, v in _L3_xattn_all.items() if k in ('wq', 'bq', 'wk', 'bk', 'wv', 'bv', 'wo', 'bo')}
    del _L3_xattn_all

    def _L3_ffn_setup():
        import jax, jax.numpy as jnp
        import numpy as np
        D, H, O, E, K = (256, 512, 256, 8, 2)
        B, S = (4, 256)
        key = jax.random.key(seed)
        ks = jax.random.split(key, 8)
        scale = 0.02
        return {'hidden_states': jax.random.normal(ks[0], (B, S, D), jnp.float32), 'router_w': jax.random.normal(ks[1], (E, D), jnp.float32) * scale, 'sg': jax.random.normal(ks[2], (H, D), jnp.float32) * scale, 'su': jax.random.normal(ks[3], (H, D), jnp.float32) * scale, 'sd': jax.random.normal(ks[4], (O, H), jnp.float32) * scale, 'eg': jax.random.normal(ks[5], (E, H, D), jnp.float32) * scale, 'eu': jax.random.normal(ks[6], (E, H, D), jnp.float32) * scale, 'ed': jax.random.normal(ks[7], (E, O, H), jnp.float32) * scale}
    _L3_ffn_all = _L3_ffn_setup()
    _L3_ffn_in = {k: v for k, v in _L3_ffn_all.items() if k in ('router_w', 'sg', 'su', 'sd', 'eg', 'eu', 'ed')}
    del _L3_ffn_all
    return {'x': x, 'ctx_1024': ctx_1024, 'mask_1x1xSxS2_bk0': mask_1x1xSxS2_bk0, 'L0_xattn_Wq': _L0_xattn_in['Wq'], 'L0_xattn_bq': _L0_xattn_in['bq'], 'L0_xattn_Wk': _L0_xattn_in['Wk'], 'L0_xattn_bk': _L0_xattn_in['bk'], 'L0_xattn_Wv': _L0_xattn_in['Wv'], 'L0_xattn_bv': _L0_xattn_in['bv'], 'L0_xattn_Wo': _L0_xattn_in['Wo'], 'L0_xattn_bo': _L0_xattn_in['bo'], 'L0_ffn_Wg': _L0_ffn_in['Wg'], 'L0_ffn_bg': _L0_ffn_in['bg'], 'L0_ffn_Wu': _L0_ffn_in['Wu'], 'L0_ffn_bu': _L0_ffn_in['bu'], 'L0_ffn_Wd': _L0_ffn_in['Wd'], 'L0_ffn_bd': _L0_ffn_in['bd'], 'L0_ffn_Wq': _L0_ffn_in['Wq'], 'L0_ffn_keys': _L0_ffn_in['keys'], 'L0_ffn_down_embed': _L0_ffn_in['down_embed'], 'L0_ffn_up_embed': _L0_ffn_in['up_embed'], 'L1_xattn_Wq': _L1_xattn_in['Wq'], 'L1_xattn_bq': _L1_xattn_in['bq'], 'L1_xattn_Wk': _L1_xattn_in['Wk'], 'L1_xattn_bk': _L1_xattn_in['bk'], 'L1_xattn_Wv': _L1_xattn_in['Wv'], 'L1_xattn_bv': _L1_xattn_in['bv'], 'L1_ffn_wqkv': _L1_ffn_in['wqkv'], 'L1_ffn_q_scale': _L1_ffn_in['q_scale'], 'L1_ffn_k_scale': _L1_ffn_in['k_scale'], 'L1_ffn_wo': _L1_ffn_in['wo'], 'L1_ffn_ln_g': _L1_ffn_in['ln_g'], 'L1_ffn_ln_b': _L1_ffn_in['ln_b'], 'L1_ffn_w1': _L1_ffn_in['w1'], 'L1_ffn_b1': _L1_ffn_in['b1'], 'L1_ffn_w2': _L1_ffn_in['w2'], 'L1_ffn_b2': _L1_ffn_in['b2'], 'L2_xattn_W_q': _L2_xattn_in['W_q'], 'L2_xattn_W_k': _L2_xattn_in['W_k'], 'L2_xattn_W_v': _L2_xattn_in['W_v'], 'L2_xattn_W_o': _L2_xattn_in['W_o'], 'L2_ffn_W_fc': _L2_ffn_in['W_fc'], 'L2_ffn_ln_w': _L2_ffn_in['ln_w'], 'L2_ffn_ln_b': _L2_ffn_in['ln_b'], 'L2_ffn_W_proj': _L2_ffn_in['W_proj'], 'L3_xattn_wq': _L3_xattn_in['wq'], 'L3_xattn_bq': _L3_xattn_in['bq'], 'L3_xattn_wk': _L3_xattn_in['wk'], 'L3_xattn_bk': _L3_xattn_in['bk'], 'L3_xattn_wv': _L3_xattn_in['wv'], 'L3_xattn_bv': _L3_xattn_in['bv'], 'L3_xattn_wo': _L3_xattn_in['wo'], 'L3_xattn_bo': _L3_xattn_in['bo'], 'L3_ffn_router_w': _L3_ffn_in['router_w'], 'L3_ffn_sg': _L3_ffn_in['sg'], 'L3_ffn_su': _L3_ffn_in['su'], 'L3_ffn_sd': _L3_ffn_in['sd'], 'L3_ffn_eg': _L3_ffn_in['eg'], 'L3_ffn_eu': _L3_ffn_in['eu'], 'L3_ffn_ed': _L3_ffn_in['ed']}

def reference(x, ctx_1024, mask_1x1xSxS2_bk0, L0_xattn_Wq, L0_xattn_bq, L0_xattn_Wk, L0_xattn_bk, L0_xattn_Wv, L0_xattn_bv, L0_xattn_Wo, L0_xattn_bo, L0_ffn_Wg, L0_ffn_bg, L0_ffn_Wu, L0_ffn_bu, L0_ffn_Wd, L0_ffn_bd, L0_ffn_Wq, L0_ffn_keys, L0_ffn_down_embed, L0_ffn_up_embed, L1_xattn_Wq, L1_xattn_bq, L1_xattn_Wk, L1_xattn_bk, L1_xattn_Wv, L1_xattn_bv, L1_ffn_wqkv, L1_ffn_q_scale, L1_ffn_k_scale, L1_ffn_wo, L1_ffn_ln_g, L1_ffn_ln_b, L1_ffn_w1, L1_ffn_b1, L1_ffn_w2, L1_ffn_b2, L2_xattn_W_q, L2_xattn_W_k, L2_xattn_W_v, L2_xattn_W_o, L2_ffn_W_fc, L2_ffn_ln_w, L2_ffn_ln_b, L2_ffn_W_proj, L3_xattn_wq, L3_xattn_bq, L3_xattn_wk, L3_xattn_bk, L3_xattn_wv, L3_xattn_bv, L3_xattn_wo, L3_xattn_bo, L3_ffn_router_w, L3_ffn_sg, L3_ffn_su, L3_ffn_sd, L3_ffn_eg, L3_ffn_eu, L3_ffn_ed):
    import jax
    import jax.numpy as jnp

    def _L0_xattn_ref(query, key, value, Wq, bq, Wk, bk, Wv, bv, Wo, bo):
        import jax, jax.numpy as jnp
        import numpy as np
        EMB = 256
        HEADS = 16
        HEAD_DIM = EMB // HEADS
        B, S = (2, 512)
        b = query.shape[0]

        def proj(x, W, bias):
            y = jnp.einsum('bse,ef->bsf', x, W) + bias
            return y.reshape(b, -1, HEADS, HEAD_DIM).transpose(0, 2, 1, 3)
        Q = proj(query, Wq, bq)
        K = proj(key, Wk, bk)
        V = proj(value, Wv, bv)
        scores = jnp.einsum('bhqd,bhkd->bhqk', Q, K) / np.sqrt(HEAD_DIM).astype(np.float32)
        weights = jax.nn.softmax(scores, axis=-1)
        ctx = jnp.einsum('bhqk,bhkd->bhqd', weights, V)
        ctx = ctx.transpose(0, 2, 1, 3).reshape(b, -1, EMB)
        return jnp.einsum('bse,ef->bsf', ctx, Wo) + bo

    def _L0_ffn_ref(hidden_states, Wg, bg, Wu, bu, Wd, bd, Wq, keys, down_embed, up_embed):
        import jax, jax.numpy as jnp
        import numpy as np
        B, T, D = (2, 512, 256)
        DCD = 1024
        RET = 128
        NEXP = 1024
        NKEYS = 64
        H = 4
        KPH = 8
        b, t, d = hidden_states.shape
        q = (hidden_states @ Wq).reshape(b, t, 2, H, RET // 2)
        sim = jnp.einsum('btphn,hkpn->pbthk', q, keys)
        sc, ix = jax.lax.top_k(sim, KPH)
        sx, sy = (sc[0], sc[1])
        ixx, ixy = (ix[0], ix[1])
        all_sc = (sx[..., :, None] + sy[..., None, :]).reshape(b, t, H, KPH * KPH)
        all_ix = (ixx[..., :, None] * NKEYS + ixy[..., None, :]).reshape(b, t, H, KPH * KPH)
        scores, pk = jax.lax.top_k(all_sc, KPH)
        idx = jnp.take_along_axis(all_ix, pk, axis=-1)
        de = down_embed[idx]
        ue = up_embed[idx]
        w = jnp.einsum('btd,bthkd->bthk', hidden_states, de)
        w = jax.nn.silu(w) * jax.nn.softmax(scores, axis=-1)
        experts_states = jnp.einsum('bthk,bthkd->btd', w, ue)
        mlp = jax.nn.silu(hidden_states @ Wg + bg) * (hidden_states @ Wu + bu) @ Wd + bd
        return mlp + experts_states

    def _L1_xattn_ref(query, key, value, Wq, bq, Wk, bk, Wv, bv):
        import jax, jax.numpy as jnp
        import numpy as np
        EMBED = 256
        B, S = (4, 1024)
        INV_SCALE = float(EMBED ** 0.5)
        q = jnp.einsum('bsd,ed->bse', query, Wq) + bq
        k = jnp.einsum('bsd,ed->bse', key, Wk) + bk
        v = jnp.einsum('bsd,ed->bse', value, Wv) + bv
        scores = jnp.einsum('bqe,bke->bqk', q, k) / INV_SCALE
        probs = jax.nn.softmax(scores, axis=-1)
        return jnp.einsum('bqk,bke->bqe', probs, v)

    def _L1_ffn_ref(x, wqkv, q_scale, k_scale, wo, ln_g, ln_b, w1, b1, w2, b2):
        import jax, jax.numpy as jnp
        import numpy as np
        DIM = 256
        DEPTH = 2
        HEADS = 8
        DIM_HEAD = 64
        WINDOW = 128
        INNER = HEADS * DIM_HEAD
        HID = int(DIM * 4 * 2 / 3)
        B, N = (2, 2048)
        QK_SCALE = 8.0

        def shift_token(t):
            t1, t2 = jnp.split(t, 2, axis=-1)
            t2 = jnp.pad(t2, ((0, 0), (1, 0), (0, 0)))[:, :-1]
            return jnp.concatenate([t1, t2], axis=-1)

        def l2norm(t):
            return t / jnp.clip(jnp.linalg.norm(t, axis=-1, keepdims=True), 1e-12)

        def rotate_half(x):
            x1, x2 = jnp.split(x, 2, axis=-1)
            return jnp.concatenate([-x2, x1], axis=-1)

        def rotary_xpos(q, k):
            n = q.shape[-2]
            half_idx = jnp.arange(0, DIM_HEAD, 2, dtype=jnp.float32)
            inv_freq = 1.0 / 10000.0 ** (half_idx / DIM_HEAD)
            t = jnp.arange(n, dtype=jnp.float32)
            freqs = t[:, None] * inv_freq[None, :]
            freqs = jnp.concatenate([freqs, freqs], axis=-1)
            base = (half_idx + 0.4 * DIM_HEAD) / (1.4 * DIM_HEAD)
            power = (t - n // 2) / float(WINDOW // 2)
            scale = base[None, :] ** power[:, None]
            scale = jnp.concatenate([scale, scale], axis=-1)
            cos, sin = (jnp.cos(freqs), jnp.sin(freqs))
            q = q * cos * scale + rotate_half(q) * sin * scale
            k = k * cos / scale + rotate_half(k) * sin / scale
            return (q, k)

        def local_attention(q, k, v):
            b, h, n, d = q.shape
            w = n // WINDOW
            bq = q.reshape(b, h, w, WINDOW, d) * QK_SCALE
            bk = k.reshape(b, h, w, WINDOW, d)
            bv = v.reshape(b, h, w, WINDOW, d)

            def look_around(t):
                p = jnp.pad(t, ((0, 0), (0, 0), (1, 0), (0, 0), (0, 0)))
                return jnp.concatenate([p[:, :, :w], p[:, :, 1:]], axis=3)
            bk, bv = (look_around(bk), look_around(bv))
            bt = jnp.arange(n).reshape(w, WINDOW)
            btp = jnp.pad(bt, ((1, 0), (0, 0)), constant_values=-1)
            btk = jnp.concatenate([btp[:w], btp[1:]], axis=1)
            sim = jnp.einsum('bhwid,bhwjd->bhwij', bq, bk)
            i = bt[:, :, None]
            j = btk[:, None, :]
            mask = (i < j) | (i > j + WINDOW) | (j == -1)
            sim = jnp.where(mask, -jnp.finfo(sim.dtype).max, sim)
            attn = jax.nn.softmax(sim, axis=-1)
            out = jnp.einsum('bhwij,bhwjd->bhwid', attn, bv)
            return out.reshape(b, h, n, d)

        def _layer(x, wqkv, qs, ksc, wo, lg, lb, w1, b1, w2, b2):
            b, n, _ = x.shape
            h = shift_token(x)
            qkv = h @ wqkv
            q, k, v = jnp.split(qkv, 3, axis=-1)
            to_heads = lambda t: t.reshape(b, n, HEADS, DIM_HEAD).transpose(0, 2, 1, 3)
            q, k, v = (to_heads(q), to_heads(k), to_heads(v))
            q = l2norm(q) * qs
            k = l2norm(k) * ksc
            q, k = rotary_xpos(q, k)
            o = local_attention(q, k, v)
            o = o.transpose(0, 2, 1, 3).reshape(b, n, INNER)
            x = x + o @ wo
            h = shift_token(x)
            mu = h.mean(-1, keepdims=True)
            var = h.var(-1, keepdims=True)
            h = (h - mu) / jnp.sqrt(var + 1e-05) * lg + lb
            h = h @ w1 + b1
            a, g = jnp.split(h, 2, axis=-1)
            h = a * jax.nn.gelu(g, approximate=False)
            x = x + h @ w2 + b2
            return x
        for l in range(DEPTH):
            x = _layer(x, wqkv[l], q_scale[l], k_scale[l], wo[l], ln_g[l], ln_b[l], w1[l], b1[l], w2[l], b2[l])
        return x

    def _L2_xattn_ref(q, k, v, W_q, W_k, W_v, W_o, mask):
        import jax, jax.numpy as jnp
        import numpy as np
        B, S, D, H = (4, 512, 256, 16)
        DK = D // H
        b, sq, _ = q.shape
        sk = k.shape[1]
        Q = (q @ W_q).reshape(b, sq, H, DK).transpose(0, 2, 1, 3)
        K = (k @ W_k).reshape(b, sk, H, DK).transpose(0, 2, 1, 3)
        V = (v @ W_v).reshape(b, sk, H, DK).transpose(0, 2, 1, 3)
        scores = jnp.einsum('bhqd,bhkd->bhqk', Q, K) / jnp.sqrt(jnp.float32(DK))
        scores = jnp.where(mask, scores, jnp.float32(-1000000000.0))
        attn = jax.nn.softmax(scores, axis=-1)
        out = jnp.einsum('bhqk,bhkd->bhqd', attn, V)
        out = out.transpose(0, 2, 1, 3).reshape(b, sq, D)
        return out @ W_o

    def _L2_ffn_ref(x, W_fc, ln_w, ln_b, W_proj):
        import jax, jax.numpy as jnp
        import numpy as np
        EPS = 1e-06
        LN_EPS = 1e-05

        def _absmean_core(W):
            gamma = jnp.mean(jnp.abs(W)) + EPS
            Ws = W / gamma
            Wq = jnp.sign(Ws) * jnp.minimum(jnp.round(jnp.abs(Ws)), 1.0)
            return (Wq, gamma)

        @jax.custom_vjp
        def absmean(W):
            return _absmean_core(W)[0]

        def _absmean_fwd(W):
            Wq, gamma = _absmean_core(W)
            return (Wq, gamma)

        def _absmean_bwd(gamma, g):
            return (g / gamma,)
        absmean.defvjp(_absmean_fwd, _absmean_bwd)

        def layernorm(x, w, b, eps=LN_EPS):
            mu = jnp.mean(x, axis=-1, keepdims=True)
            var = jnp.mean((x - mu) ** 2, axis=-1, keepdims=True)
            return (x - mu) * jax.lax.rsqrt(var + eps) * w + b
        h = jnp.einsum('btd,hd->bth', x, absmean(W_fc))
        h = jax.nn.gelu(h, approximate=False)
        h = layernorm(h, ln_w, ln_b)
        return jnp.einsum('bth,dh->btd', h, absmean(W_proj))

    def _L3_xattn_ref(q, k, v, wq, bq, wk, bk, wv, bv, wo, bo):
        import jax, jax.numpy as jnp
        import numpy as np
        D_MODEL = 256
        NUM_HEADS = 16
        HEAD_DIM = D_MODEL // NUM_HEADS

        def _split_heads(x, B):
            return x.reshape(B, -1, NUM_HEADS, HEAD_DIM).transpose(0, 2, 1, 3)
        B = q.shape[0]
        qh = _split_heads(q @ wq + bq, B)
        kh = _split_heads(k @ wk + bk, B)
        vh = _split_heads(v @ wv + bv, B)
        scale = 1.0 / np.sqrt(HEAD_DIM).astype(np.float32)
        scores = jnp.einsum('bhqd,bhkd->bhqk', qh, kh) * scale
        probs = jax.nn.softmax(scores, axis=-1)
        out = jnp.einsum('bhqk,bhkd->bhqd', probs, vh)
        out = out.transpose(0, 2, 1, 3).reshape(B, -1, D_MODEL)
        return out @ wo + bo

    def _L3_ffn_ref(hidden_states, router_w, sg, su, sd, eg, eu, ed):
        import jax, jax.numpy as jnp
        import numpy as np
        D, H, O, E, K = (256, 512, 256, 8, 2)
        B, S = (4, 256)
        b, s, d = hidden_states.shape
        shared_out = jnp.einsum('bsh,oh->bso', jax.nn.silu(jnp.einsum('bsd,hd->bsh', hidden_states, sg)) * jnp.einsum('bsd,hd->bsh', hidden_states, su), sd)
        flat = hidden_states.reshape(-1, d)
        T = flat.shape[0]
        logits = flat @ router_w.T
        probs = jax.nn.softmax(logits.astype(jnp.float32), axis=-1)
        topk_w, topk_idx = jax.lax.top_k(probs, K)
        topk_w = topk_w / jnp.sum(topk_w, axis=-1, keepdims=True)
        topk_w = topk_w.astype(hidden_states.dtype)
        combine = jnp.zeros((T, probs.shape[-1]), hidden_states.dtype)
        combine = combine.at[jnp.arange(T)[:, None], topk_idx].add(topk_w)
        gate = jnp.einsum('td,ehd->teh', flat, eg)
        up = jnp.einsum('td,ehd->teh', flat, eu)
        eout = jnp.einsum('teh,eoh->teo', jax.nn.silu(gate) * up, ed)
        routed = jnp.einsum('teo,te->to', eout, combine)
        return shared_out + routed.reshape(b, s, -1)
    x = x + _L0_xattn_ref(_layernorm(x, axis=-1), ctx_1024, ctx_1024, L0_xattn_Wq, L0_xattn_bq, L0_xattn_Wk, L0_xattn_bk, L0_xattn_Wv, L0_xattn_bv, L0_xattn_Wo, L0_xattn_bo)
    x = x + _L0_ffn_ref(_layernorm(x, axis=-1), L0_ffn_Wg, L0_ffn_bg, L0_ffn_Wu, L0_ffn_bu, L0_ffn_Wd, L0_ffn_bd, L0_ffn_Wq, L0_ffn_keys, L0_ffn_down_embed, L0_ffn_up_embed)
    x = x + _L1_xattn_ref(_layernorm(x, axis=-1), ctx_1024, ctx_1024, L1_xattn_Wq, L1_xattn_bq, L1_xattn_Wk, L1_xattn_bk, L1_xattn_Wv, L1_xattn_bv)
    x = x + _L1_ffn_ref(_layernorm(x, axis=-1), L1_ffn_wqkv, L1_ffn_q_scale, L1_ffn_k_scale, L1_ffn_wo, L1_ffn_ln_g, L1_ffn_ln_b, L1_ffn_w1, L1_ffn_b1, L1_ffn_w2, L1_ffn_b2)
    x = x + _L2_xattn_ref(_layernorm(x, axis=-1), ctx_1024, ctx_1024, L2_xattn_W_q, L2_xattn_W_k, L2_xattn_W_v, L2_xattn_W_o, mask_1x1xSxS2_bk0)
    x = x + _L2_ffn_ref(_layernorm(x, axis=-1), L2_ffn_W_fc, L2_ffn_ln_w, L2_ffn_ln_b, L2_ffn_W_proj)
    x = x + _L3_xattn_ref(_layernorm(x, axis=-1), ctx_1024, ctx_1024, L3_xattn_wq, L3_xattn_bq, L3_xattn_wk, L3_xattn_bk, L3_xattn_wv, L3_xattn_bv, L3_xattn_wo, L3_xattn_bo)
    x = x + _L3_ffn_ref(_layernorm(x, axis=-1), L3_ffn_router_w, L3_ffn_sg, L3_ffn_su, L3_ffn_sd, L3_ffn_eg, L3_ffn_eu, L3_ffn_ed)
    return x

_drawn_inputs = setup_inputs


def setup_inputs(seed=0):
    import zlib

    import numpy as np

    out = dict(_drawn_inputs(seed))
    spreads = {'L0_xattn_bq': (0.0, 0.394),
     'L0_xattn_bk': (0.0, 0.8),
     'L0_xattn_bv': (0.0, 0.1),
     'L0_xattn_bo': (0.0, 0.1),
     'L0_ffn_bg': (0.0, 0.8),
     'L0_ffn_bu': (0.0, 0.8),
     'L0_ffn_bd': (0.0, 0.1),
     'L1_xattn_bq': (0.0, 0.427),
     'L1_xattn_bk': (0.0, 0.8),
     'L1_xattn_bv': (0.0, 0.1),
     'L1_ffn_q_scale': (1.0, 0.6),
     'L1_ffn_k_scale': (1.0, 0.6),
     'L1_ffn_ln_g': (1.0, 0.6),
     'L1_ffn_ln_b': (0.0, 0.8),
     'L1_ffn_b1': (0.0, 0.8),
     'L1_ffn_b2': (0.0, 0.1),
     'L2_ffn_ln_w': (1.0, 0.2),
     'L2_ffn_ln_b': (0.0, 0.1),
     'L3_xattn_bq': (0.0, 0.8),
     'L3_xattn_bk': (0.0, 0.8),
     'L3_xattn_bv': (0.0, 0.8),
     'L3_xattn_bo': (0.0, 0.8)}
    factors = {'L0_ffn_Wq': 8.0,
     'L0_ffn_keys': 8.0,
     'L0_ffn_down_embed': 6.758,
     'L0_ffn_up_embed': 6.573,
     'L3_xattn_wq': 7.22,
     'L3_xattn_wk': 7.134,
     'L3_xattn_wv': 2.836,
     'L3_xattn_wo': 2.733,
     'L3_ffn_router_w': 8.0,
     'L3_ffn_sg': 8.0,
     'L3_ffn_su': 8.0,
     'L3_ffn_sd': 8.0,
     'L3_ffn_eg': 8.0,
     'L3_ffn_eu': 8.0,
     'L3_ffn_ed': 8.0}
    for name, (base, spread) in spreads.items():
        noise = np.random.default_rng([zlib.crc32(name.encode()), seed]).standard_normal(out[name].shape)
        drawn = base * np.exp(spread * noise) if base else spread * noise
        out[name] = jnp.asarray(drawn.astype(out[name].dtype))
    for name, factor in factors.items():
        out[name] = (out[name] * factor).astype(out[name].dtype)
    return out
```

```python
import concourse.bass as bass
from concourse import mybir
from contextlib import ExitStack

F32 = mybir.dt.float32
U8 = mybir.dt.uint8
ALU = mybir.AluOpType
ACT = mybir.ActivationFunctionType
AXIS_X = mybir.AxisListType.X

P = 128
D = 256
KD = D // P
NB = 16
TOK = 256
NT = TOK // P
S2 = 77
H = 16
HD = D // H
GRP = 4
EPS = 1e-5

FF0 = 1024
NEXP = 1024
PH = 4
NKEYS = 64
TOPK = 8
PROWS = NEXP // NKEYS

WH = 8
WD = 64
INNER = WH * WD
HID = 682
NHC = 6
HREM = HID - 5 * P
QK_SCALE = 8.0
MASKED = -1e30

FF2 = 1024
NE = 8
FF3 = 512

STAGES = ["L0x", "L0f", "L1x", "L1a", "L1b", "L2x", "L2f", "L3x", "L3f"]

COLS = dict(L0x_bq=2, L0x_bk=2, L0f_bg=8, L0f_bu=8, L1x_bq=2, L1x_bk=2,
            L1a_g=2, L1a_b=2, L1a_b1a=6, L1a_b1g=6, L1b_g=2, L1b_b=2, L1b_b1a=6, L1b_b1g=6,
            L2f_w=8, L2f_b=8, L3x_bq=2, L3x_bk=2)
ROWS = dict(L0x_bv=D, L0x_bo=D, L0f_bd=D, L1x_bv=D, L1a_b2=D, L1b_b2=D, L1a_qs=WD, L1a_ks=WD,
            L1b_qs=WD, L1b_ks=WD, L3x_bv=D, L3x_bo=D)
CONSTS = dict(iota=NE, ident=P, headmask=P // HD, causal=P, band=2 * P, shift=P, edge=P,
              cos_q=NT * WD, sin_q=NT * WD, cos_k=NT * WD, sin_k=NT * WD)


def places(sizes):
    at, out = 0, {}
    for name, n in sizes.items():
        out[name] = (at, at + n)
        at += n
    return out, at


COL_AT, NCOLS = places(COLS)
ROW_AT, NROWS = places(ROWS)
CONST_AT, NCONSTS = places(CONSTS)

ATTN_W = 4 * KD * D
L1X_W = 3 * KD * D
L1F_W = KD * 3 * INNER + (INNER // P) * D + KD * 2 * HID + NHC * D
L0F_W = 3 * KD * FF0 + KD * 4 * P + 4 * 2 * NKEYS + 2 * KD * NEXP
EXPERT_W = 3 * KD * FF3
ARENA = 39472
AT_L1A = 0
AT_L0F = L1F_W
AT_L1B = AT_L0F
AT_L0X = AT_L0F + L0F_W
AT_L1X = AT_L0X
WORK1 = AT_L0X + ATTN_W
WORK2 = AT_L1B + L1F_W
AT_Z = ARENA - NB * NT * D
AT_EXPERT = 0
EARLY = 7
AT_L2X = EARLY * EXPERT_W
AT_L2F = AT_L2X + ATTN_W
AT_L3X = AT_L2F + 2 * KD * FF2
WORK3 = AT_L3X + ATTN_W
assert AT_L3X == (NE + 1) * EXPERT_W


class Link:

    def __init__(self, make, name):
        self.make, self.name, self.sems = make, name, {}
        self.base, self.uses, self.total = {}, {}, 0

    def sem(self, kind):
        if kind not in self.sems:
            self.sems[kind] = self.make(f"{self.name}_{kind}")
        return self.sems[kind]

    @property
    def ready(self):
        return self.sem("ready")

    @property
    def free(self):
        return self.sem("free")

    def plan(self, stage, uses, nb):
        self.uses[stage] = uses.split()
        self.base[stage] = self.total
        self.total += nb * len(self.uses[stage])

    def n(self, stage, batch, use=None):
        uses = self.uses[stage]
        return self.base[stage] + batch * len(uses) + (uses.index(use) if use else 0)


class Steps:

    def __init__(self):
        self.done = 0

    def one(self):
        self.done += 1
        return 1


def build(nc, a, out, nb=NB, stages=STAGES):
    with ExitStack() as ctx:
        program(nc, a, out, nb, stages, ctx)


def program(nc, a, out, nb, stages, ctx):
    def sem(name):
        return ctx.enter_context(nc.semaphore(name))

    def sbuf(name, shape, dt=F32):
        return ctx.enter_context(nc.sbuf_tensor(name, shape, dt))

    X = sbuf("X", [P, nb, NT, D])
    arena = sbuf("arena", [P, ARENA])
    cols = sbuf("cols", [P, NCOLS])
    rows = sbuf("rows", [P, NROWS])
    consts = sbuf("consts", [P, NCONSTS])
    h = sbuf("h", [P, NT, D])
    hT = sbuf("hT", [P, KD, TOK])
    stats = sbuf("stats", [P, NT, 6])
    moments = sbuf("moments", [P, NT, 2])
    variance = sbuf("variance", [P, NT])
    rstd = sbuf("rstd", [P, NT])
    minus_half = sbuf("minus_half", [P, 2 * NT * WH])
    pad = sbuf("pad", [P, 8])
    pad_act = sbuf("pad_act", [P, 2])
    router = sbuf("router", [P, KD, NE])
    mask_bytes = sbuf("mask_bytes", [P, NT, S2], U8)
    small = sbuf("small", [P, 690])
    psum = ctx.enter_context(nc.psum_tensor("psum", [P, 8, 512], F32))

    def view(at, shape, pattern=None, base=arena, parts=P, **sizes):
        n = 1
        for s in shape:
            n *= s
        v = base[0:parts, at:at + n]
        if len(shape) == 1:
            return v
        names = "abcd"[:len(shape)]
        return v.rearrange(f"p ({' '.join(names)}) -> p {' '.join(names)}", **dict(zip(names[1:], shape[1:])))

    class Area:

        def __init__(self, at, base=arena):
            self.at, self.base = at, base

        def take(self, *shape, parts=P):
            v = view(self.at, shape, base=self.base, parts=parts)
            n = 1
            for s in shape:
                n *= s
            self.at += n
            assert self.at <= self.base.shape[1], self.at
            return v

    def col(name, k=0):
        return cols[:, COL_AT[name][0] + k:COL_AT[name][0] + k + 1]

    def row(name):
        return rows[:, slice(*ROW_AT[name])]

    def const(name):
        return consts[:, slice(*CONST_AT[name])]

    ident = const("ident")

    def bank(b, n=512, parts=P):
        return psum[0:parts, b, 0:n]

    def attn_weights(at):
        area = Area(at)
        return {n: area.take(KD, D) for n in ("wq", "wk", "wv", "wo")}

    W = {"L0x": attn_weights(AT_L0X), "L2x": attn_weights(AT_L2X), "L3x": attn_weights(AT_L3X)}
    area = Area(AT_L1X)
    W["L1x"] = {n: area.take(KD, D) for n in ("wq", "wk", "wv")}
    area = Area(AT_L0F)
    W["L0f"] = dict(wg=area.take(KD, FF0), wu=area.take(KD, FF0), wd=area.take(FF0 // P, D),
                    wq=area.take(KD, 4 * P), keys=area.take(4, 2 * NKEYS),
                    down=area.take(KD, NEXP), up=area.take(NEXP // P, D))
    for s, at in (("L1a", AT_L1A), ("L1b", AT_L1B)):
        area = Area(at)
        W[s] = dict(wqkv=area.take(KD, 3 * INNER), wo=area.take(INNER // P, D),
                    w1=area.take(KD, 2 * HID), w2=area.take(NHC, D))
    area = Area(AT_L2F)
    W["L2f"] = dict(fc=area.take(KD, FF2), proj=area.take(FF2 // P, D))
    area = Area(AT_EXPERT)
    W["L3f"] = [dict(g=area.take(KD, FF3), u=area.take(KD, FF3), d=area.take(FF3 // P, D)) for _ in range(NE + 1)]
    zbuf = view(AT_Z, (NB, NT, D))

    loaded = {s: sem(f"loaded_{s}") for s in ["base"] + list(STAGES) + ["L3f_late"]}
    made = sem("made")
    updated = sem("updated")
    stored = sem("stored")
    dve_steps, act_steps = sem("dve_steps"), sem("act_steps")
    B = [Link(sem, f"bank{b}") for b in range(8)]
    AHEAD = 7
    links = {}

    def link(name):
        if name not in links:
            links[name] = Link(sem, name)
        return links[name]

    variance_l, rstd_l, h_l = link("variance"), link("rstd"), link("h")
    number = {s: n for n, s in enumerate(stages)}

    def batches(eng):
        if nb > 1:
            with eng.Fori(0, nb - 1) as i:
                yield i, True
        yield nb - 1, False

    def begin(eng, s):
        eng.wait_ge(updated, number[s] * nb)

    def plan(s, banks, **others):
        h_l.plan(s, "h", nb)
        for l in (variance_l, rstd_l):
            l.plan(s, "" if s == "L1b" else "h", nb)
        for b, uses in banks.items():
            B[b].plan(s, uses, nb)
        for name, uses in others.items():
            link(name).plan(s, uses, nb)

    FFNS = {}
    zeroed = sem("zeroed")

    def weight_loads(s):
        if s == "L3f_late":
            return [p for e in range(EARLY, NE + 1) for p in expert_loads(e)]
        if s == "L3f":
            return [p for e in range(min(EARLY, NE + 1)) for p in expert_loads(e)] + [(router[:], chunks(a["L3f_router"]))]
        out = []
        for n, dst in W[s].items():
            src = a[f"{s}_{n}"]
            if n == "w2":
                out.append((dst[:, 0:NHC - 1, :], chunks(src[0:(NHC - 1) * P])))
                out.append((dst[0:HREM, NHC - 1, :], src[(NHC - 1) * P:HID]))
            elif n == "keys":
                for q in range(2):
                    r = slice(q * NKEYS, (q + 1) * NKEYS)
                    out.append((dst[r, :, r], src[:, r, :].rearrange("c p k -> p c k")))
            else:
                out.append((dst, chunks(src)))
        return out

    def chunks(src):
        return src.rearrange("(c p) n -> p c n", p=P)

    def expert_loads(e):
        return [(W["L3f"][e][n], chunks(a[f"L3f_{n}"][e])) for n in ("g", "u", "d")]

    LOADS = {s: 16 * len(weight_loads(s)) for s in list(STAGES) + ["L3f_late"]}
    LOADS["base"] = 16 * (nb + 4)
    AFTER = {"L1x": "L0x", "L1b": "L0f", "L2x": "L1b", "L2f": "L1b", "L3x": "L1b", "L3f": "L1b", "L3f_late": "L2f"}
    WHEN = {}
    for s in list(STAGES) + ["L3f_late"]:
        if s.split("_")[0] in stages:
            before = [x for x in stages if s in AFTER and STAGES.index(x) <= STAGES.index(AFTER[s])]
            k = len(before)
            WHEN.setdefault(stages[min(k, len(stages) - 1)], []).append((s, k))

    def load_weights(eng, at):
        for s, k in WHEN.get(at, []):
            if k:
                eng.wait_ge(updated, k * nb)
            if s == "L0f":
                eng.memset(W[s]["keys"], 0.0).then_inc(zeroed, 1)
                eng.wait_ge(zeroed, 1)
            for dst, src in weight_loads(s):
                eng.dma_start(dst, src).then_inc(loaded[s], 16)

    def ln_stats(dve, s, i, step, src):
        for j in range(NT):
            dve.bn_stats(stats[:, j, :], src[:, j, :]).then_inc(dve_steps, step.one())
        dve.wait_ge(dve_steps, step.done)
        dve.memset(pad[:, 0:1], 0.0)
        for j in range(NT):
            dve.bn_aggr(moments[:, j, :], stats[:, j, :]).then_inc(dve_steps, step.one())
        dve.wait_ge(dve_steps, step.done)
        dve.tensor_scalar(variance[:], moments[:, :, 1], EPS, None, ALU.add).then_inc(variance_l.ready, 1)

    def ln_apply(dve, s, i, src):
        dve.wait_ge(rstd_l.ready, rstd_l.n(s, i) + 1)
        dve.wait_ge(B[AHEAD].ready, B[AHEAD].n(s, i, "T"))
        for j in range(NT):
            ins = dve.tensor_scalar(h[:, j, :], src[:, j, :], moments[:, j, 0:1], rstd[:, j:j + 1],
                                    ALU.subtract, ALU.mult)
        ins.then_inc(h_l.ready, 1)

    def ln_power(pool, s, i):
        pool.wait_ge(variance_l.ready, variance_l.n(s, i) + 1)
        pool.tensor_tensor(rstd[:], variance[:], minus_half[:, 0:NT], ALU.pow).then_inc(rstd_l.ready, 1)

    def transpose_h(pe, s, i):
        b = B[AHEAD]
        pe.wait_ge(b.free, b.n(s, i, "T"))
        pe.wait_ge(h_l.ready, h_l.n(s, i) + 1)
        for k in range(KD):
            for j in range(NT):
                ins = pe.transpose(psum[:, AHEAD, k * TOK + j * P:k * TOK + (j + 1) * P],
                                   h[:, j, k * P:(k + 1) * P], ident)
        ins.then_inc(b.ready, 1)

    def copy_hT(act, s, i):
        b = B[AHEAD]
        act.wait_ge(b.ready, b.n(s, i, "T") + 1)
        act.activation(hT[:].rearrange("p a b -> p (a b)"), bank(AHEAD), ACT.Copy).then_inc(b.free, 1)

    def need_hT(pe, s, i):
        b = B[AHEAD]
        pe.wait_ge(b.free, b.n(s, i, "T") + 1)

    def context_load(sp, s, context):
        def load(i):
            sp.dma_start(context, a["ctx"][i, :, :]).then_inc(link("context").ready, 16)
        begin(sp, s)
        load(0)
        if nb > 1:
            with sp.Fori(1, nb) as i:
                sp.wait_ge(B[AHEAD].ready, B[AHEAD].n(s, i - 1, "c") + 1)
                load(i)

    def context_pe(pe, s, i, w, wt):
        b = B[AHEAD]
        pe.wait_ge(link("context").ready, 16 * link("context").n(s, i) + 16)
        pe.wait_ge(b.free, b.n(s, i, "c"))
        for k in range(KD):
            ins = pe.transpose(psum[:, AHEAD, k * S2:(k + 1) * S2], w["context"][:, k * P:(k + 1) * P],
                               ident[0:S2, 0:S2])
        ins.then_inc(b.ready, 1)
        pe.wait_ge(b.free, b.n(s, i, "K"))
        for m in range(KD):
            for k in range(KD):
                ins = pe.matmul(psum[:, AHEAD, m * S2:(m + 1) * S2], wt["wk"][:, k, m * P:(m + 1) * P],
                                w["contextT"][:, k, :], start=k == 0, stop=k == KD - 1)
        ins.then_inc(b.ready, 1)
        pe.wait_ge(b.free, b.n(s, i, "V"))
        for k in range(KD):
            ins = pe.matmul(psum[0:S2, AHEAD, 0:D], w["contextT"][:, k, :], wt["wv"][:, k, :],
                            start=k == 0, stop=k == KD - 1)
        ins.then_inc(b.ready, 1)

    def context_act(act, s, i, w):
        b = B[AHEAD]
        act.wait_ge(b.ready, b.n(s, i, "c") + 1)
        act.activation(w["contextT"].rearrange("p a b -> p (a b)"), psum[:, AHEAD, 0:KD * S2],
                       ACT.Copy).then_inc(b.free, 1)
        act.wait_ge(b.ready, b.n(s, i, "K") + 1)
        if "Kd" in w:
            act.wait_ge(link("Kd").ready, link("Kd").n(s, i))
        for m in range(KD):
            src = psum[:, AHEAD, m * S2:(m + 1) * S2]
            if s + "_bk" in COL_AT:
                ins = act.activation(w["KT"][:, m, :], src, ACT.Identity, bias=col(s + "_bk", m))
            else:
                ins = act.activation(w["KT"][:, m, :], src, ACT.Copy)
        ins.then_inc(b.free, 1)

    def queries_pe(pe, s, i, wt, b):
        need_hT(pe, s, i)
        pe.wait_ge(B[b].free, B[b].n(s, i, "Q"))
        for m in range(KD):
            for k in range(KD):
                ins = pe.matmul(psum[:, b, m * TOK:(m + 1) * TOK], wt["wq"][:, k, m * P:(m + 1) * P],
                                hT[:, k, :], start=k == 0, stop=k == KD - 1)
        ins.then_inc(B[b].ready, 1)

    def queries_act(act, s, i, QT, b):
        act.wait_ge(B[b].ready, B[b].n(s, i, "Q") + 1)
        for m in range(KD):
            src = psum[:, b, m * TOK:(m + 1) * TOK]
            if s + "_bq" in COL_AT:
                ins = act.activation(QT[:, m, :], src, ACT.Identity, bias=col(s + "_bq", m))
            else:
                ins = act.activation(QT[:, m, :], src, ACT.Copy)
        ins.then_inc(B[b].free, 1)

    def cross(s):
        biased, masked = s != "L2x", s == "L2x"
        area = Area(WORK1 if s == "L0x" else WORK3)
        wt = W[s]
        w = dict(context=area.take(D, parts=S2), contextT=area.take(KD, S2), KT=area.take(KD, S2),
                 Kd=area.take(H, S2), V=area.take(H, HD + 1, parts=S2), QT=area.take(KD, TOK))
        Pj, O, OT, PT = [], [], [], []
        for j in range(NT):
            at = area.at
            Pj.append(area.take(H, S2))
            O.append(view(at, (D,)))
            OT.append(view(at + D, (KD, P)))
        for j in range(NT):
            PT.append(area.take(H, P, parts=S2))
        sm = Area(0, small)
        nmax, rden = sm.take(NT, H), sm.take(NT, H)
        keep, fill = sm.take(NT, S2), sm.take(NT, S2)
        Kd, V, QT, KT = w["Kd"], w["V"], w["QT"], w["KT"]
        plan(s, {0: "Q S0 S1", 4: "t00 t02 t10 t12 OT0 Y0", 5: "t01 t03 t11 t13 OT1 Y1", 6: "O0 O1",
                 AHEAD: "T c K V"}, context="c", Kd="K", P="S0 S1", E="S0 S1", O="O0 O1")
        Pl, El, Ol, Kdl = link("P"), link("E"), link("O"), link("Kd")
        scores = psum[:, 0:4, 0:GRP * S2].rearrange("p g (h k) -> p g h k", k=S2)

        def sp(sp):
            context_load(sp, s, w["context"])

        def pe(pe):
            begin(pe, s)
            pe.wait_ge(loaded["base"], LOADS["base"])
            pe.wait_ge(made, 1)
            pe.wait_ge(loaded[s], LOADS[s])
            transpose_h(pe, s, 0)
            context_pe(pe, s, 0, w, wt)
            for i, more in batches(pe):
                queries_pe(pe, s, i, wt, 0)
                pe.wait_ge(Kdl.ready, Kdl.n(s, i) + 1)
                for j in range(NT):
                    pe.wait_ge(B[0].free, B[0].n(s, i, f"S{j}"))
                    for g in range(H // GRP):
                        k = g * GRP * HD // P
                        ins = pe.matmul(psum[:, g, 0:GRP * S2], QT[:, k, j * P:(j + 1) * P],
                                        Kd[:, g * GRP:(g + 1) * GRP, :].rearrange("p h k -> p (h k)"),
                                        start=True, stop=True)
                    ins.then_inc(B[0].ready, 1)
                pe.wait_ge(B[AHEAD].free, B[AHEAD].n(s, i, "V") + 1)
                if more:
                    transpose_h(pe, s, i + 1)
                    context_pe(pe, s, i + 1, w, wt)
                for j in range(NT):
                    pe.wait_ge(El.ready, El.n(s, i, f"S{j}") + 1)
                    for g in range(H // GRP):
                        t = 4 + g % 2
                        pe.wait_ge(B[t].free, B[t].n(s, i, f"t{j}{g}"))
                        for q in range(GRP):
                            ins = pe.transpose(psum[0:S2, t, q * P:(q + 1) * P], Pj[j][:, g * GRP + q, :], ident)
                        ins.then_inc(B[t].ready, 1)
                    pe.wait_ge(B[6].free, B[6].n(s, i, f"O{j}"))
                    for t in (4, 5):
                        pe.wait_ge(B[t].free, B[t].n(s, i, f"t{j}{t - 2}") + 1)
                    for hh in range(H):
                        ins = pe.matmul(psum[:, 6, hh * (HD + 1):(hh + 1) * (HD + 1)], PT[j][:, hh, :],
                                        V[:, hh, :], start=True, stop=True)
                    ins.then_inc(B[6].ready, 1)
                for j in range(NT):
                    b = 4 + j
                    pe.wait_ge(Ol.ready, Ol.n(s, i, f"O{j}") + 1)
                    pe.wait_ge(B[b].free, B[b].n(s, i, f"OT{j}"))
                    for k in range(KD):
                        ins = pe.transpose(psum[:, b, k * P:(k + 1) * P], O[j][:, k * P:(k + 1) * P], ident)
                    ins.then_inc(B[b].ready, 1)
                for j in range(NT):
                    b = 4 + j
                    pe.wait_ge(B[b].free, B[b].n(s, i, f"Y{j}"))
                    for k in range(KD):
                        ins = pe.matmul(psum[:, b, 0:D], OT[j][:, k, :], wt["wo"][:, k, :],
                                        start=k == 0, stop=k == KD - 1)
                    ins.then_inc(B[b].ready, 1)

        def act(act):
            begin(act, s)
            act.wait_ge(loaded["base"], LOADS["base"])
            copy_hT(act, s, 0)
            context_act(act, s, 0, w)
            for i, more in batches(act):
                queries_act(act, s, i, QT, 0)
                for j in range(NT):
                    act.wait_ge(Pl.ready, Pl.n(s, i, f"S{j}") + 1)
                    p = Pj[j].rearrange("p a b -> p (a b)")
                    act.activation(p, p, ACT.Exp, scale=HD ** -0.5).then_inc(El.ready, 1)
                if more:
                    copy_hT(act, s, i + 1)
                    context_act(act, s, i + 1, w)
                for j in range(NT):
                    for g in range(H // GRP):
                        t = 4 + g % 2
                        act.wait_ge(B[t].ready, B[t].n(s, i, f"t{j}{g}") + 1)
                        act.activation(PT[j][:, g * GRP:(g + 1) * GRP, :].rearrange("p a b -> p (a b)"),
                                       bank(t, parts=S2), ACT.Copy).then_inc(B[t].free, 1)
                for j in range(NT):
                    b = 4 + j
                    act.wait_ge(B[b].ready, B[b].n(s, i, f"OT{j}") + 1)
                    act.activation(OT[j].rearrange("p a b -> p (a b)"), psum[:, b, 0:D], ACT.Copy).then_inc(B[b].free, 1)

        def pool(pool):
            begin(pool, s)
            pool.wait_ge(loaded["base"], LOADS["base"])
            pool.wait_ge(made, 1)

            def ahead(i):
                ln_power(pool, s, i)
                pool.wait_ge(B[AHEAD].free, B[AHEAD].n(s, i, "K") + 1)
                for m in range(KD):
                    n = P // HD
                    ins = pool.tensor_tensor(Kd[:, m * n:(m + 1) * n, :], KT[:, m, :].unsqueeze(1).broadcast_to([P, n, S2]),
                                             const("headmask").unsqueeze(2).broadcast_to([P, n, S2]), ALU.mult)
                ins.then_inc(Kdl.ready, 1)
            ahead(0)
            for i, more in batches(pool):
                if more:
                    ahead(i + 1)

        def values(dve, i):
            b = B[AHEAD]
            dve.wait_ge(b.ready, b.n(s, i, "V") + 1)
            src = psum[0:S2, AHEAD, 0:D].rearrange("p (h d) -> p h d", d=HD)
            if biased:
                bv = rows[0:S2, slice(*ROW_AT[s + "_bv"])].rearrange("p (h d) -> p h d", d=HD)
                dve.tensor_tensor(V[:, :, 0:HD], src, bv, ALU.add).then_inc(b.free, 1)
            else:
                dve.tensor_copy(V[:, :, 0:HD], src).then_inc(b.free, 1)

        def dve(dve):
            step = Steps()
            begin(dve, s)
            dve.memset(V[:, :, HD:HD + 1], 1.0)
            if masked:
                dve.wait_ge(loaded["base"], LOADS["base"])
                dve.tensor_copy(keep, mask_bytes[:]).then_inc(dve_steps, step.one())
                dve.wait_ge(dve_steps, step.done)
                dve.tensor_scalar(fill, keep, 1.0, 1e9 * HD ** 0.5, ALU.subtract, ALU.mult).then_inc(dve_steps, step.one())
            ln_stats(dve, s, 0, step, X[:, 0])
            ln_apply(dve, s, 0, X[:, 0])
            values(dve, 0)
            dve.wait_ge(dve_steps, step.done)
            dve.sem_clear(dve_steps)
            for i, more in batches(dve):
                step = Steps()
                for j in range(NT):
                    dve.wait_ge(B[0].ready, B[0].n(s, i, f"S{j}") + 1)
                    p = Pj[j].rearrange("p (g h) k -> p g h k", h=GRP)
                    src = scores
                    if masked:
                        for m, op in ((keep, ALU.mult), (fill, ALU.add)):
                            bc = m[:, j, :].unsqueeze(1).unsqueeze(1).broadcast_to([P, 4, GRP, S2])
                            ins = dve.tensor_tensor(p, src, bc, op)
                            ins.then_inc(B[0].free if m is keep else dve_steps, 1 if m is keep else step.one())
                            if m is keep:
                                dve.wait_ge(B[0].free, B[0].n(s, i, f"S{j}") + 1)
                            else:
                                dve.wait_ge(dve_steps, step.done)
                            src = p
                    dve.tensor_reduce(nmax[:, j, :], src, AXIS_X, ALU.max, negate=True).then_inc(dve_steps, step.one())
                    dve.wait_ge(dve_steps, step.done)
                    nm = nmax[:, j, :].rearrange("p (g h) -> p g h", h=GRP).unsqueeze(3).broadcast_to([P, 4, GRP, S2])
                    ins = dve.tensor_tensor(p, src, nm, ALU.add)
                    if not masked:
                        ins.then_inc(B[0].free, 1)
                        dve.wait_ge(B[0].free, B[0].n(s, i, f"S{j}") + 1)
                        dve.memset(pad[:, 0:1], 0.0).then_inc(Pl.ready, 1)
                    else:
                        ins.then_inc(Pl.ready, 1)
                if more:
                    ln_stats(dve, s, i + 1, step, X[:, i + 1])
                    ln_apply(dve, s, i + 1, X[:, i + 1])
                for j in range(NT):
                    dve.wait_ge(B[6].ready, B[6].n(s, i, f"O{j}") + 1)
                    o = psum[:, 6, 0:H * (HD + 1)].rearrange("p (h d) -> p h d", d=HD + 1)
                    dve.reciprocal(rden[:, j, :], o[:, :, HD]).then_inc(dve_steps, step.one())
                    dve.wait_ge(dve_steps, step.done)
                    dve.tensor_tensor(O[j].rearrange("p (h d) -> p h d", d=HD), o[:, :, 0:HD],
                                      rden[:, j, :].unsqueeze(2).broadcast_to([P, H, HD]), ALU.mult).then_inc(B[6].free, 1)
                    dve.wait_ge(B[6].free, B[6].n(s, i, f"O{j}") + 1)
                    dve.memset(pad[:, 1:2], 0.0).then_inc(Ol.ready, 1)
                if more:
                    values(dve, i + 1)
                for j in range(NT):
                    b = 4 + j
                    dve.wait_ge(B[b].ready, B[b].n(s, i, f"Y{j}") + 1)
                    dve.tensor_tensor(X[:, i, j, :], psum[:, b, 0:D], X[:, i, j, :], ALU.add).then_inc(B[b].free, 1)
                if biased:
                    for b in (4, 5):
                        dve.wait_ge(B[b].free, B[b].n(s, i, f"Y{b - 4}") + 1)
                    dve.tensor_tensor(X[:, i], X[:, i], row(s + "_bo").unsqueeze(1).broadcast_to([P, NT, D]),
                                      ALU.add).then_inc(updated, 1)
                else:
                    for b in (4, 5):
                        dve.wait_ge(B[b].free, B[b].n(s, i, f"Y{b - 4}") + 1)
                    dve.memset(pad[:, 0:1], 0.0).then_inc(updated, 1)
                dve.wait_ge(dve_steps, step.done)
                dve.sem_clear(dve_steps)
        return dict(sync=sp, tensor=pe, scalar=act, gpsimd=pool, vector=dve)

    def single(s):
        area = Area(WORK1)
        wt = W[s]
        w = dict(context=area.take(D, parts=S2), contextT=area.take(KD, S2), KT=area.take(KD, S2))
        V, QT = area.take(D, parts=S2), area.take(KD, TOK)
        E = [area.take(S2) for _ in range(NT)]
        ET = area.take(NT, P, parts=S2)
        sm = Area(0, small)
        mx, nmax, den, rden = (sm.take(NT) for _ in range(4))
        KT = w["KT"]
        plan(s, {0: "Q t", 1: "S0", 2: "S1", 3: "O0", 4: "O1", AHEAD: "T c K V"},
             context="c", nmax="S0 S1", E="S0 S1")
        nl, El = link("nmax"), link("E")

        def sp(sp):
            context_load(sp, s, w["context"])

        def pe(pe):
            begin(pe, s)
            pe.wait_ge(loaded["base"], LOADS["base"])
            pe.wait_ge(made, 1)
            pe.wait_ge(loaded[s], LOADS[s])
            transpose_h(pe, s, 0)
            context_pe(pe, s, 0, w, wt)
            for i, more in batches(pe):
                queries_pe(pe, s, i, wt, 0)
                pe.wait_ge(B[0].free, B[0].n(s, i, "Q") + 1)
                for j in range(NT):
                    pe.wait_ge(B[1 + j].free, B[1 + j].n(s, i))
                    for k in range(KD):
                        ins = pe.matmul(psum[:, 1 + j, 0:S2], QT[:, k, j * P:(j + 1) * P], KT[:, k, :],
                                        start=k == 0, stop=k == KD - 1)
                    ins.then_inc(B[1 + j].ready, 1)
                pe.wait_ge(B[AHEAD].free, B[AHEAD].n(s, i, "V") + 1)
                if more:
                    transpose_h(pe, s, i + 1)
                    context_pe(pe, s, i + 1, w, wt)
                pe.wait_ge(B[0].free, B[0].n(s, i, "t"))
                for j in range(NT):
                    pe.wait_ge(El.ready, El.n(s, i, f"S{j}") + 1)
                    ins = pe.transpose(psum[0:S2, 0, j * P:(j + 1) * P], E[j], ident)
                ins.then_inc(B[0].ready, 1)
                pe.wait_ge(B[0].free, B[0].n(s, i, "t") + 1)
                for j in range(NT):
                    pe.wait_ge(B[3 + j].free, B[3 + j].n(s, i))
                    pe.matmul(psum[:, 3 + j, 0:D], ET[:, j, :], V, start=True, stop=True).then_inc(B[3 + j].ready, 1)

        def act(act):
            begin(act, s)
            copy_hT(act, s, 0)
            context_act(act, s, 0, w)
            for i, more in batches(act):
                queries_act(act, s, i, QT, 0)
                for j in range(NT):
                    act.wait_ge(nl.ready, nl.n(s, i, f"S{j}") + 1)
                    act.activation(E[j], psum[:, 1 + j, 0:S2], ACT.Exp, scale=D ** -0.5, bias=nmax[:, j:j + 1],
                                   accum_out=den[:, j:j + 1]).then_inc(B[1 + j].free, 1)
                    act.wait_ge(B[1 + j].free, B[1 + j].n(s, i) + 1)
                    act.activation(pad_act[:, 0:1], pad_act[:, 1:2], ACT.Copy).then_inc(El.ready, 1)
                if more:
                    copy_hT(act, s, i + 1)
                    context_act(act, s, i + 1, w)
                act.wait_ge(B[0].ready, B[0].n(s, i, "t") + 1)
                act.activation(ET.rearrange("p a b -> p (a b)"), psum[0:S2, 0, 0:NT * P], ACT.Copy).then_inc(B[0].free, 1)

        def pool(pool):
            begin(pool, s)
            ln_power(pool, s, 0)
            for i, more in batches(pool):
                if more:
                    ln_power(pool, s, i + 1)

        def values(dve, i):
            b = B[AHEAD]
            dve.wait_ge(b.ready, b.n(s, i, "V") + 1)
            dve.tensor_tensor(V, psum[0:S2, AHEAD, 0:D], rows[0:S2, slice(*ROW_AT[s + "_bv"])], ALU.add).then_inc(b.free, 1)

        def dve(dve):
            step = Steps()
            begin(dve, s)
            dve.wait_ge(loaded["base"], LOADS["base"])
            ln_stats(dve, s, 0, step, X[:, 0])
            ln_apply(dve, s, 0, X[:, 0])
            values(dve, 0)
            dve.wait_ge(dve_steps, step.done)
            dve.sem_clear(dve_steps)
            for i, more in batches(dve):
                step = Steps()
                for j in range(NT):
                    dve.wait_ge(B[1 + j].ready, B[1 + j].n(s, i) + 1)
                    dve.tensor_reduce(mx[:, j:j + 1], psum[:, 1 + j, 0:S2], AXIS_X, ALU.max).then_inc(dve_steps, step.one())
                    dve.wait_ge(dve_steps, step.done)
                    dve.tensor_scalar(nmax[:, j:j + 1], mx[:, j:j + 1], -D ** -0.5, None, ALU.mult).then_inc(nl.ready, 1)
                if more:
                    ln_stats(dve, s, i + 1, step, X[:, i + 1])
                    ln_apply(dve, s, i + 1, X[:, i + 1])
                for j in range(NT):
                    dve.wait_ge(El.ready, El.n(s, i, f"S{j}") + 1)
                    dve.reciprocal(rden[:, j:j + 1], den[:, j:j + 1]).then_inc(dve_steps, step.one())
                dve.wait_ge(dve_steps, step.done)
                for j in range(NT):
                    dve.wait_ge(B[3 + j].ready, B[3 + j].n(s, i) + 1)
                    dve.scalar_tensor_tensor(X[:, i, j, :], psum[:, 3 + j, 0:D], rden[:, j:j + 1], X[:, i, j, :],
                                             ALU.mult, ALU.add).then_inc(B[3 + j].free, 1)
                if more:
                    values(dve, i + 1)
                for j in range(NT):
                    dve.wait_ge(B[3 + j].free, B[3 + j].n(s, i) + 1)
                dve.memset(pad[:, 0:1], 0.0).then_inc(updated, 1)
                dve.wait_ge(dve_steps, step.done)
                dve.sem_clear(dve_steps)
        return dict(sync=sp, tensor=pe, scalar=act, gpsimd=pool, vector=dve)
    def ternary(s):
        wt = W[s]
        area = Area(WORK3)
        G = area.take(NT, FF2)
        CT = area.take(FF2 // P, TOK)
        NF = FF2 // P
        ones, scratch = G[:, 0, 0:P], CT.rearrange("p a b -> p (a b)")
        sm = Area(0, small)
        part, total, half, nhalf = sm.take(2, 16), sm.take(2), sm.take(2), sm.take(2)
        st, mo, var, rs = sm.take(NT, 2, 6), sm.take(NT, 2), sm.take(NT), sm.take(NT)
        plan(s, {0: "f0", 2: "f1", 4: "c0 c2", 5: "c1 c3", 6: "Y", AHEAD: "T"},
             inner_variance="f0 f1", inner_rstd="f0 f1", G="f0 f1")
        vl, rl, Gl = link("inner_variance"), link("inner_rstd"), link("G")
        sums, summed, ternaries = sem("weight_sums"), sem("weight_totals"), sem("ternary_weights")
        flat = [wt["fc"].rearrange("p a b -> p (a b)"), wt["proj"].rearrange("p a b -> p (a b)")]

        def pe(pe):
            begin(pe, s)
            pe.wait_ge(loaded["base"], LOADS["base"])
            pe.wait_ge(sums, 1)
            pe.matmul(psum[:, 6, 0:2], ones, total, start=True, stop=True).then_inc(summed, 1)
            transpose_h(pe, s, 0)
            pe.wait_ge(ternaries, 2)
            for i, more in batches(pe):
                need_hT(pe, s, i)
                for j in range(NT):
                    b = 2 * j
                    pe.wait_ge(B[b].free, B[b].n(s, i))
                    for m in range(FF2 // 512):
                        for k in range(KD):
                            ins = pe.matmul(bank(b + m), hT[:, k, j * P:(j + 1) * P], wt["fc"][:, k, m * 512:(m + 1) * 512],
                                            start=k == 0, stop=k == KD - 1)
                    ins.then_inc(B[b].ready, 1)
                if more:
                    transpose_h(pe, s, i + 1)
                pe.wait_ge(Gl.ready, Gl.n(s, i, "f1") + 1)
                for q in range(NF // 2):
                    b = 4 + q % 2
                    pe.wait_ge(B[b].free, B[b].n(s, i, f"c{q}"))
                    for m in range(2):
                        for j in range(NT):
                            ins = pe.transpose(psum[:, b, m * TOK + j * P:m * TOK + (j + 1) * P],
                                               G[:, j, (2 * q + m) * P:(2 * q + m + 1) * P], ident)
                    ins.then_inc(B[b].ready, 1)
                pe.wait_ge(B[6].free, B[6].n(s, i))
                for b, q in ((4, 2), (5, 3)):
                    pe.wait_ge(B[b].free, B[b].n(s, i, f"c{q}") + 1)
                for j in range(NT):
                    for m in range(NF):
                        ins = pe.matmul(psum[:, 6, j * D:(j + 1) * D], CT[:, m, j * P:(j + 1) * P], wt["proj"][:, m, :],
                                        start=m == 0, stop=m == NF - 1)
                ins.then_inc(B[6].ready, 1)

        def act(act):
            begin(act, s)
            copy_hT(act, s, 0)
            for i, more in batches(act):
                for j in range(NT):
                    b = 2 * j
                    act.wait_ge(B[b].ready, B[b].n(s, i) + 1)
                    if j == 0:
                        act.wait_ge(ternaries, 2)
                    act.activation(G[:, j, :].rearrange("p (a b) -> p a b", a=2), psum[:, b:b + 2, :], ACT.Gelu).then_inc(B[b].free, 1)
                if more:
                    copy_hT(act, s, i + 1)
                for q in range(NF // 2):
                    b = 4 + q % 2
                    act.wait_ge(B[b].ready, B[b].n(s, i, f"c{q}") + 1)
                    for m in range(2):
                        c = 2 * q + m
                        ins = act.activation(CT[:, c, :], psum[:, b, m * TOK:(m + 1) * TOK], ACT.Identity,
                                             scale=col("L2f_w", c), bias=col("L2f_b", c))
                    ins.then_inc(B[b].free, 1)

        def pool(pool):
            begin(pool, s)
            ln_power(pool, s, 0)
            for i, more in batches(pool):
                for j in range(NT):
                    pool.wait_ge(vl.ready, vl.n(s, i, f"f{j}") + 1)
                    pool.tensor_tensor(rs[:, j:j + 1], var[:, j:j + 1], minus_half[:, 0:1], ALU.pow).then_inc(rl.ready, 1)
                if more:
                    ln_power(pool, s, i + 1)

        def dve(dve):
            step = Steps()
            begin(dve, s)
            ln_stats(dve, s, 0, step, X[:, 0])
            dve.wait_ge(loaded[s], LOADS[s])
            dve.memset(ones, 1.0).then_inc(dve_steps, step.one())
            for m in range(2):
                dve.tensor_reduce(part[:, m, :], flat[m].rearrange("p (a b) -> p a b", a=16), AXIS_X, ALU.add,
                                  apply_absolute_value=True).then_inc(dve_steps, step.one())
            dve.wait_ge(dve_steps, step.done)
            dve.tensor_reduce(total, part, AXIS_X, ALU.add).then_inc(sums, 1)
            ln_apply(dve, s, 0, X[:, 0])
            dve.wait_ge(summed, 1)
            dve.tensor_scalar(total, psum[:, 6, 0:2], 1.0 / (D * FF2), 1e-6, ALU.mult, ALU.add).then_inc(dve_steps, step.one())
            dve.wait_ge(dve_steps, step.done)
            dve.tensor_scalar(half, total, 0.5, None, ALU.mult).then_inc(dve_steps, step.one())
            dve.tensor_scalar(nhalf, total, -0.5, None, ALU.mult).then_inc(dve_steps, step.one())
            dve.wait_ge(dve_steps, step.done)
            for m in range(2):
                if m:
                    dve.wait_ge(ternaries, 1)
                dve.tensor_scalar(scratch, flat[m], nhalf[:, m:m + 1], None, ALU.is_lt).then_inc(dve_steps, step.one())
                dve.wait_ge(dve_steps, step.done)
                dve.scalar_tensor_tensor(flat[m], flat[m], half[:, m:m + 1], scratch, ALU.is_gt, ALU.subtract).then_inc(ternaries, 1)
            dve.wait_ge(dve_steps, step.done)
            dve.sem_clear(dve_steps)
            for i, more in batches(dve):
                step = Steps()
                for j in range(NT):
                    b = 2 * j
                    dve.wait_ge(B[b].free, B[b].n(s, i) + 1)
                    for m in range(2):
                        dve.bn_stats(st[:, j, m, :], G[:, j, m * 512:(m + 1) * 512]).then_inc(dve_steps, step.one())
                    dve.wait_ge(dve_steps, step.done)
                    dve.memset(pad[:, 0:1], 0.0)
                    dve.bn_aggr(mo[:, j, :], st[:, j].rearrange("p a b -> p (a b)")).then_inc(dve_steps, step.one())
                    dve.wait_ge(dve_steps, step.done)
                    dve.tensor_scalar(var[:, j:j + 1], mo[:, j, 1:2], EPS, None, ALU.add).then_inc(vl.ready, 1)
                if more:
                    ln_stats(dve, s, i + 1, step, X[:, i + 1])
                for j in range(NT):
                    dve.wait_ge(rl.ready, rl.n(s, i, f"f{j}") + 1)
                    dve.tensor_scalar(G[:, j, :], G[:, j, :], mo[:, j, 0:1], rs[:, j:j + 1], ALU.subtract, ALU.mult).then_inc(Gl.ready, 1)
                if more:
                    ln_apply(dve, s, i + 1, X[:, i + 1])
                dve.wait_ge(B[6].ready, B[6].n(s, i) + 1)
                dve.tensor_tensor(X[:, i].rearrange("p a b -> p (a b)"), bank(6), X[:, i].rearrange("p a b -> p (a b)"), ALU.add).then_inc(B[6].free, 1)
                dve.wait_ge(B[6].free, B[6].n(s, i) + 1)
                dve.memset(pad[:, 0:1], 0.0).then_inc(updated, 1)
                dve.wait_ge(dve_steps, step.done)
                dve.sem_clear(dve_steps)
        return dict(tensor=pe, scalar=act, gpsimd=pool, vector=dve)
    FFNS["L2f"] = ternary

    def experts(s):
        NC = FF3 // P
        area = Area((NE + 1) * EXPERT_W)
        hid = [area.take(NC, TOK) for _ in range(2)]
        sg = [area.take(TOK) for _ in range(2)]
        acc = area.take(NT, D)
        sm = Area(0, small)
        logits, top, index, turn = sm.take(NT, NE), sm.take(NT, 8), sm.take(NT, 8), sm.take(NT)
        index_f, weight, share, combine = sm.take(NT, 2), sm.take(NT, 2), sm.take(NT, 2, NE), sm.take(NT, NE)
        index = index.bitcast(mybir.dt.uint32)
        gu = {m: " ".join(f"m{x}" for x in range(m, (NE + 1) * NC, 2)) for m in range(2)}
        plan(s, {0: gu[0], 1: gu[1], 2: gu[0], 3: gu[1], 4: " ".join(f"e{e}" for e in range(0, NE + 1, 2)),
                 5: " ".join(f"e{e}" for e in range(1, NE + 1, 2)), 6: "logits", AHEAD: "T"},
             turn="t", tanh="t")
        turn_l, tanh_l = link("turn"), link("tanh")

        def gate_up(pe, i, e, wt):
            for c in range(NC):
                m = e * NC + c
                for b, n in ((m % 2, "g"), (2 + m % 2, "u")):
                    pe.wait_ge(B[b].free, B[b].n(s, i, f"m{m}"))
                    for k in range(KD):
                        ins = pe.matmul(bank(b, TOK), wt[n][:, k, c * P:(c + 1) * P], hT[:, k, :], start=k == 0, stop=k == KD - 1)
                    ins.then_inc(B[b].ready, 1)

        def down(pe, i, e, wt):
            b = 4 + e % 2
            pe.wait_ge(B[b].free, B[b].n(s, i, f"e{e}"))
            for x in (2, 3):
                m = e * NC + NC - 4 + x
                pe.wait_ge(B[2 + m % 2].free, B[2 + m % 2].n(s, i, f"m{m}") + 1)
            for j in range(NT):
                for c in range(NC):
                    ins = pe.matmul(psum[:, b, j * D:(j + 1) * D], hid[e % 2][:, c, j * P:(j + 1) * P], wt["d"][:, c, :],
                                    start=c == 0, stop=c == NC - 1)
            ins.then_inc(B[b].ready, 1)

        def pe(pe):
            begin(pe, s)
            pe.wait_ge(loaded["base"], LOADS["base"])
            pe.wait_ge(loaded[s], LOADS[s])
            transpose_h(pe, s, 0)
            for i, more in batches(pe):
                need_hT(pe, s, i)
                pe.wait_ge(B[6].free, B[6].n(s, i))
                for j in range(NT):
                    for k in range(KD):
                        ins = pe.matmul(psum[:, 6, j * NE:(j + 1) * NE], hT[:, k, j * P:(j + 1) * P], router[:, k, :],
                                        start=k == 0, stop=k == KD - 1)
                ins.then_inc(B[6].ready, 1)
                for e in range(NE + 1):
                    if e == EARLY:
                        pe.wait_ge(loaded["L3f_late"], LOADS["L3f_late"])
                    gate_up(pe, i, e, W[s][e])
                    if e:
                        down(pe, i, e - 1, W[s][e - 1])
                if more:
                    transpose_h(pe, s, i + 1)
                down(pe, i, NE, W[s][NE])

        def act(act):
            begin(act, s)
            copy_hT(act, s, 0)
            for i, more in batches(act):
                for m in range((NE + 1) * NC):
                    b = m % 2
                    act.wait_ge(B[b].ready, B[b].n(s, i, f"m{m}") + 1)
                    act.wait_ge(B[2 + b].free, B[2 + b].n(s, i, f"m{m}"))
                    act.activation(sg[b], bank(b, TOK), ACT.Silu).then_inc(B[b].free, 1)
                    if m == 2 * NC - 1:
                        act.wait_ge(turn_l.ready, turn_l.n(s, i) + 1)
                        act.activation(turn, turn, ACT.Tanh, scale=0.5).then_inc(tanh_l.ready, 1)
                if more:
                    copy_hT(act, s, i + 1)

        def pool(pool):
            begin(pool, s)
            ln_power(pool, s, 0)
            for i, more in batches(pool):
                if more:
                    ln_power(pool, s, i + 1)

        def route(dve, i, step):
            dve.wait_ge(B[6].ready, B[6].n(s, i) + 1)
            dve.tensor_copy(logits.rearrange("p a b -> p (a b)"), psum[:, 6, 0:NT * NE]).then_inc(B[6].free, 1)
            dve.wait_ge(B[6].free, B[6].n(s, i) + 1)
            dve.memset(pad[:, 0:1], 0.0)
            for j in range(NT):
                dve.max(top[:, j, :], logits[:, j, :]).then_inc(dve_steps, step.one())
            dve.wait_ge(dve_steps, step.done)
            dve.tensor_tensor(turn, top[:, :, 0], top[:, :, 1], ALU.subtract).then_inc(turn_l.ready, 1)
            for j in range(NT):
                dve.max_index(index[:, j, :], top[:, j, :], logits[:, j, :]).then_inc(dve_steps, step.one())
            dve.wait_ge(dve_steps, step.done)
            dve.tensor_copy(index_f, index[:, :, 0:2]).then_inc(dve_steps, step.one())

        def weigh(dve, i, step):
            dve.wait_ge(tanh_l.ready, tanh_l.n(s, i) + 1)
            dve.tensor_scalar(weight[:, :, 0], turn, 0.5, 0.5, ALU.mult, ALU.add).then_inc(dve_steps, step.one())
            dve.tensor_scalar(weight[:, :, 1], turn, -0.5, 0.5, ALU.mult, ALU.add).then_inc(dve_steps, step.one())
            dve.wait_ge(dve_steps, step.done)
            for j in range(NT):
                for q in range(2):
                    dve.tensor_scalar(share[:, j, q, :], const("iota"), index_f[:, j, q:q + 1], weight[:, j, q:q + 1],
                                      ALU.is_equal, ALU.mult).then_inc(dve_steps, step.one())
            dve.wait_ge(dve_steps, step.done)
            dve.tensor_tensor(combine, share[:, :, 0, :], share[:, :, 1, :], ALU.add).then_inc(dve_steps, step.one())
            dve.wait_ge(dve_steps, step.done)

        def add_expert(dve, i, e):
            b = 4 + e % 2
            if e:
                dve.wait_ge(B[4 + (e - 1) % 2].free, B[4 + (e - 1) % 2].n(s, i, f"e{e - 1}") + 1)
            dve.wait_ge(B[b].ready, B[b].n(s, i, f"e{e}") + 1)
            for j in range(NT):
                y, into = psum[:, b, j * D:(j + 1) * D], X[:, i, j, :] if e == NE else acc[:, j, :]
                if e == 0:
                    ins = dve.tensor_tensor(into, y, X[:, i, j, :], ALU.add)
                else:
                    ins = dve.scalar_tensor_tensor(into, y, combine[:, j, e - 1:e], acc[:, j, :], ALU.mult, ALU.add)
            ins.then_inc(B[b].free, 1)

        def dve(dve):
            step = Steps()
            begin(dve, s)
            ln_stats(dve, s, 0, step, X[:, 0])
            ln_apply(dve, s, 0, X[:, 0])
            dve.wait_ge(dve_steps, step.done)
            dve.sem_clear(dve_steps)
            for i, more in batches(dve):
                step = Steps()
                for e in range(NE + 1):
                    for c in range(NC):
                        m = e * NC + c
                        b = 2 + m % 2
                        dve.wait_ge(B[b].ready, B[b].n(s, i, f"m{m}") + 1)
                        dve.wait_ge(B[b - 2].free, B[b - 2].n(s, i, f"m{m}") + 1)
                        dve.tensor_tensor(hid[e % 2][:, c, :], bank(b, TOK), sg[m % 2], ALU.mult).then_inc(B[b].free, 1)
                    if e == 0:
                        route(dve, i, step)
                    if e == 2:
                        weigh(dve, i, step)
                    if e == 4 and more:
                        ln_stats(dve, s, i + 1, step, X[:, i + 1])
                    if e == 6 and more:
                        ln_apply(dve, s, i + 1, X[:, i + 1])
                    if e:
                        if e == 2:
                            pass
                        add_expert(dve, i, e - 1)
                add_expert(dve, i, NE)
                dve.wait_ge(B[4].free, B[4].n(s, i, f"e{NE}") + 1)
                dve.memset(pad[:, 0:1], 0.0).then_inc(updated, 1)
                dve.wait_ge(dve_steps, step.done)
                dve.sem_clear(dve_steps)
        return dict(tensor=pe, scalar=act, gpsimd=pool, vector=dve)
    FFNS["L3f"] = experts

    def memory(s):
        wt = W[s]
        NC = FF0 // P
        area = Area(WORK1)
        qT, sims = area.take(4, TOK), area.take(NT, 2, PH, NKEYS)
        S = [area.take(PROWS, NKEYS) for _ in range(PH)]
        E = [area.take(NEXP) for _ in range(2)]
        G = [area.take(NEXP) for _ in range(NT)]
        C = [area.take(NEXP) for _ in range(NT)]
        CT = area.take(NEXP // P, TOK)
        hid = area.take(NC, TOK)
        sg = [area.take(TOK) for _ in range(2)]
        sm = Area(0, small)
        tx, ty, top = sm.take(PH, TOPK), sm.take(PH, TOPK), sm.take(PH, TOPK)
        grid = sm.take(PH, TOPK, TOPK)
        thr, ntop = sm.take(NT, PH), sm.take(NT, PH)
        shifted, e8 = sm.take(NT, PH, TOPK), sm.take(NT, PH, TOPK)
        z, rz, left = sm.take(NT, PH), sm.take(NT, PH), sm.take(NT, 2)
        heads = " ".join(f"{j}{h}" for j in range(NT) for h in range(PH))
        plan(s, {0: "m0 m2 m4 m6 w0 w1", 1: "m1 m3 m5 m7 w0 w1", 2: "m0 m2 m4 m6", 3: "m1 m3 m5 m7",
                 4: "q s0 c0 c1", 5: "q s1 c0 c1", 6: "Y", AHEAD: "T"},
             shifted="t0 t1", e8="t0 t1", S=heads, exps=heads, picked=heads, G=heads, C="t0 t1")
        shifted_l, e8_l, S_l, E_l, picked_l, G_l, C_l = (link(n) for n in ("shifted", "e8", "S", "exps", "picked", "G", "C"))

        def gate_up(pe, i, m):
            for b, n in ((m % 2, "wg"), (2 + m % 2, "wu")):
                pe.wait_ge(B[b].free, B[b].n(s, i, f"m{m}"))
                for k in range(KD):
                    ins = pe.matmul(bank(b, TOK), wt[n][:, k, m * P:(m + 1) * P], hT[:, k, :], start=k == 0, stop=k == KD - 1)
                ins.then_inc(B[b].ready, 1)

        def pe(pe):
            begin(pe, s)
            pe.wait_ge(loaded["base"], LOADS["base"])
            pe.wait_ge(loaded[s], LOADS[s])
            transpose_h(pe, s, 0)
            for i, more in batches(pe):
                need_hT(pe, s, i)
                for b in (4, 5):
                    pe.wait_ge(B[b].free, B[b].n(s, i, "q"))
                    for x in range(2):
                        c = 2 * (b - 4) + x
                        for k in range(KD):
                            ins = pe.matmul(psum[:, b, x * TOK:(x + 1) * TOK], wt["wq"][:, k, c * P:(c + 1) * P], hT[:, k, :],
                                            start=k == 0, stop=k == KD - 1)
                    ins.then_inc(B[b].ready, 1)
                for m in range(2):
                    gate_up(pe, i, m)
                for b in (4, 5):
                    pe.wait_ge(B[b].free, B[b].n(s, i, "q") + 1)
                for j in range(NT):
                    b = 4 + j
                    pe.wait_ge(B[b].free, B[b].n(s, i, f"s{j}"))
                    for c in range(4):
                        ins = pe.matmul(psum[:, b, c * P:(c + 1) * P], qT[:, c, j * P:(j + 1) * P], wt["keys"][:, c, :],
                                        start=True, stop=True)
                    ins.then_inc(B[b].ready, 1)
                for m in range(2, NC):
                    gate_up(pe, i, m)
                for j in range(NT):
                    for m in range(2):
                        pe.wait_ge(B[m].free, B[m].n(s, i, f"w{j}"))
                        for k in range(KD):
                            ins = pe.matmul(bank(m), hT[:, k, j * P:(j + 1) * P], wt["down"][:, k, m * 512:(m + 1) * 512],
                                            start=k == 0, stop=k == KD - 1)
                        ins.then_inc(B[m].ready, 1)
                if more:
                    transpose_h(pe, s, i + 1)
                pe.wait_ge(B[6].free, B[6].n(s, i))
                for b in (2, 3):
                    pe.wait_ge(B[b].free, B[b].n(s, i, f"m{b + 4}") + 1)
                for j in range(NT):
                    y = psum[:, 6, j * D:(j + 1) * D]
                    for m in range(NC):
                        pe.matmul(y, hid[:, m, j * P:(j + 1) * P], wt["wd"][:, m, :], start=m == 0, stop=False)
                    pe.wait_ge(C_l.ready, C_l.n(s, i, f"t{j}") + 1)
                    for b in (4, 5):
                        pe.wait_ge(B[b].free, B[b].n(s, i, f"c{j}"))
                        for m in range(4):
                            e = (b - 4) * 4 + m
                            ins = pe.transpose(psum[:, b, m * P:(m + 1) * P], C[j][:, e * P:(e + 1) * P], ident)
                        ins.then_inc(B[b].ready, 1)
                    for b in (4, 5):
                        pe.wait_ge(B[b].free, B[b].n(s, i, f"c{j}") + 1)
                        for m in range(4):
                            e = (b - 4) * 4 + m
                            ins = pe.matmul(y, CT[:, e, j * P:(j + 1) * P], wt["up"][:, e, :], start=False, stop=e == NEXP // P - 1)
                ins.then_inc(B[6].ready, 1)

        def act(act):
            begin(act, s)
            act.wait_ge(loaded["base"], LOADS["base"])
            copy_hT(act, s, 0)

            def silu(i, m):
                b = m % 2
                act.wait_ge(B[b].ready, B[b].n(s, i, f"m{m}") + 1)
                act.wait_ge(B[2 + b].free, B[2 + b].n(s, i, f"m{m}"))
                act.activation(sg[b], bank(b, TOK), ACT.Silu, bias=col("L0f_bg", m)).then_inc(B[b].free, 1)

            def exps(i, j, pair):
                if pair == 0:
                    act.wait_ge(shifted_l.ready, shifted_l.n(s, i, f"t{j}") + 1)
                    act.activation(e8[:, j], shifted[:, j], ACT.Exp).then_inc(e8_l.ready, 1)
                for hh in (2 * pair, 2 * pair + 1):
                    act.wait_ge(S_l.ready, S_l.n(s, i, f"{j}{hh}") + 1)
                    if j or hh > 1:
                        act.wait_ge(G_l.ready, G_l.n(s, i, f"{j}{hh}") - 1)
                    act.activation(E[hh % 2], S[hh].rearrange("p a b -> p (a b)"), ACT.Exp, bias=ntop[:, j, hh:hh + 1]).then_inc(E_l.ready, 1)

            def silu_w(i, j):
                for m in range(2):
                    act.wait_ge(B[m].ready, B[m].n(s, i, f"w{j}") + 1)
                    act.activation(C[j][:, m * 512:(m + 1) * 512], bank(m), ACT.Silu).then_inc(B[m].free, 1)

            for i, more in batches(act):
                for b in (4, 5):
                    act.wait_ge(B[b].ready, B[b].n(s, i, "q") + 1)
                    act.activation(qT[:, 2 * (b - 4):2 * (b - 4) + 2, :].rearrange("p a b -> p (a b)"), bank(b), ACT.Copy).then_inc(B[b].free, 1)
                silu(i, 0)
                silu(i, 1)
                for j in range(NT):
                    b = 4 + j
                    act.wait_ge(B[b].ready, B[b].n(s, i, f"s{j}") + 1)
                    act.activation(sims[:, j].rearrange("p a b c -> p (a b c)"), bank(b), ACT.Copy).then_inc(B[b].free, 1)
                silu(i, 2)
                silu(i, 3)
                exps(i, 0, 0)
                silu(i, 4)
                silu(i, 5)
                exps(i, 0, 1)
                silu(i, 6)
                silu(i, 7)
                exps(i, 1, 0)
                silu_w(i, 0)
                exps(i, 1, 1)
                silu_w(i, 1)
                if more:
                    copy_hT(act, s, i + 1)
                for j in range(NT):
                    for b in (4, 5):
                        act.wait_ge(B[b].ready, B[b].n(s, i, f"c{j}") + 1)
                        act.activation(CT[:, 4 * (b - 4):4 * (b - 4) + 4, j * P:(j + 1) * P],
                                       bank(b).rearrange("p (a b) -> p a b", a=4), ACT.Copy).then_inc(B[b].free, 1)

        def pool(pool):
            begin(pool, s)
            ln_power(pool, s, 0)
            for i, more in batches(pool):
                for j in range(NT):
                    pool.wait_ge(B[4 + j].free, B[4 + j].n(s, i, f"s{j}") + 1)
                    for hh in range(PH):
                        if j:
                            pool.wait_ge(picked_l.ready, picked_l.n(s, i, f"{j - 1}{hh}") + 1)
                        x = sims[:, j, 0, hh, 0:PROWS].unsqueeze(2).broadcast_to([P, PROWS, NKEYS])
                        y = sims[:, j, 1, hh, :].unsqueeze(1).broadcast_to([P, PROWS, NKEYS])
                        pool.tensor_tensor(S[hh], x, y, ALU.add).then_inc(S_l.ready, 1)
                    if more and j == 0:
                        ln_power(pool, s, i + 1)

        def dve(dve):
            step = Steps()
            begin(dve, s)
            ln_stats(dve, s, 0, step, X[:, 0])
            ln_apply(dve, s, 0, X[:, 0])
            dve.wait_ge(dve_steps, step.done)
            dve.sem_clear(dve_steps)

            def hidden(i, m):
                b = 2 + m % 2
                dve.wait_ge(B[b].ready, B[b].n(s, i, f"m{m}") + 1)
                dve.wait_ge(B[b - 2].free, B[b - 2].n(s, i, f"m{m}") + 1)
                dve.scalar_tensor_tensor(hid[:, m, :], bank(b, TOK), col("L0f_bu", m), sg[m % 2], ALU.add, ALU.mult).then_inc(B[b].free, 1)

            def select(i, j, step):
                dve.wait_ge(B[4 + j].free, B[4 + j].n(s, i, f"s{j}") + 1)
                dve.memset(pad[:, 0:1], 0.0)
                for hh in range(PH):
                    dve.max(tx[:, hh, :], sims[:, j, 0, hh, :]).then_inc(dve_steps, step.one())
                    dve.max(ty[:, hh, :], sims[:, j, 1, hh, :]).then_inc(dve_steps, step.one())
                dve.wait_ge(dve_steps, step.done)
                dve.tensor_tensor(grid, tx.unsqueeze(3).broadcast_to([P, PH, TOPK, TOPK]),
                                  ty.unsqueeze(2).broadcast_to([P, PH, TOPK, TOPK]), ALU.add).then_inc(dve_steps, step.one())
                dve.wait_ge(dve_steps, step.done)
                dve.memset(pad[:, 0:1], 0.0)
                for hh in range(PH):
                    dve.max(top[:, hh, :], grid[:, hh].rearrange("p a b -> p (a b)")).then_inc(dve_steps, step.one())
                dve.wait_ge(dve_steps, step.done)
                dve.tensor_scalar(ntop[:, j, :], top[:, :, 0], -1.0, None, ALU.mult).then_inc(dve_steps, step.one())
                dve.tensor_copy(thr[:, j, :], top[:, :, TOPK - 1]).then_inc(dve_steps, step.one())
                dve.wait_ge(dve_steps, step.done)
                dve.tensor_tensor(shifted[:, j], top, ntop[:, j, :].unsqueeze(2).broadcast_to([P, PH, TOPK]),
                                  ALU.add).then_inc(shifted_l.ready, 1)

            def normalise(i, j, step):
                dve.wait_ge(e8_l.ready, e8_l.n(s, i, f"t{j}") + 1)
                dve.tensor_reduce(z[:, j, :], e8[:, j], AXIS_X, ALU.add).then_inc(dve_steps, step.one())
                dve.wait_ge(dve_steps, step.done)
                dve.reciprocal(rz[:, j, :], z[:, j, :]).then_inc(dve_steps, step.one())

            def accumulate(i, j, hh, step):
                at = f"{j}{hh}"
                dve.wait_ge(E_l.ready, E_l.n(s, i, at) + 1)
                dve.scalar_tensor_tensor(E[hh % 2], S[hh].rearrange("p a b -> p (a b)"), thr[:, j, hh:hh + 1], E[hh % 2],
                                         ALU.is_ge, ALU.mult).then_inc(picked_l.ready, 1)
                dve.wait_ge(picked_l.ready, picked_l.n(s, i, at) + 1)
                if hh == 0:
                    dve.wait_ge(dve_steps, step.done)
                    dve.tensor_scalar(G[j], E[hh % 2], rz[:, j, hh:hh + 1], None, ALU.mult).then_inc(G_l.ready, 1)
                    return
                dve.wait_ge(G_l.ready, G_l.n(s, i, at))
                last = hh == PH - 1
                dve.scalar_tensor_tensor(G[j], E[hh % 2], rz[:, j, hh:hh + 1], G[j], ALU.mult, ALU.add,
                                         accum_out=left[:, j, 0:1] if last else None).then_inc(G_l.ready, 1)
                if last:
                    dve.wait_ge(G_l.ready, G_l.n(s, i, at) + 1)
                    dve.tensor_scalar(left[:, j, 1:2], left[:, j, 0:1], -1.0, float(PH), ALU.mult, ALU.add).then_inc(dve_steps, step.one())
                    dve.wait_ge(dve_steps, step.done)
                    dve.tensor_tensor(G[j][:, NEXP - 1:NEXP], G[j][:, NEXP - 1:NEXP], left[:, j, 1:2], ALU.add).then_inc(dve_steps, step.one())

            def combine(i, j, step):
                dve.wait_ge(B[1].free, B[1].n(s, i, f"w{j}") + 1)
                dve.wait_ge(B[0].free, B[0].n(s, i, f"w{j}") + 1)
                dve.wait_ge(dve_steps, step.done)
                dve.tensor_tensor(C[j], C[j], G[j], ALU.mult).then_inc(C_l.ready, 1)

            for i, more in batches(dve):
                step = Steps()
                for m in range(2):
                    hidden(i, m)
                select(i, 0, step)
                for m in range(2, 4):
                    hidden(i, m)
                normalise(i, 0, step)
                accumulate(i, 0, 0, step)
                accumulate(i, 0, 1, step)
                for m in range(4, 6):
                    hidden(i, m)
                accumulate(i, 0, 2, step)
                accumulate(i, 0, 3, step)
                if more:
                    ln_stats(dve, s, i + 1, step, X[:, i + 1])
                for m in range(6, 8):
                    hidden(i, m)
                select(i, 1, step)
                normalise(i, 1, step)
                accumulate(i, 1, 0, step)
                accumulate(i, 1, 1, step)
                if more:
                    ln_apply(dve, s, i + 1, X[:, i + 1])
                combine(i, 0, step)
                accumulate(i, 1, 2, step)
                accumulate(i, 1, 3, step)
                combine(i, 1, step)
                dve.wait_ge(B[6].ready, B[6].n(s, i) + 1)
                x = X[:, i].rearrange("p a b -> p (a b)")
                dve.tensor_tensor(x, bank(6), x, ALU.add).then_inc(B[6].free, 1)
                dve.wait_ge(B[6].free, B[6].n(s, i) + 1)
                dve.tensor_tensor(X[:, i], X[:, i], row(s + "_bd").unsqueeze(1).broadcast_to([P, NT, D]), ALU.add).then_inc(updated, 1)
                dve.wait_ge(dve_steps, step.done)
                dve.sem_clear(dve_steps)
        return dict(tensor=pe, scalar=act, gpsimd=pool, vector=dve)
    FFNS["L0f"] = memory

    def local(s):
        wt = W[s]
        NI = INNER // P
        area = Area(WORK2)
        cos = {n: area.take(NT, WD) for n in "qk"}
        sin = {n: area.take(NT, WD) for n in "qk"}
        shared = area.at
        qk, sq, turned, other = (area.take(2, WH, WD) for _ in range(4))
        mlp = Area(shared)
        hid, gel, hs, hsT = mlp.take(NHC, TOK), mlp.take(2, TOK), mlp.take(NT, D), mlp.take(KD, TOK)
        assert mlp.at <= area.at
        v = area.take(NT, INNER)
        qT, kT = area.take(NI, TOK), area.take(NI, TOK)
        at_p = area.at
        Pj = [area.take(WH, P), area.take(WH, 2 * P)]
        o, oT = view(at_p, (NT, INNER)), view(at_p + WH * P, (NI, TOK))
        PT = [area.take(WH, P), area.take(2 * WH, P)]
        z1 = area.take(NT, D)
        assert area.at <= AT_Z
        sm = Area(0, small)
        ssq, rn = sm.take(2 * WH), sm.take(2 * WH)
        mx, nmax, den, rden = sm.take(NT, WH), sm.take(NT, WH), sm.take(NT, WH), sm.take(NT, WH)
        st, mo, var, rs = sm.take(NT, 6), sm.take(NT, 2), sm.take(NT), sm.take(NT)
        plan(s, {0: "q0 q1 S1 g0 g2 g4", 1: "k0 k1 S1 g1 g3 g5", 2: "v0 v1 S1 g0 g2 g4", 3: "S1 g1 g3 g5",
                 4: "tq0 tq1 S0 p0 p2 p4 o0", 5: "tk0 tk1 S0 p1 p3 p5 o1", 6: "O0 O1 Y sh hf Y2", AHEAD: "T"},
             squares="0 1", norms="0 1", inverse_norms="0 1", other="0 1", rotated="0 1", scaled="0 1",
             nmax="S0 S1", E="S0 S1", o="0 1", z1="z", hs_variance="h", hs_rstd="h", hs="h")
        sq_l, ssq_l, rn_l, other_l, rot_l, scaled_l, nmax_l, E_l, o_l, z1_l, var_l, rs_l, hs_l = (link(n) for n in (
            "squares", "norms", "inverse_norms", "other", "rotated", "scaled", "nmax", "E", "o", "z1",
            "hs_variance", "hs_rstd", "hs"))
        tables = sem(f"rotary_tables_{s}")
        HALF = WD // 2
        GROUPS = [[(0, hh, 0) for hh in range(g * 4, g * 4 + 4)] for g in range(2)] + \
                 [[(1, hh, kb) for hh in (2 * g, 2 * g + 1) for kb in range(2)] for g in range(4)]

        def chunk(m):
            return P if m < NHC - 1 else HREM

        def pe(pe):
            begin(pe, s)
            pe.wait_ge(loaded["base"], LOADS["base"])
            pe.wait_ge(loaded[s], LOADS[s])
            transpose_h(pe, s, 0)
            for i, more in batches(pe):
                need_hT(pe, s, i)
                for j in range(NT):
                    for b, n in enumerate("qkv"):
                        pe.wait_ge(B[b].free, B[b].n(s, i, f"{n}{j}"))
                        for k in range(KD):
                            ins = pe.matmul(bank(b), hT[:, k, j * P:(j + 1) * P], wt["wqkv"][:, k, b * INNER:(b + 1) * INNER],
                                            start=k == 0, stop=k == KD - 1)
                        ins.then_inc(B[b].ready, 1)
                for j in range(NT):
                    pe.wait_ge(scaled_l.ready, scaled_l.n(s, i, f"{j}") + 1)
                    for b, n in ((4, "tq"), (5, "tk")):
                        pe.wait_ge(B[b].free, B[b].n(s, i, f"{n}{j}"))
                        src = turned[:, b - 4].rearrange("p h d -> p (h d)")
                        for c in range(NI):
                            ins = pe.transpose(psum[:, b, c * P:(c + 1) * P], src[:, c * P:(c + 1) * P], ident)
                        ins.then_inc(B[b].ready, 1)
                for odd in range(2):
                    pe.wait_ge(B[4 + odd].free, B[4 + odd].n(s, i, "S0"))
                pe.wait_ge(B[5].free, B[5].n(s, i, "S0"))
                for odd in range(2):
                    r = slice(odd * WD, (odd + 1) * WD)
                    for c in range(NI):
                        ins = pe.matmul(psum[:, 4 + odd, c * P:(c + 1) * P], qT[r, c, 0:P], kT[r, c, 0:P], start=True, stop=True)
                    ins.then_inc(B[4 + odd].ready, 1)
                for odd in range(2):
                    r = slice(odd * WD, (odd + 1) * WD)
                    for c in range(NI):
                        b = 2 * odd + c // 2
                        if c % 2 == 0:
                            pe.wait_ge(B[b].free, B[b].n(s, i, "S1"))
                        ins = pe.matmul(psum[:, b, (c % 2) * 2 * P:(c % 2 + 1) * 2 * P], qT[r, c, P:2 * P], kT[r, c, :], start=True, stop=True)
                        if c % 2:
                            ins.then_inc(B[b].ready, 1)

                def transposed(j):
                    pe.wait_ge(E_l.ready, E_l.n(s, i, f"S{j}") + 1)
                    for g, group in enumerate(GROUPS):
                        if group[0][0] != j:
                            continue
                        b = 4 + g % 2
                        pe.wait_ge(B[b].free, B[b].n(s, i, f"p{g}"))
                        for x, (_, hh, kb) in enumerate(group):
                            ins = pe.transpose(psum[:, b, x * P:(x + 1) * P], Pj[j][:, hh, kb * P:(kb + 1) * P], ident)
                        ins.then_inc(B[b].ready, 1)

                transposed(0)
                pe.wait_ge(B[6].free, B[6].n(s, i, "O0"))
                for g in (0, 1):
                    pe.wait_ge(B[4 + g].free, B[4 + g].n(s, i, f"p{g}") + 1)
                for hh in range(WH):
                    ins = pe.matmul(psum[:, 6, hh * WD:(hh + 1) * WD], PT[0][:, hh, :], v[:, 0, hh * WD:(hh + 1) * WD], start=True, stop=True)
                ins.then_inc(B[6].ready, 1)
                transposed(1)
                pe.wait_ge(B[6].free, B[6].n(s, i, "O1"))
                for g in (4, 5):
                    pe.wait_ge(B[g].free, B[g].n(s, i, f"p{g}") + 1)
                for hh in range(WH):
                    for kb in range(2):
                        ins = pe.matmul(psum[:, 6, hh * WD:(hh + 1) * WD], PT[1][:, 2 * hh + kb, :], v[:, kb, hh * WD:(hh + 1) * WD],
                                        start=kb == 0, stop=kb == 1)
                ins.then_inc(B[6].ready, 1)
                for j in range(NT):
                    b = 4 + j
                    pe.wait_ge(o_l.ready, o_l.n(s, i, f"{j}") + 1)
                    pe.wait_ge(B[b].free, B[b].n(s, i, f"o{j}"))
                    for c in range(NI):
                        ins = pe.transpose(psum[:, b, c * P:(c + 1) * P], o[:, j, c * P:(c + 1) * P], ident)
                    ins.then_inc(B[b].ready, 1)
                pe.wait_ge(B[6].free, B[6].n(s, i, "Y"))
                for j in range(NT):
                    pe.wait_ge(B[4 + j].free, B[4 + j].n(s, i, f"o{j}") + 1)
                    for c in range(NI):
                        ins = pe.matmul(psum[:, 6, j * D:(j + 1) * D], oT[:, c, j * P:(j + 1) * P], wt["wo"][:, c, :],
                                        start=c == 0, stop=c == NI - 1)
                ins.then_inc(B[6].ready, 1)
                pe.wait_ge(z1_l.ready, z1_l.n(s, i) + 1)
                pe.wait_ge(B[6].free, B[6].n(s, i, "sh"))
                for j in range(NT):
                    out_ = psum[:, 6, j * P:(j + 1) * P]
                    ins = pe.matmul(out_, const("shift"), z1[:, j, P:D], start=True, stop=j == 0)
                    if j:
                        ins = pe.matmul(out_, const("edge"), z1[:, j - 1, P:D], start=False, stop=True)
                ins.then_inc(B[6].ready, 1)
                pe.wait_ge(hs_l.ready, hs_l.n(s, i) + 1)
                pe.wait_ge(B[6].free, B[6].n(s, i, "hf"))
                for k in range(KD):
                    for j in range(NT):
                        ins = pe.transpose(psum[:, 6, k * TOK + j * P:k * TOK + (j + 1) * P], hs[:, j, k * P:(k + 1) * P], ident)
                ins.then_inc(B[6].ready, 1)
                pe.wait_ge(B[6].free, B[6].n(s, i, "hf") + 1)
                for m in range(NHC):
                    M = chunk(m)
                    for b, at in ((m % 2, HID), (2 + m % 2, 0)):
                        pe.wait_ge(B[b].free, B[b].n(s, i, f"g{m}"))
                        for k in range(KD):
                            ins = pe.matmul(psum[0:M, b, 0:TOK], wt["w1"][:, k, at + m * P:at + m * P + M], hsT[:, k, :],
                                            start=k == 0, stop=k == KD - 1)
                        ins.then_inc(B[b].ready, 1)
                if more:
                    transpose_h(pe, s, i + 1)
                pe.wait_ge(B[6].free, B[6].n(s, i, "Y2"))
                for b in (2, 3):
                    pe.wait_ge(B[b].free, B[b].n(s, i, f"g{b + 2}") + 1)
                for j in range(NT):
                    for m in range(NHC):
                        M = chunk(m)
                        ins = pe.matmul(psum[:, 6, j * D:(j + 1) * D], hid[0:M, m, j * P:(j + 1) * P], wt["w2"][0:M, m, :],
                                        start=m == 0, stop=m == NHC - 1)
                ins.then_inc(B[6].ready, 1)

        def act(act):
            begin(act, s)
            act.wait_ge(loaded["base"], LOADS["base"])

            def shifted_hT(i):
                b = B[AHEAD]
                act.wait_ge(b.ready, b.n(s, i, "T") + 1)
                act.activation(hT[:, 0, :], psum[:, AHEAD, 0:TOK], ACT.Copy)
                act.activation(hT[:, 1, 1:TOK], psum[:, AHEAD, TOK:2 * TOK - 1], ACT.Copy).then_inc(b.free, 1)

            act.activation(hT[:, 1, 0:1], pad_act[:, 0:1], ACT.Copy)
            shifted_hT(0)
            for i, more in batches(act):
                for j in range(NT):
                    act.wait_ge(rot_l.ready, rot_l.n(s, i, f"{j}"))
                    for b, dst in enumerate((qk[:, 0], qk[:, 1])):
                        act.wait_ge(B[b].ready, B[b].n(s, i, f"{'qk'[b]}{j}") + 1)
                        act.activation(dst.rearrange("p h d -> p (h d)"), bank(b), ACT.Copy).then_inc(B[b].free, 1)
                    act.wait_ge(B[2].ready, B[2].n(s, i, f"v{j}") + 1)
                    act.activation(v[:, j, :], bank(2), ACT.Copy).then_inc(B[2].free, 1)
                    act.wait_ge(B[0].free, B[0].n(s, i, f"q{j}") + 1)
                    act.wait_ge(B[1].free, B[1].n(s, i, f"k{j}") + 1)
                    act.activation(sq.rearrange("p a b c -> p (a b c)"), qk.rearrange("p a b c -> p (a b c)"), ACT.Square).then_inc(sq_l.ready, 1)
                for j in range(NT):
                    for b, n, dst in ((4, "tq", qT), (5, "tk", kT)):
                        act.wait_ge(B[b].ready, B[b].n(s, i, f"{n}{j}") + 1)
                        act.activation(dst[:, :, j * P:(j + 1) * P], bank(b).rearrange("p (a b) -> p a b", a=NI), ACT.Copy).then_inc(B[b].free, 1)

                def exps(j):
                    act.wait_ge(nmax_l.ready, nmax_l.n(s, i, f"S{j}") + 1)
                    for hh in range(WH):
                        ins = act.activation(Pj[j][:, hh, :], Pj[j][:, hh, :], ACT.Exp, scale=QK_SCALE, bias=nmax[:, j, hh:hh + 1],
                                             accum_out=den[:, j, hh:hh + 1])
                    ins.then_inc(E_l.ready, 1)

                def copies(j):
                    for g, group in enumerate(GROUPS):
                        if group[0][0] == j:
                            b = 4 + g % 2
                            act.wait_ge(B[b].ready, B[b].n(s, i, f"p{g}") + 1)
                            x = 4 * (g - 2 * j)
                            act.activation(PT[j][:, x:x + 4, :].rearrange("p a b -> p (a b)"), bank(b), ACT.Copy).then_inc(B[b].free, 1)

                exps(0)
                exps(1)
                copies(0)
                copies(1)
                for j in range(NT):
                    b = 4 + j
                    act.wait_ge(B[b].ready, B[b].n(s, i, f"o{j}") + 1)
                    act.activation(oT[:, :, j * P:(j + 1) * P], bank(b).rearrange("p (a b) -> p a b", a=NI), ACT.Copy).then_inc(B[b].free, 1)
                act.wait_ge(B[6].ready, B[6].n(s, i, "hf") + 1)
                for k in range(KD):
                    ins = act.activation(hsT[:, k, :], psum[:, 6, k * TOK:(k + 1) * TOK], ACT.Identity, scale=col(s + "_g", k), bias=col(s + "_b", k))
                ins.then_inc(B[6].free, 1)
                for m in range(NHC):
                    M, b = chunk(m), m % 2
                    act.wait_ge(B[b].ready, B[b].n(s, i, f"g{m}") + 1)
                    act.wait_ge(B[2 + b].free, B[2 + b].n(s, i, f"g{m}"))
                    act.activation(gel[0:M, b, :], psum[0:M, b, 0:TOK], ACT.Gelu,
                                   bias=cols[0:M, COL_AT[s + "_b1g"][0] + m:COL_AT[s + "_b1g"][0] + m + 1]).then_inc(B[b].free, 1)
                if more:
                    shifted_hT(i + 1)

        def pool(pool):
            begin(pool, s)
            if s == "L1a":
                ln_power(pool, s, 0)
            pool.wait_ge(tables, 1)
            for i, more in batches(pool):
                for j in range(NT):
                    pool.wait_ge(ssq_l.ready, ssq_l.n(s, i, f"{j}") + 1)
                    pool.tensor_tensor(rn, ssq, minus_half[:, 0:2 * WH], ALU.pow).then_inc(rn_l.ready, 1)
                    pool.wait_ge(B[1].free, B[1].n(s, i, f"k{j}") + 1)
                    pool.wait_ge(B[0].free, B[0].n(s, i, f"q{j}") + 1)
                    pool.wait_ge(rot_l.ready, rot_l.n(s, i, f"{j}"))
                    for x, n in enumerate("qk"):
                        for a_, b_ in ((slice(0, HALF), slice(HALF, WD)), (slice(HALF, WD), slice(0, HALF))):
                            ins = pool.tensor_tensor(other[:, x, :, a_], qk[:, x, :, b_],
                                                     sin[n][:, j, a_].unsqueeze(1).broadcast_to([P, WH, HALF]), ALU.mult)
                    ins.then_inc(other_l.ready, 1)
                pool.wait_ge(var_l.ready, var_l.n(s, i) + 1)
                pool.tensor_tensor(rs, var, minus_half[:, 0:NT], ALU.pow).then_inc(rs_l.ready, 1)
                if more and s == "L1a":
                    ln_power(pool, s, i + 1)

        def ahead(dve, i, step):
            if s == "L1a":
                ln_stats(dve, s, i, step, X[:, i])
                ln_apply(dve, s, i, X[:, i])
            else:
                dve.wait_ge(B[AHEAD].ready, B[AHEAD].n(s, i, "T"))
                dve.tensor_copy(h[:], zbuf[:, i]).then_inc(h_l.ready, 1)

        def dve(dve):
            step = Steps()
            begin(dve, s)
            ahead(dve, 0, step)
            for n in "qk":
                scale = row(f"{s}_{n}s")
                c, t = (const(f"{x}_{n}").rearrange("p (j d) -> p j d", j=NT) for x in ("cos", "sin"))
                dve.tensor_tensor(cos[n], c, scale.unsqueeze(1).broadcast_to([P, NT, WD]), ALU.mult).then_inc(dve_steps, step.one())
                for a_, b_ in ((slice(0, HALF), slice(HALF, WD)), (slice(HALF, WD), slice(0, HALF))):
                    ins = dve.tensor_tensor(sin[n][:, :, a_], t[:, :, a_], scale[:, b_].unsqueeze(1).broadcast_to([P, NT, HALF]), ALU.mult)
            ins.then_inc(tables, 1)
            dve.wait_ge(dve_steps, step.done)
            dve.sem_clear(dve_steps)
            for i, more in batches(dve):
                step = Steps()
                for j in range(NT):
                    dve.wait_ge(sq_l.ready, sq_l.n(s, i, f"{j}") + 1)
                    dve.tensor_reduce(ssq, sq.rearrange("p a b c -> p (a b) c"), AXIS_X, ALU.add).then_inc(dve_steps, step.one())
                    dve.wait_ge(dve_steps, step.done)
                    dve.tensor_scalar(ssq, ssq, 1e-24, None, ALU.max).then_inc(ssq_l.ready, 1)
                    if j:
                        for b, n in ((4, "tq"), (5, "tk")):
                            dve.wait_ge(B[b].ready, B[b].n(s, i, f"{n}{j - 1}") + 1)
                    for x, n in enumerate("qk"):
                        dve.tensor_tensor(turned[:, x], qk[:, x], cos[n][:, j].unsqueeze(1).broadcast_to([P, WH, WD]),
                                          ALU.mult).then_inc(dve_steps, step.one())
                    dve.wait_ge(other_l.ready, other_l.n(s, i, f"{j}") + 1)
                    dve.wait_ge(dve_steps, step.done)
                    flat = turned.rearrange("p a b c -> p (a b c)")
                    dve.tensor_tensor(flat, flat, other.rearrange("p a b c -> p (a b c)"), ALU.add).then_inc(rot_l.ready, 1)
                    dve.wait_ge(rot_l.ready, rot_l.n(s, i, f"{j}") + 1)
                    dve.wait_ge(rn_l.ready, rn_l.n(s, i, f"{j}") + 1)
                    t16 = turned.rearrange("p a b c -> p (a b) c")
                    dve.tensor_tensor(t16, t16, rn.unsqueeze(2).broadcast_to([P, 2 * WH, WD]), ALU.mult).then_inc(scaled_l.ready, 1)
                for j in range(NT):
                    mask = const("band") if j else const("causal")
                    for odd in range(2):
                        for c in range(NI):
                            hh = 2 * c + odd
                            if j:
                                b, src = 2 * odd + c // 2, psum[:, 2 * odd + c // 2, (c % 2) * 2 * P:(c % 2 + 1) * 2 * P]
                                first, last = c % 2 == 0, c % 2 == 1
                            else:
                                b, src = 4 + odd, psum[:, 4 + odd, c * P:(c + 1) * P]
                                first, last = c == 0, c == NI - 1
                            if first:
                                dve.wait_ge(B[b].ready, B[b].n(s, i, f"S{j}") + 1)
                                dve.memset(pad[:, b:b + 1], 0.0)
                            ins = dve.tensor_tensor_reduce(out=Pj[j][:, hh, :], in0=src, in1=mask, scale=1.0, scalar=MASKED,
                                                           op0=ALU.add, op1=ALU.max, accum_out=mx[:, j, hh:hh + 1])
                            if last:
                                ins.then_inc(B[b].free, 1)
                    for b in ((0, 1, 2, 3) if j else (4, 5)):
                        dve.wait_ge(B[b].free, B[b].n(s, i, f"S{j}") + 1)
                    dve.tensor_scalar(nmax[:, j, :], mx[:, j, :], -QK_SCALE, None, ALU.mult).then_inc(nmax_l.ready, 1)
                for j in range(NT):
                    dve.wait_ge(E_l.ready, E_l.n(s, i, f"S{j}") + 1)
                    dve.reciprocal(rden[:, j, :], den[:, j, :]).then_inc(dve_steps, step.one())
                    dve.wait_ge(dve_steps, step.done)
                    dve.wait_ge(B[6].ready, B[6].n(s, i, f"O{j}") + 1)
                    dve.tensor_tensor(o[:, j, :].rearrange("p (h d) -> p h d", d=WD), bank(6).rearrange("p (h d) -> p h d", d=WD),
                                      rden[:, j, :].unsqueeze(2).broadcast_to([P, WH, WD]), ALU.mult).then_inc(B[6].free, 1)
                    dve.wait_ge(B[6].free, B[6].n(s, i, f"O{j}") + 1)
                    dve.memset(pad[:, 0:1], 0.0).then_inc(o_l.ready, 1)
                zf, hf = z1.rearrange("p a b -> p (a b)"), h[:].rearrange("p a b -> p (a b)")
                dve.wait_ge(B[6].ready, B[6].n(s, i, "Y") + 1)
                dve.tensor_tensor(zf, bank(6), hf, ALU.add).then_inc(B[6].free, 1)
                dve.wait_ge(B[6].free, B[6].n(s, i, "Y") + 1)
                dve.tensor_copy(hs[:, :, 0:P], z1[:, :, 0:P]).then_inc(z1_l.ready, 1)
                dve.wait_ge(B[6].ready, B[6].n(s, i, "sh") + 1)
                dve.tensor_copy(hs[:, :, P:D], psum[:, 6, 0:NT * P].rearrange("p (a b) -> p a b", a=NT)).then_inc(B[6].free, 1)
                dve.wait_ge(B[6].free, B[6].n(s, i, "sh") + 1)
                dve.wait_ge(z1_l.ready, z1_l.n(s, i) + 1)
                for j in range(NT):
                    dve.bn_stats(st[:, j, :], hs[:, j, :]).then_inc(dve_steps, step.one())
                dve.wait_ge(dve_steps, step.done)
                dve.memset(pad[:, 0:1], 0.0)
                for j in range(NT):
                    dve.bn_aggr(mo[:, j, :], st[:, j, :]).then_inc(dve_steps, step.one())
                dve.wait_ge(dve_steps, step.done)
                dve.tensor_scalar(var, mo[:, :, 1], EPS, None, ALU.add).then_inc(var_l.ready, 1)
                dve.wait_ge(rs_l.ready, rs_l.n(s, i) + 1)
                for j in range(NT):
                    ins = dve.tensor_scalar(hs[:, j, :], hs[:, j, :], mo[:, j, 0:1], rs[:, j:j + 1], ALU.subtract, ALU.mult)
                ins.then_inc(hs_l.ready, 1)
                if more:
                    ahead(dve, i + 1, step)
                for m in range(NHC):
                    M, b = chunk(m), 2 + m % 2
                    dve.wait_ge(B[b].ready, B[b].n(s, i, f"g{m}") + 1)
                    dve.wait_ge(B[b - 2].free, B[b - 2].n(s, i, f"g{m}") + 1)
                    k = COL_AT[s + "_b1a"][0] + m
                    dve.scalar_tensor_tensor(hid[0:M, m, :], psum[0:M, b, 0:TOK], cols[0:M, k:k + 1], gel[0:M, m % 2, :],
                                             ALU.add, ALU.mult).then_inc(B[b].free, 1)
                dve.wait_ge(B[6].ready, B[6].n(s, i, "Y2") + 1)
                dve.tensor_tensor(zf, bank(6), zf, ALU.add).then_inc(B[6].free, 1)
                dve.wait_ge(B[6].free, B[6].n(s, i, "Y2") + 1)
                b2 = row(s + "_b2").unsqueeze(1).broadcast_to([P, NT, D])
                if s == "L1a":
                    dve.tensor_tensor(zbuf[:, i], z1, b2, ALU.add).then_inc(updated, 1)
                else:
                    dve.tensor_tensor(z1, z1, b2, ALU.add).then_inc(dve_steps, step.one())
                    dve.wait_ge(dve_steps, step.done)
                    dve.tensor_tensor(X[:, i], z1, X[:, i], ALU.add).then_inc(updated, 1)
                dve.wait_ge(dve_steps, step.done)
                dve.sem_clear(dve_steps)
        return dict(tensor=pe, scalar=act, gpsimd=pool, vector=dve)
    FFNS["L1a"] = FFNS["L1b"] = local

    MAKE = dict(L0x=cross, L1x=single, L2x=cross, L3x=cross)
    for f in ("L0f", "L1a", "L1b", "L2f", "L3f"):
        MAKE[f] = FFNS[f] if f in FFNS else None
    parts = [MAKE[s](s) for s in stages]
    block = ctx.enter_context(nc.Block())

    @block.sync
    def _(sp):
        x = a["x"].rearrange("(b t p) d -> b p t d", p=P, t=NT)
        for b in range(nb):
            sp.dma_start(X[:, b], x[b]).then_inc(loaded["base"], 16)
        sp.dma_start(consts[:], a["consts"]).then_inc(loaded["base"], 16)
        sp.dma_start(cols[:], a["cols"]).then_inc(loaded["base"], 16)
        sp.dma_start(rows[:], a["rows"].partition_broadcast(P)).then_inc(loaded["base"], 16)
        sp.dma_start(mask_bytes[:], a["mask"].rearrange("(j p) k -> p j k", p=P)).then_inc(loaded["base"], 16)

        for s, part in zip(stages, parts):
            if "sync" in part:
                part["sync"](sp)
        sp.wait_ge(updated, len(stages) * nb)
        for b in range(nb):
            sp.dma_start(out.rearrange("(b t p) d -> b p t d", p=P, t=NT)[b], X[:, b]).then_inc(stored, 16)
        sp.wait_ge(stored, 16 * nb)

    @block.gpsimd
    def _(pool):
        for s, part in zip(stages, parts):
            load_weights(pool, s)
            part["gpsimd"](pool)

    @block.scalar
    def _(act):
        act.wait_ge(made, 1)
        for part in parts:
            part["scalar"](act)

    @block.tensor
    def _(pe):
        for part in parts:
            part["tensor"](pe)

    @block.vector
    def _(dve):
        dve.memset(minus_half[:], -0.5)
        dve.memset(pad_act[:], 0.0)
        dve.memset(pad[:], 0.0).then_inc(made, 1)
        dve.wait_ge(loaded["base"], LOADS["base"])
        for part in parts:
            part["vector"](dve)


def layout(inputs):
    import numpy as np

    g = {k: np.asarray(v) for k, v in inputs.items()}
    a = {"x": g["x"].reshape(-1, D), "ctx": g["ctx_1024"],
         "mask": g["mask_1x1xSxS2_bk0"].reshape(TOK, S2)}
    for s, names in (("L0x", ("L0_xattn_Wq", "L0_xattn_Wk", "L0_xattn_Wv", "L0_xattn_Wo")),
                     ("L2x", ("L2_xattn_W_q", "L2_xattn_W_k", "L2_xattn_W_v", "L2_xattn_W_o")),
                     ("L3x", ("L3_xattn_wq", "L3_xattn_wk", "L3_xattn_wv", "L3_xattn_wo"))):
        for n, name in zip(("wq", "wk", "wv", "wo"), names):
            a[f"{s}_{n}"] = g[name]
    for n in "qkv":
        a[f"L1x_w{n}"] = g[f"L1_xattn_W{n}"].T
    a["L0f_wg"], a["L0f_wu"], a["L0f_wd"], a["L0f_wq"] = (g[f"L0_ffn_{n}"] for n in ("Wg", "Wu", "Wd", "Wq"))
    a["L0f_keys"] = g["L0_ffn_keys"].transpose(2, 0, 3, 1).reshape(4, P, NKEYS)
    a["L0f_down"], a["L0f_up"] = g["L0_ffn_down_embed"].T, g["L0_ffn_up_embed"]
    for l, s in enumerate(("L1a", "L1b")):
        for n in ("wqkv", "wo", "w1", "w2"):
            a[f"{s}_{n}"] = g[f"L1_ffn_{n}"][l]
    a["L2f_fc"], a["L2f_proj"] = g["L2_ffn_W_fc"].T, g["L2_ffn_W_proj"].T
    a["L3f_router"] = g["L3_ffn_router_w"].T
    for n in "gud":
        shared, routed = g[f"L3_ffn_s{n}"], g[f"L3_ffn_e{n}"]
        a[f"L3f_{n}"] = np.concatenate([shared[None], routed]).transpose(0, 2, 1)

    def column(v, k):
        return np.concatenate([v, np.zeros(k * P - v.size, v.dtype)]).reshape(k, P).T

    c = {f"{s}_b{n}": g[f"{s[:2]}_xattn_b{n}"] for s in ("L0x", "L1x", "L3x") for n in "qk"}
    c.update(L0f_bg=g["L0_ffn_bg"], L0f_bu=g["L0_ffn_bu"], L2f_w=g["L2_ffn_ln_w"], L2f_b=g["L2_ffn_ln_b"])
    r = {f"{s}_b{n}": g[f"{s[:2]}_xattn_b{n}"] for s in ("L0x", "L3x") for n in "vo"}
    r.update(L0f_bd=g["L0_ffn_bd"], L1x_bv=g["L1_xattn_bv"])
    for l, s in enumerate(("L1a", "L1b")):
        b1 = g["L1_ffn_b1"][l]
        c.update({f"{s}_g": g["L1_ffn_ln_g"][l], f"{s}_b": g["L1_ffn_ln_b"][l], f"{s}_b1a": b1[:HID], f"{s}_b1g": b1[HID:]})
        r.update({f"{s}_b2": g["L1_ffn_b2"][l], f"{s}_qs": g["L1_ffn_q_scale"][l], f"{s}_ks": g["L1_ffn_k_scale"][l]})
    a["cols"] = np.concatenate([column(c[n], k) for n, k in COLS.items()], axis=1)
    a["rows"] = np.concatenate([r[n] for n in ROWS])
    a["consts"] = constants()
    return {k: np.ascontiguousarray(v) for k, v in a.items()}


def constants():
    import numpy as np

    p, f32 = np.arange(P)[:, None], np.float32
    q, j = p, np.arange(P)[None, :]
    j2 = np.arange(2 * P)[None, :]
    half = np.arange(0, WD, 2, dtype=f32)
    inv_freq = (f32(1.0) / f32(10000.0) ** (half / f32(WD))).astype(f32)
    t = np.arange(TOK, dtype=f32)
    freqs = t[:, None] * inv_freq[None, :]
    freqs = np.concatenate([freqs, freqs], axis=-1)
    base = (half + f32(0.4 * WD)) / f32(1.4 * WD)
    power = (t - f32(TOK // 2)) / f32(P // 2)
    scale = base[None, :] ** power[:, None]
    scale = np.concatenate([scale, scale], axis=-1)
    cos, sin = np.cos(freqs), np.sin(freqs)
    sin = sin * np.where(np.arange(WD) < WD // 2, -1, 1)

    def tokens(v):
        return v.reshape(NT, P, WD).transpose(1, 0, 2).reshape(P, NT * WD)

    c = dict(iota=np.broadcast_to(np.arange(NE), (P, NE)), ident=np.eye(P), headmask=p // HD == np.arange(P // HD)[None, :],
             causal=np.where(j > q, MASKED, 0), band=np.where((j2 > P + q) | (j2 < q), MASKED, 0),
             shift=j == p + 1, edge=(p == P - 1) & (j == 0),
             cos_q=tokens(cos * scale), sin_q=tokens(sin * scale),
             cos_k=tokens(cos / scale), sin_k=tokens(sin / scale))
    return np.concatenate([c[n].astype(f32) for n in CONSTS], axis=1)


def kernel(**inputs):
    import numpy as np
    import concourse.bacc as bacc
    from concourse.bass_utils import run_bass_kernel_spmd

    nc = bacc.Bacc("TRN2", target_bir_lowering=False, num_devices=1)
    arrays = layout(inputs)
    a = {n: nc.dram_tensor(f"in_{n}", v.shape, U8 if v.dtype == bool else F32, kind="ExternalInput").ap()
         for n, v in arrays.items()}
    out = nc.dram_tensor("out", (NB * TOK, D), F32, kind="ExternalOutput").ap()
    build(nc, a, out)
    r = run_bass_kernel_spmd(nc, [{f"in_{n}": v for n, v in arrays.items()}], core_ids=[0])
    return r.results[0]["out"].reshape(NB, TOK, D)
```

```python
import concourse.bass as bass
from concourse import mybir
from contextlib import ExitStack

F32 = mybir.dt.float32
U8 = mybir.dt.uint8
ALU = mybir.AluOpType
ACT = mybir.ActivationFunctionType
AXIS_X = mybir.AxisListType.X

P = 128
D = 256
KD = D // P
NB = 16
TOK = 256
NT = TOK // P
S2 = 77
H = 16
HD = D // H
GRP = 4
EPS = 1e-5

FF0 = 1024
NEXP = 1024
PH = 4
NKEYS = 64
TOPK = 8
PROWS = NEXP // NKEYS

WH = 8
WD = 64
INNER = WH * WD
HID = 682
NHC = 6
HREM = HID - 5 * P
QK_SCALE = 8.0
MASKED = -1e30

FF2 = 1024
NE = 8
FF3 = 512

STAGES = ["L0x", "L0f", "L1x", "L1f", "L2x", "L2f", "L3x", "L3f"]

COLS = dict(L0x_bq=2, L0x_bk=2, L0f_bg=8, L0f_bu=8, L1x_bq=2, L1x_bk=2,
            L1a_g=2, L1a_b=2, L1a_b1a=6, L1a_b1g=6, L1b_g=2, L1b_b=2, L1b_b1a=6, L1b_b1g=6,
            L2f_w=8, L2f_b=8, L3x_bq=2, L3x_bk=2)
ROWS = dict(L0x_bv=D, L0x_bo=D, L0f_bd=D, L1x_bv=D, L1a_b2=D, L1b_b2=D, L1a_qs=WD, L1a_ks=WD,
            L1b_qs=WD, L1b_ks=WD, L3x_bv=D, L3x_bo=D)
CONSTS = dict(iota=NE, ident=P, headmask=P // HD, causal=P, band=2 * P, shift=P, edge=P,
              cos_q=NT * WD, sin_q=NT * WD, cos_k=NT * WD, sin_k=NT * WD)


def places(sizes):
    at, out = 0, {}
    for name, n in sizes.items():
        out[name] = (at, at + n)
        at += n
    return out, at


COL_AT, NCOLS = places(COLS)
ROW_AT, NROWS = places(ROWS)
CONST_AT, NCONSTS = places(CONSTS)

ATTN_W = 4 * KD * D
L1X_W = 3 * KD * D
L1F_W = KD * 3 * INNER + (INNER // P) * D + KD * 2 * HID + NHC * D
L0F_W = 3 * KD * FF0 + KD * 4 * P + 4 * 2 * NKEYS + 2 * KD * NEXP
EXPERT_W = 3 * KD * FF3
ARENA = 38400
AT_L1A = 0
AT_L0F = L1F_W
AT_L1B = AT_L0F
AT_L0X = AT_L0F + L0F_W
AT_L1X = AT_L0X
WORK1 = AT_L0X + ATTN_W
WORK2 = AT_L1B + L1F_W
AT_EXPERT = 0
EARLY = 3
AT_L2X = EARLY * EXPERT_W
AT_L2F = AT_L2X + ATTN_W
AT_L3X = AT_L2F + 2 * KD * FF2
WORK3 = AT_L3X + ATTN_W


class Link:

    def __init__(self, make, name, kinds=("ready",)):
        self.sems = [make(f"{name}_{kind}") for kind in kinds]
        self.ready, self.free = self.sems[0], self.sems[-1]
        self.base, self.uses, self.total = {}, {}, 1

    def plan(self, stage, uses, rounds):
        self.uses[stage] = uses.split()
        self.base[stage] = self.total
        self.total += rounds * len(self.uses[stage])

    def n(self, stage, round_, use=None):
        uses = self.uses[stage]
        return self.base[stage] + round_ * len(uses) + (uses.index(use) if use else 0)


class Steps:

    def __init__(self):
        self.done = 0

    def one(self):
        self.done += 1
        return 1


def build(nc, a, out, nb=NB, stages=STAGES):
    with ExitStack() as ctx:
        program(nc, a, out, nb, stages, ctx)


def program(nc, a, out, nb, stages, ctx):
    def sem(name):
        return ctx.enter_context(nc.semaphore(name))

    def sbuf(name, shape, dt=F32):
        return ctx.enter_context(nc.sbuf_tensor(name, shape, dt))

    X = sbuf("X", [P, nb, NT, D])
    arena = sbuf("arena", [P, ARENA])
    cols = sbuf("cols", [P, NCOLS])
    rows = sbuf("rows", [P, NROWS])
    consts = sbuf("consts", [P, NCONSTS])
    minus_half = sbuf("minus_half", [P, 2 * NT * WH])
    pad = sbuf("pad", [P, 8])
    pad_act = sbuf("pad_act", [P, 2])
    router = sbuf("router", [P, KD, NE])
    mask_bytes = sbuf("mask_bytes", [P, NT, S2], U8)
    small = sbuf("small", [P, 690])
    psum = ctx.enter_context(nc.psum_tensor("psum", [P, 8, 512], F32))

    def view(at, shape, pattern=None, base=arena, parts=P, **sizes):
        n = 1
        for s in shape:
            n *= s
        v = base[0:parts, at:at + n]
        if len(shape) == 1:
            return v
        names = "abcd"[:len(shape)]
        return v.rearrange(f"p ({' '.join(names)}) -> p {' '.join(names)}", **dict(zip(names[1:], shape[1:])))

    class Area:

        def __init__(self, at, base=arena):
            self.at, self.base = at, base

        def take(self, *shape, parts=P):
            v = view(self.at, shape, base=self.base, parts=parts)
            n = 1
            for s in shape:
                n *= s
            self.at += n
            assert self.at <= self.base.shape[1], self.at
            return v

    def col(name, k=0):
        return cols[:, COL_AT[name][0] + k:COL_AT[name][0] + k + 1]

    def row(name):
        return rows[:, slice(*ROW_AT[name])]

    def const(name):
        return consts[:, slice(*CONST_AT[name])]

    ident = const("ident")

    def bank(b, n=512, parts=P):
        return psum[0:parts, b, 0:n]

    def attn_weights(at):
        area = Area(at)
        return {n: area.take(KD, D) for n in ("wq", "wk", "wv", "wo")}

    W = {"L0x": attn_weights(AT_L0X), "L2x": attn_weights(AT_L2X), "L3x": attn_weights(AT_L3X)}
    area = Area(AT_L1X)
    W["L1x"] = {n: area.take(KD, D) for n in ("wq", "wk", "wv")}
    area = Area(AT_L0F)
    W["L0f"] = dict(wg=area.take(KD, FF0), wu=area.take(KD, FF0), wd=area.take(FF0 // P, D),
                    wq=area.take(KD, 4 * P), keys=area.take(4, 2 * NKEYS),
                    down=area.take(KD, NEXP), up=area.take(NEXP // P, D))
    for s, at in (("L1a", AT_L1A), ("L1b", AT_L1B)):
        area = Area(at)
        W[s] = dict(wqkv=area.take(KD, 3 * INNER), wo=area.take(INNER // P, D),
                    w1=area.take(KD, 2 * HID), w2=area.take(NHC, D))
    area = Area(AT_L2F)
    W["L2f"] = dict(fc=area.take(KD, FF2), proj=area.take(FF2 // P, D))
    area = Area(AT_EXPERT)
    W["L3f"] = [dict(g=area.take(KD, FF3), u=area.take(KD, FF3), d=area.take(FF3 // P, D)) for _ in range(NE + 1)]

    LATE = {f"L3f_expert{e}": e for e in range(EARLY, NE + 1)}
    loaded = {s: sem(f"loaded_{s}") for s in ["base"] + list(STAGES) + list(LATE)}
    made = sem("made")
    updated = sem("updated")
    stored = sem("stored")
    dve_steps, act_steps = sem("dve_steps"), sem("act_steps")
    B = [Link(sem, f"bank{b}", ("ready", "free")) for b in range(8)]
    AHEAD = 7
    links = {}

    def link(name):
        if name not in links:
            links[name] = Link(sem, name)
        return links[name]

    number = {s: n for n, s in enumerate(stages)}

    def batches(eng):
        if nb > 1:
            with eng.Fori(0, nb - 1) as i:
                yield i, True
        yield nb - 1, False

    def begin(eng, s):
        eng.wait_ge(updated, number[s] * nb)

    def rounds(eng):
        if nb > 2:
            with eng.Fori(0, nb // 2 - 1) as i:
                yield i, True
        yield nb // 2 - 1, False

    def by_turns(*programs):
        live = list(programs)
        while live:
            for p in list(live):
                try:
                    next(p)
                except StopIteration:
                    live.remove(p)

    def plan(s, banks, **others):
        whole.plan(s, nb)
        plan_uses(s, nb, banks, **others)

    def plan_uses(s, n, banks, **others):
        for b, uses in banks.items():
            B[b].plan(s, uses, n)
        for name, uses in others.items():
            link(name).plan(s, uses, n)

    FFNS = {}
    zeroed = sem("zeroed")

    def weight_loads(s):
        if s in LATE:
            return expert_loads(LATE[s])
        if s == "L3f":
            return [p for e in range(min(EARLY, NE + 1)) for p in expert_loads(e)] + [(router[:], chunks(a["L3f_router"]))]
        if s == "L1f":
            return weight_loads("L1a") + weight_loads("L1b")
        out = []
        for n, dst in W[s].items():
            src = a[f"{s}_{n}"]
            if n == "w2":
                out.append((dst[:, 0:NHC - 1, :], chunks(src[0:(NHC - 1) * P])))
                out.append((dst[0:HREM, NHC - 1, :], src[(NHC - 1) * P:HID]))
            elif n == "keys":
                for q in range(2):
                    r = slice(q * NKEYS, (q + 1) * NKEYS)
                    out.append((dst[r, :, r], src[:, r, :].rearrange("c p k -> p c k")))
            else:
                out.append((dst, chunks(src)))
        return out

    def chunks(src):
        return src.rearrange("(c p) n -> p c n", p=P)

    def expert_loads(e):
        return [(W["L3f"][e][n], chunks(a[f"L3f_{n}"][e])) for n in ("g", "u", "d")]

    LOADS = {s: 16 * len(weight_loads(s)) for s in list(STAGES) + list(LATE)}
    LOADS["base"] = 16 * (nb + 4)
    AFTER = {"L1x": "L0x", "L1f": "L0f", "L2x": "L1f", "L2f": "L1f", "L3x": "L1f", "L3f": "L1f"}
    AFTER.update({n: "L3x" for n in LATE})
    WHEN = {}
    for s in list(STAGES) + list(LATE):
        if s.split("_")[0] in stages:
            before = [x for x in stages if s in AFTER and STAGES.index(x) <= STAGES.index(AFTER[s])]
            k = len(before)
            WHEN.setdefault(stages[min(k, len(stages) - 1)], []).append((s, k))

    def load_weights(eng, at):
        for s, k in WHEN.get(at, []):
            if k:
                eng.wait_ge(updated, k * nb)
            if s == "L0f":
                eng.memset(W[s]["keys"], 0.0).then_inc(zeroed, 1)
                eng.wait_ge(zeroed, 1)
            for dst, src in weight_loads(s):
                eng.dma_start(dst, src).then_inc(loaded[s], 16)

    class Front:

        def __init__(self, x):
            self.bank_at = 4 * x + 3
            self.bank = B[self.bank_at]
            self.h = sbuf(f"h{x}", [P, NT, D])
            self.hT = sbuf(f"hT{x}", [P, KD, TOK])
            self.stats = sbuf(f"stats{x}", [P, NT, 6])
            self.moments = sbuf(f"moments{x}", [P, NT, 2])
            self.variance = sbuf(f"variance{x}", [P, NT])
            self.rstd = sbuf(f"rstd{x}", [P, NT])
            self.variance_l, self.rstd_l, self.h_l = link(f"variance{x}"), link(f"rstd{x}"), link(f"h{x}")

        def plan(self, s, n, uses="h", h_uses="h"):
            self.h_l.plan(s, h_uses, n)
            for l in (self.variance_l, self.rstd_l):
                l.plan(s, uses, n)

        def ln_stats(self, dve, s, i, step, src):
            for j in range(NT):
                dve.bn_stats(self.stats[:, j, :], src[:, j, :]).then_inc(dve_steps, step.one())
            dve.wait_ge(dve_steps, step.done)
            for j in range(NT):
                dve.bn_aggr(self.moments[:, j, :], self.stats[:, j, :]).then_inc(dve_steps, step.one())
            dve.wait_ge(dve_steps, step.done)
            dve.tensor_scalar(self.variance[:], self.moments[:, :, 1], EPS, None, ALU.add).then_inc(self.variance_l.ready, 1)

        def ln_apply(self, dve, s, i, src, use="T"):
            dve.wait_ge(self.rstd_l.ready, self.rstd_l.n(s, i) + 1)
            dve.wait_ge(self.bank.ready, self.bank.n(s, i, use))
            for j in range(NT):
                ins = dve.tensor_scalar(self.h[:, j, :], src[:, j, :], self.moments[:, j, 0:1], self.rstd[:, j:j + 1],
                                        ALU.subtract, ALU.mult)
            ins.then_inc(self.h_l.ready, 1)

        def ln_power(self, pool, s, i):
            pool.wait_ge(self.variance_l.ready, self.variance_l.n(s, i) + 1)
            pool.tensor_tensor(self.rstd[:], self.variance[:], minus_half[:, 0:NT], ALU.pow).then_inc(self.rstd_l.ready, 1)

        def transpose_h(self, pe, s, i):
            b = self.bank
            pe.wait_ge(b.free, b.n(s, i, "T"))
            pe.wait_ge(self.h_l.ready, self.h_l.n(s, i) + 1)
            for k in range(KD):
                for j in range(NT):
                    ins = pe.transpose(psum[:, self.bank_at, k * TOK + j * P:k * TOK + (j + 1) * P],
                                       self.h[:, j, k * P:(k + 1) * P], ident)
            ins.then_inc(b.ready, 1)

        def copy_hT(self, act, s, i):
            b = self.bank
            act.wait_ge(b.ready, b.n(s, i, "T") + 1)
            act.activation(self.hT[:].rearrange("p a b -> p (a b)"), bank(self.bank_at), ACT.Copy).then_inc(b.free, 1)

        def need_hT(self, pe, s, i):
            pe.wait_ge(self.bank.free, self.bank.n(s, i, "T") + 1)

    front = [Front(x) for x in range(2)]
    whole = front[1]
    h, hT = whole.h, whole.hT
    ln_stats, ln_apply, ln_power = whole.ln_stats, whole.ln_apply, whole.ln_power
    transpose_h, copy_hT, need_hT = whole.transpose_h, whole.copy_hT, whole.need_hT
    XR = X[:].rearrange("p (r x) t d -> p r x t d", x=2)
    contexts = a["ctx"].rearrange("(r x) s d -> r x s d", x=2)

    def context_load(sp, s, context):
        def load(i):
            sp.dma_start(context, a["ctx"][i, :, :]).then_inc(link("context").ready, 16)
        begin(sp, s)
        load(0)
        if nb > 1:
            with sp.Fori(1, nb) as i:
                sp.wait_ge(B[AHEAD].ready, B[AHEAD].n(s, i - 1, "c") + 1)
                load(i)

    def context_pe(pe, s, i, w, wt):
        b = B[AHEAD]
        pe.wait_ge(link("context").ready, 16 * link("context").n(s, i) + 1)
        pe.wait_ge(b.free, b.n(s, i, "c"))
        for k in range(KD):
            ins = pe.transpose(psum[:, AHEAD, k * S2:(k + 1) * S2], w["context"][:, k * P:(k + 1) * P],
                               ident[0:S2, 0:S2])
        ins.then_inc(b.ready, 1)
        pe.wait_ge(b.free, b.n(s, i, "K"))
        for m in range(KD):
            for k in range(KD):
                ins = pe.matmul(psum[:, AHEAD, m * S2:(m + 1) * S2], wt["wk"][:, k, m * P:(m + 1) * P],
                                w["contextT"][:, k, :], start=k == 0, stop=k == KD - 1)
        ins.then_inc(b.ready, 1)
        pe.wait_ge(b.free, b.n(s, i, "V"))
        for k in range(KD):
            ins = pe.matmul(psum[0:S2, AHEAD, 0:D], w["contextT"][:, k, :], wt["wv"][:, k, :],
                            start=k == 0, stop=k == KD - 1)
        ins.then_inc(b.ready, 1)

    def context_act(act, s, i, w):
        b = B[AHEAD]
        act.wait_ge(b.ready, b.n(s, i, "c") + 1)
        act.activation(w["contextT"].rearrange("p a b -> p (a b)"), psum[:, AHEAD, 0:KD * S2],
                       ACT.Copy).then_inc(b.free, 1)
        act.wait_ge(b.ready, b.n(s, i, "K") + 1)
        if "Kd" in w:
            act.wait_ge(link("Kd").ready, link("Kd").n(s, i))
        for m in range(KD):
            src = psum[:, AHEAD, m * S2:(m + 1) * S2]
            if s + "_bk" in COL_AT:
                ins = act.activation(w["KT"][:, m, :], src, ACT.Identity, bias=col(s + "_bk", m))
            else:
                ins = act.activation(w["KT"][:, m, :], src, ACT.Copy)
        ins.then_inc(b.free, 1)

    def queries_pe(pe, s, i, wt, b):
        need_hT(pe, s, i)
        pe.wait_ge(B[b].free, B[b].n(s, i, "Q"))
        for m in range(KD):
            for k in range(KD):
                ins = pe.matmul(psum[:, b, m * TOK:(m + 1) * TOK], wt["wq"][:, k, m * P:(m + 1) * P],
                                hT[:, k, :], start=k == 0, stop=k == KD - 1)
        ins.then_inc(B[b].ready, 1)

    def queries_act(act, s, i, QT, b):
        act.wait_ge(B[b].ready, B[b].n(s, i, "Q") + 1)
        for m in range(KD):
            src = psum[:, b, m * TOK:(m + 1) * TOK]
            if s + "_bq" in COL_AT:
                ins = act.activation(QT[:, m, :], src, ACT.Identity, bias=col(s + "_bq", m))
            else:
                ins = act.activation(QT[:, m, :], src, ACT.Copy)
        ins.then_inc(B[b].free, 1)

    def cross(s):
        biased, masked = s != "L2x", s == "L2x"
        area = Area(WORK1 if s == "L0x" else WORK3)
        sm = Area(0, small)
        wt = W[s]
        NG = H // GRP
        keep, fill = sm.take(NT, S2), sm.take(NT, S2)
        steps = [Steps()]

        def stream(x):
            f = front[x]
            c0 = 4 * x
            t, Ob, ahead = (B[c0], B[c0 + 1]), B[c0 + 2], B[c0 + 3]
            Sb = t[0]
            context, contextT, KT = area.take(D, parts=S2), area.take(KD, S2), area.take(KD, S2)
            Kd, V, QT = area.take(H, S2), area.take(H, HD + 1, parts=S2), area.take(KD, TOK)
            at = area.at
            Pj = [area.take(H, S2) for _ in range(NT)]
            O, OT = view(at, (NT, D)), view(at + NT * D, (KD, TOK))
            PT = area.take(H, P, parts=S2)
            nmax, rden = sm.take(NT, H), sm.take(NT, H)
            f.plan(s, nb // 2)
            plan_uses(s, nb // 2, {c0: "Q S0 S1 t00 t02 t10 t12 OT", c0 + 1: "t01 t03 t11 t13 Y", c0 + 2: "O0 O1",
                                   c0 + 3: "T c K V"},
                      **{f"context{x}": "c", f"Kd{x}": "K", f"P{x}": "S0 S1" if masked else "", f"E{x}": "S0 S1"})
            Pl, El, Kdl, context_l = (link(f"{n}{x}") for n in ("P", "E", "Kd", "context"))
            scores = psum[:, c0:c0 + 4, 0:GRP * S2].rearrange("p g (h k) -> p g h k", k=S2)

            def context_pe(pe, i):
                pe.wait_ge(context_l.ready, 16 * context_l.n(s, i) + 1)
                pe.wait_ge(ahead.free, ahead.n(s, i, "c"))
                for k in range(KD):
                    ins = pe.transpose(psum[:, c0 + 3, k * S2:(k + 1) * S2], context[:, k * P:(k + 1) * P],
                                       ident[0:S2, 0:S2])
                ins.then_inc(ahead.ready, 1)

            def keys_pe(pe, i):
                pe.wait_ge(ahead.free, ahead.n(s, i, "K"))
                for m in range(KD):
                    for k in range(KD):
                        ins = pe.matmul(psum[:, c0 + 3, m * S2:(m + 1) * S2], wt["wk"][:, k, m * P:(m + 1) * P],
                                        contextT[:, k, :], start=k == 0, stop=k == KD - 1)
                ins.then_inc(ahead.ready, 1)

            def values_pe(pe, i):
                pe.wait_ge(ahead.free, ahead.n(s, i, "V"))
                for k in range(KD):
                    ins = pe.matmul(psum[0:S2, c0 + 3, 0:D], contextT[:, k, :], wt["wv"][:, k, :],
                                    start=k == 0, stop=k == KD - 1)
                ins.then_inc(ahead.ready, 1)

            def scores_pe(pe, i, j):
                pe.wait_ge(Sb.free, Sb.n(s, i, f"S{j}"))
                for g in range(NG):
                    k = g * GRP * HD // P
                    ins = pe.matmul(psum[:, c0 + g, 0:GRP * S2], QT[:, k, j * P:(j + 1) * P],
                                    Kd[:, g * GRP:(g + 1) * GRP, :].rearrange("p h k -> p (h k)"), start=True, stop=True)
                ins.then_inc(Sb.ready, 1)

            def turn_pe(pe, i, j):
                pe.wait_ge(El.ready, El.n(s, i, f"S{j}") + 1)
                for g in range(NG):
                    b = t[g % 2]
                    pe.wait_ge(b.free, b.n(s, i, f"t{j}{g}"))
                    for q in range(GRP):
                        ins = pe.transpose(psum[0:S2, c0 + g % 2, q * P:(q + 1) * P], Pj[j][:, g * GRP + q, :], ident)
                    ins.then_inc(b.ready, 1)

            def mix_pe(pe, i, j):
                pe.wait_ge(Ob.free, Ob.n(s, i, f"O{j}"))
                for g in (2, 3):
                    pe.wait_ge(t[g % 2].free, t[g % 2].n(s, i, f"t{j}{g}") + 1)
                for hh in range(H):
                    ins = pe.matmul(psum[:, c0 + 2, hh * (HD + 1):(hh + 1) * (HD + 1)], PT[:, hh, :],
                                    V[:, hh, :], start=True, stop=True)
                ins.then_inc(Ob.ready, 1)

            def pe_first(pe):
                f.transpose_h(pe, s, 0)
                context_pe(pe, 0)
                yield
                keys_pe(pe, 0)
                yield
                values_pe(pe, 0)
                yield

            def pe_scores(pe, i):
                f.need_hT(pe, s, i)
                pe.wait_ge(Sb.free, Sb.n(s, i, "Q"))
                for m in range(KD):
                    for k in range(KD):
                        ins = pe.matmul(psum[:, c0, m * TOK:(m + 1) * TOK], wt["wq"][:, k, m * P:(m + 1) * P],
                                        f.hT[:, k, :], start=k == 0, stop=k == KD - 1)
                ins.then_inc(Sb.ready, 1)
                yield
                pe.wait_ge(Kdl.ready, Kdl.n(s, i) + 1)
                pe.wait_ge(t[1].free, t[1].n(s, i))
                pe.wait_ge(Ob.free, Ob.n(s, i))
                pe.wait_ge(ahead.free, ahead.n(s, i, "V") + 1)
                scores_pe(pe, i, 0)
                yield
                scores_pe(pe, i, 1)
                yield

            def pe_values(pe, i, more):
                pe.wait_ge(Sb.free, Sb.n(s, i, "S1") + 1)
                turn_pe(pe, i, 0)
                yield
                mix_pe(pe, i, 0)
                turn_pe(pe, i, 1)
                if more:
                    f.transpose_h(pe, s, i + 1)
                    context_pe(pe, i + 1)
                yield
                mix_pe(pe, i, 1)
                if more:
                    keys_pe(pe, i + 1)
                yield
                if more:
                    values_pe(pe, i + 1)
                pe.wait_ge(Ob.free, Ob.n(s, i, "O1") + 1)
                pe.wait_ge(Sb.free, Sb.n(s, i, "OT"))
                for k in range(KD):
                    for j in range(NT):
                        ins = pe.transpose(psum[:, c0, k * TOK + j * P:k * TOK + (j + 1) * P], O[:, j, k * P:(k + 1) * P], ident)
                ins.then_inc(Sb.ready, 1)
                yield
                pe.wait_ge(t[1].free, t[1].n(s, i, "Y"))
                pe.wait_ge(Sb.free, Sb.n(s, i, "OT") + 1)
                for j in range(NT):
                    for k in range(KD):
                        ins = pe.matmul(psum[:, c0 + 1, j * D:(j + 1) * D], OT[:, k, j * P:(j + 1) * P], wt["wo"][:, k, :],
                                        start=k == 0, stop=k == KD - 1)
                ins.then_inc(t[1].ready, 1)
                yield

            def context_act(act, i):
                act.wait_ge(ahead.ready, ahead.n(s, i, "c") + 1)
                act.activation(contextT.rearrange("p a b -> p (a b)"), psum[:, c0 + 3, 0:KD * S2],
                               ACT.Copy).then_inc(ahead.free, 1)

            def keys_act(act, i):
                act.wait_ge(ahead.ready, ahead.n(s, i, "K") + 1)
                act.wait_ge(Kdl.ready, Kdl.n(s, i))
                for m in range(KD):
                    src = psum[:, c0 + 3, m * S2:(m + 1) * S2]
                    if biased:
                        ins = act.activation(KT[:, m, :], src, ACT.Identity, bias=col(s + "_bk", m))
                    else:
                        ins = act.activation(KT[:, m, :], src, ACT.Copy)
                ins.then_inc(ahead.free, 1)

            def act_first(act):
                f.copy_hT(act, s, 0)
                context_act(act, 0)
                yield
                keys_act(act, 0)
                yield

            def act_scores(act, i):
                act.wait_ge(Sb.ready, Sb.n(s, i, "Q") + 1)
                for m in range(KD):
                    src = psum[:, c0, m * TOK:(m + 1) * TOK]
                    if biased:
                        ins = act.activation(QT[:, m, :], src, ACT.Identity, bias=col(s + "_bq", m))
                    else:
                        ins = act.activation(QT[:, m, :], src, ACT.Copy)
                ins.then_inc(Sb.free, 1)
                yield
                for j in range(NT):
                    if masked:
                        act.wait_ge(Pl.ready, Pl.n(s, i, f"S{j}") + 1)
                    else:
                        act.wait_ge(Sb.free, Sb.n(s, i, f"S{j}") + 1)
                    p = Pj[j].rearrange("p a b -> p (a b)")
                    act.activation(p, p, ACT.Exp, scale=HD ** -0.5).then_inc(El.ready, 1)
                    yield

            def act_values(act, i, more):
                for j in range(NT):
                    for g in range(NG):
                        b = t[g % 2]
                        act.wait_ge(b.ready, b.n(s, i, f"t{j}{g}") + 1)
                        act.activation(PT[:, g * GRP:(g + 1) * GRP, :].rearrange("p a b -> p (a b)"),
                                       bank(c0 + g % 2, parts=S2), ACT.Copy).then_inc(b.free, 1)
                    if more and j:
                        f.copy_hT(act, s, i + 1)
                        context_act(act, i + 1)
                    yield
                if more:
                    keys_act(act, i + 1)
                yield
                act.wait_ge(Sb.ready, Sb.n(s, i, "OT") + 1)
                act.activation(OT.rearrange("p a b -> p (a b)"), bank(c0), ACT.Copy).then_inc(Sb.free, 1)
                yield
                yield

            def spread(pool, i):
                pool.wait_ge(ahead.free, ahead.n(s, i, "K") + 1)
                for m in range(KD):
                    n = P // HD
                    ins = pool.tensor_tensor(Kd[:, m * n:(m + 1) * n, :], KT[:, m, :].unsqueeze(1).broadcast_to([P, n, S2]),
                                             const("headmask").unsqueeze(2).broadcast_to([P, n, S2]), ALU.mult)
                ins.then_inc(Kdl.ready, 1)

            def pool_first(pool):
                f.ln_power(pool, s, 0)
                yield
                spread(pool, 0)
                yield

            def pool_scores(pool, i):
                for _ in range(3):
                    yield

            def pool_values(pool, i, more):
                if more:
                    f.ln_power(pool, s, i + 1)
                yield
                yield
                yield
                if more:
                    spread(pool, i + 1)
                yield
                yield

            def values_dve(dve, i):
                dve.wait_ge(ahead.ready, ahead.n(s, i, "V") + 1)
                src = psum[0:S2, c0 + 3, 0:D].rearrange("p (h d) -> p h d", d=HD)
                if biased:
                    bv = rows[0:S2, slice(*ROW_AT[s + "_bv"])].rearrange("p (h d) -> p h d", d=HD)
                    dve.tensor_tensor(V[:, :, 0:HD], src, bv, ALU.add).then_inc(ahead.free, 1)
                else:
                    dve.tensor_copy(V[:, :, 0:HD], src).then_inc(ahead.free, 1)

            def dve_first(dve):
                step = steps[0]
                dve.memset(V[:, :, HD:HD + 1], 1.0)
                f.ln_stats(dve, s, 0, step, XR[:, 0, x])
                yield
                f.ln_apply(dve, s, 0, XR[:, 0, x])
                yield
                values_dve(dve, 0)
                yield

            def dve_scores(dve, i):
                step = steps[0]
                yield
                for j in range(NT):
                    dve.wait_ge(Sb.ready, Sb.n(s, i, f"S{j}") + 1)
                    p = Pj[j].rearrange("p (g h) k -> p g h k", h=GRP)
                    src = scores
                    if masked:
                        bc = [m[:, j, :].unsqueeze(1).unsqueeze(1).broadcast_to([P, NG, GRP, S2]) for m in (keep, fill)]
                        dve.tensor_tensor(p, scores, bc[0], ALU.mult).then_inc(Sb.free, 1)
                        dve.wait_ge(Sb.free, Sb.n(s, i, f"S{j}") + 1)
                        dve.tensor_tensor(p, p, bc[1], ALU.add).then_inc(dve_steps, step.one())
                        dve.wait_ge(dve_steps, step.done)
                        src = p
                    dve.tensor_reduce(nmax[:, j, :], src, AXIS_X, ALU.max, negate=True).then_inc(dve_steps, step.one())
                    dve.wait_ge(dve_steps, step.done)
                    nm = nmax[:, j, :].rearrange("p (g h) -> p g h", h=GRP).unsqueeze(3).broadcast_to([P, NG, GRP, S2])
                    dve.tensor_tensor(p, src, nm, ALU.add).then_inc(Pl.ready if masked else Sb.free, 1)
                    yield

            def dve_values(dve, i, more):
                step = steps[0]
                if more:
                    f.ln_stats(dve, s, i + 1, step, XR[:, i + 1, x])
                    f.ln_apply(dve, s, i + 1, XR[:, i + 1, x])
                yield
                for j in range(NT):
                    dve.wait_ge(Ob.ready, Ob.n(s, i, f"O{j}") + 1)
                    o = psum[:, c0 + 2, 0:H * (HD + 1)].rearrange("p (h d) -> p h d", d=HD + 1)
                    dve.reciprocal(rden[:, j, :], o[:, :, HD]).then_inc(dve_steps, step.one())
                    dve.wait_ge(dve_steps, step.done)
                    dve.tensor_tensor(O[:, j, :].rearrange("p (h d) -> p h d", d=HD), o[:, :, 0:HD],
                                      rden[:, j, :].unsqueeze(2).broadcast_to([P, H, HD]), ALU.mult).then_inc(Ob.free, 1)
                    yield
                if more:
                    values_dve(dve, i + 1)
                yield
                dve.wait_ge(t[1].ready, t[1].n(s, i, "Y") + 1)
                xt = XR[:, i, x].rearrange("p t d -> p (t d)")
                dve.tensor_tensor(xt, bank(c0 + 1), xt, ALU.add).then_inc(t[1].free, 1)
                dve.wait_ge(t[1].free, t[1].n(s, i, "Y") + 1)
                if biased:
                    dve.tensor_tensor(XR[:, i, x], XR[:, i, x], row(s + "_bo").unsqueeze(1).broadcast_to([P, NT, D]),
                                      ALU.add).then_inc(updated, 1)
                else:
                    dve.memset(pad[:, x:x + 1], 0.0).then_inc(updated, 1)
                yield

            return dict(pe_first=pe_first, pe_scores=pe_scores, pe_values=pe_values,
                        act_first=act_first, act_scores=act_scores, act_values=act_values,
                        pool_first=pool_first, pool_scores=pool_scores, pool_values=pool_values,
                        dve_first=dve_first, dve_scores=dve_scores, dve_values=dve_values,
                        context=context, context_l=context_l, ahead=ahead)

        pair = [stream(x) for x in range(2)]

        def first(name, eng):
            by_turns(*(p[name + "_first"](eng) for p in pair))
            for _ in pair[1][name + "_scores"](eng, 0):
                pass

        def both(name, eng, i, more):
            def leading():
                yield from pair[1][name + "_values"](eng, i, more)
                if more:
                    yield from pair[1][name + "_scores"](eng, i + 1)

            def following():
                yield from pair[0][name + "_scores"](eng, i)
                yield from pair[0][name + "_values"](eng, i, more)
            by_turns(leading(), following())

        def sp(sp):
            begin(sp, s)
            for x, p in enumerate(pair):
                sp.dma_start(p["context"], contexts[0, x]).then_inc(p["context_l"].ready, 16)
            if nb > 2:
                with sp.Fori(1, nb // 2) as i:
                    for x, p in enumerate(pair):
                        sp.wait_ge(p["ahead"].ready, p["ahead"].n(s, i - 1, "c") + 1)
                        sp.dma_start(p["context"], contexts[i, x]).then_inc(p["context_l"].ready, 16)

        def pe(pe):
            begin(pe, s)
            pe.wait_ge(loaded["base"], LOADS["base"])
            pe.wait_ge(made, 1)
            pe.wait_ge(loaded[s], LOADS[s])
            first("pe", pe)
            for i, more in rounds(pe):
                both("pe", pe, i, more)

        def act(act):
            begin(act, s)
            act.wait_ge(loaded["base"], LOADS["base"])
            first("act", act)
            for i, more in rounds(act):
                both("act", act, i, more)

        def pool(pool):
            begin(pool, s)
            pool.wait_ge(loaded["base"], LOADS["base"])
            pool.wait_ge(made, 1)
            first("pool", pool)
            for i, more in rounds(pool):
                both("pool", pool, i, more)

        def dve(dve):
            begin(dve, s)
            steps[0] = step = Steps()
            if masked:
                dve.tensor_copy(keep, mask_bytes[:]).then_inc(dve_steps, step.one())
                dve.wait_ge(dve_steps, step.done)
                dve.tensor_scalar(fill, keep, 1.0, 1e9 * HD ** 0.5, ALU.subtract, ALU.mult).then_inc(dve_steps, step.one())
            first("dve", dve)
            dve.wait_ge(dve_steps, step.done)
            dve.sem_clear(dve_steps)
            for i, more in rounds(dve):
                steps[0] = step = Steps()
                both("dve", dve, i, more)
                dve.wait_ge(dve_steps, step.done)
                dve.sem_clear(dve_steps)
        return dict(sync=sp, tensor=pe, scalar=act, gpsimd=pool, vector=dve)

    def single(s):
        area = Area(WORK1)
        wt = W[s]
        w = dict(context=area.take(D, parts=S2), contextT=area.take(KD, S2), KT=area.take(KD, S2))
        V, QT = area.take(D, parts=S2), area.take(KD, TOK)
        E = [area.take(S2) for _ in range(NT)]
        ET = area.take(NT, P, parts=S2)
        sm = Area(0, small)
        mx, nmax, den, rden = (sm.take(NT) for _ in range(4))
        KT = w["KT"]
        plan(s, {0: "Q t", 1: "S0", 2: "S1", 3: "O0", 4: "O1", AHEAD: "T c K V"},
             context="c", nmax="S0 S1", E="S0 S1")
        nl, El = link("nmax"), link("E")

        def sp(sp):
            context_load(sp, s, w["context"])

        def pe(pe):
            begin(pe, s)
            pe.wait_ge(loaded["base"], LOADS["base"])
            pe.wait_ge(made, 1)
            pe.wait_ge(loaded[s], LOADS[s])
            transpose_h(pe, s, 0)
            context_pe(pe, s, 0, w, wt)
            for i, more in batches(pe):
                queries_pe(pe, s, i, wt, 0)
                pe.wait_ge(B[0].free, B[0].n(s, i, "Q") + 1)
                for j in range(NT):
                    pe.wait_ge(B[1 + j].free, B[1 + j].n(s, i))
                    for k in range(KD):
                        ins = pe.matmul(psum[:, 1 + j, 0:S2], QT[:, k, j * P:(j + 1) * P], KT[:, k, :],
                                        start=k == 0, stop=k == KD - 1)
                    ins.then_inc(B[1 + j].ready, 1)
                pe.wait_ge(B[AHEAD].free, B[AHEAD].n(s, i, "V") + 1)
                if more:
                    transpose_h(pe, s, i + 1)
                    context_pe(pe, s, i + 1, w, wt)
                pe.wait_ge(B[0].free, B[0].n(s, i, "t"))
                for j in range(NT):
                    pe.wait_ge(El.ready, El.n(s, i, f"S{j}") + 1)
                    ins = pe.transpose(psum[0:S2, 0, j * P:(j + 1) * P], E[j], ident)
                ins.then_inc(B[0].ready, 1)
                pe.wait_ge(B[0].free, B[0].n(s, i, "t") + 1)
                for j in range(NT):
                    pe.wait_ge(B[3 + j].free, B[3 + j].n(s, i))
                    pe.matmul(psum[:, 3 + j, 0:D], ET[:, j, :], V, start=True, stop=True).then_inc(B[3 + j].ready, 1)

        def act(act):
            begin(act, s)
            copy_hT(act, s, 0)
            context_act(act, s, 0, w)
            for i, more in batches(act):
                queries_act(act, s, i, QT, 0)
                for j in range(NT):
                    act.wait_ge(nl.ready, nl.n(s, i, f"S{j}") + 1)
                    act.activation(E[j], psum[:, 1 + j, 0:S2], ACT.Exp, scale=D ** -0.5, bias=nmax[:, j:j + 1],
                                   accum_out=den[:, j:j + 1]).then_inc(B[1 + j].free, 1)
                    act.wait_ge(B[1 + j].free, B[1 + j].n(s, i) + 1)
                    act.activation(pad_act[:, 0:1], pad_act[:, 1:2], ACT.Copy).then_inc(El.ready, 1)
                if more:
                    copy_hT(act, s, i + 1)
                    context_act(act, s, i + 1, w)
                act.wait_ge(B[0].ready, B[0].n(s, i, "t") + 1)
                act.activation(ET.rearrange("p a b -> p (a b)"), psum[0:S2, 0, 0:NT * P], ACT.Copy).then_inc(B[0].free, 1)

        def pool(pool):
            begin(pool, s)
            ln_power(pool, s, 0)
            for i, more in batches(pool):
                if more:
                    ln_power(pool, s, i + 1)

        def values(dve, i):
            b = B[AHEAD]
            dve.wait_ge(b.ready, b.n(s, i, "V") + 1)
            dve.tensor_tensor(V, psum[0:S2, AHEAD, 0:D], rows[0:S2, slice(*ROW_AT[s + "_bv"])], ALU.add).then_inc(b.free, 1)

        def dve(dve):
            step = Steps()
            begin(dve, s)
            dve.wait_ge(loaded["base"], LOADS["base"])
            ln_stats(dve, s, 0, step, X[:, 0])
            ln_apply(dve, s, 0, X[:, 0])
            values(dve, 0)
            dve.wait_ge(dve_steps, step.done)
            dve.sem_clear(dve_steps)
            for i, more in batches(dve):
                step = Steps()
                for j in range(NT):
                    dve.wait_ge(B[1 + j].ready, B[1 + j].n(s, i) + 1)
                    dve.tensor_reduce(mx[:, j:j + 1], psum[:, 1 + j, 0:S2], AXIS_X, ALU.max).then_inc(dve_steps, step.one())
                    dve.wait_ge(dve_steps, step.done)
                    dve.tensor_scalar(nmax[:, j:j + 1], mx[:, j:j + 1], -D ** -0.5, None, ALU.mult).then_inc(nl.ready, 1)
                if more:
                    ln_stats(dve, s, i + 1, step, X[:, i + 1])
                    ln_apply(dve, s, i + 1, X[:, i + 1])
                for j in range(NT):
                    dve.wait_ge(El.ready, El.n(s, i, f"S{j}") + 1)
                    dve.reciprocal(rden[:, j:j + 1], den[:, j:j + 1]).then_inc(dve_steps, step.one())
                dve.wait_ge(dve_steps, step.done)
                for j in range(NT):
                    dve.wait_ge(B[3 + j].ready, B[3 + j].n(s, i) + 1)
                    dve.scalar_tensor_tensor(X[:, i, j, :], psum[:, 3 + j, 0:D], rden[:, j:j + 1], X[:, i, j, :],
                                             ALU.mult, ALU.add).then_inc(B[3 + j].free, 1)
                if more:
                    values(dve, i + 1)
                for j in range(NT):
                    dve.wait_ge(B[3 + j].free, B[3 + j].n(s, i) + 1)
                dve.memset(pad[:, 0:1], 0.0).then_inc(updated, 1)
                dve.wait_ge(dve_steps, step.done)
                dve.sem_clear(dve_steps)
        return dict(sync=sp, tensor=pe, scalar=act, gpsimd=pool, vector=dve)
    def ternary(s):
        wt = W[s]
        area = Area(WORK3)
        G = area.take(NT, FF2)
        CT = area.take(FF2 // P, TOK)
        NF = FF2 // P
        ones, scratch = G[:, 0, 0:P], CT.rearrange("p a b -> p (a b)")
        sm = Area(0, small)
        part, total, half, nhalf = sm.take(2, 16), sm.take(2), sm.take(2), sm.take(2)
        st, mo, var, rs = sm.take(NT, 2, 6), sm.take(NT, 2), sm.take(NT), sm.take(NT)
        plan(s, {0: "f0", 2: "f1", 4: "c0 c2", 5: "c1 c3", 6: "Y", AHEAD: "T"},
             inner_variance="f0 f1", inner_rstd="f0 f1", G="f0 f1")
        vl, rl, Gl = link("inner_variance"), link("inner_rstd"), link("G")
        sums, summed, ternaries = sem("weight_sums"), sem("weight_totals"), sem("ternary_weights")
        flat = [wt["fc"].rearrange("p a b -> p (a b)"), wt["proj"].rearrange("p a b -> p (a b)")]

        def pe(pe):
            begin(pe, s)
            pe.wait_ge(loaded["base"], LOADS["base"])
            pe.wait_ge(sums, 1)
            pe.matmul(psum[:, 6, 0:2], ones, total, start=True, stop=True).then_inc(summed, 1)
            transpose_h(pe, s, 0)
            pe.wait_ge(ternaries, 2)
            for i, more in batches(pe):
                need_hT(pe, s, i)
                for j in range(NT):
                    b = 2 * j
                    pe.wait_ge(B[b].free, B[b].n(s, i))
                    for m in range(FF2 // 512):
                        for k in range(KD):
                            ins = pe.matmul(bank(b + m), hT[:, k, j * P:(j + 1) * P], wt["fc"][:, k, m * 512:(m + 1) * 512],
                                            start=k == 0, stop=k == KD - 1)
                    ins.then_inc(B[b].ready, 1)
                if more:
                    transpose_h(pe, s, i + 1)
                pe.wait_ge(Gl.ready, Gl.n(s, i, "f1") + 1)
                for q in range(NF // 2):
                    b = 4 + q % 2
                    pe.wait_ge(B[b].free, B[b].n(s, i, f"c{q}"))
                    for m in range(2):
                        for j in range(NT):
                            ins = pe.transpose(psum[:, b, m * TOK + j * P:m * TOK + (j + 1) * P],
                                               G[:, j, (2 * q + m) * P:(2 * q + m + 1) * P], ident)
                    ins.then_inc(B[b].ready, 1)
                pe.wait_ge(B[6].free, B[6].n(s, i))
                for b, q in ((4, 2), (5, 3)):
                    pe.wait_ge(B[b].free, B[b].n(s, i, f"c{q}") + 1)
                for j in range(NT):
                    for m in range(NF):
                        ins = pe.matmul(psum[:, 6, j * D:(j + 1) * D], CT[:, m, j * P:(j + 1) * P], wt["proj"][:, m, :],
                                        start=m == 0, stop=m == NF - 1)
                ins.then_inc(B[6].ready, 1)

        def act(act):
            begin(act, s)
            copy_hT(act, s, 0)
            for i, more in batches(act):
                for j in range(NT):
                    b = 2 * j
                    act.wait_ge(B[b].ready, B[b].n(s, i) + 1)
                    if j == 0:
                        act.wait_ge(ternaries, 2)
                    act.activation(G[:, j, :].rearrange("p (a b) -> p a b", a=2), psum[:, b:b + 2, :], ACT.Gelu).then_inc(B[b].free, 1)
                if more:
                    copy_hT(act, s, i + 1)
                for q in range(NF // 2):
                    b = 4 + q % 2
                    act.wait_ge(B[b].ready, B[b].n(s, i, f"c{q}") + 1)
                    for m in range(2):
                        c = 2 * q + m
                        ins = act.activation(CT[:, c, :], psum[:, b, m * TOK:(m + 1) * TOK], ACT.Identity,
                                             scale=col("L2f_w", c), bias=col("L2f_b", c))
                    ins.then_inc(B[b].free, 1)

        def pool(pool):
            begin(pool, s)
            ln_power(pool, s, 0)
            for i, more in batches(pool):
                for j in range(NT):
                    pool.wait_ge(vl.ready, vl.n(s, i, f"f{j}") + 1)
                    pool.tensor_tensor(rs[:, j:j + 1], var[:, j:j + 1], minus_half[:, 0:1], ALU.pow).then_inc(rl.ready, 1)
                if more:
                    ln_power(pool, s, i + 1)

        def dve(dve):
            step = Steps()
            begin(dve, s)
            ln_stats(dve, s, 0, step, X[:, 0])
            dve.wait_ge(loaded[s], LOADS[s])
            dve.memset(ones, 1.0).then_inc(dve_steps, step.one())
            for m in range(2):
                dve.tensor_reduce(part[:, m, :], flat[m].rearrange("p (a b) -> p a b", a=16), AXIS_X, ALU.add,
                                  apply_absolute_value=True).then_inc(dve_steps, step.one())
            dve.wait_ge(dve_steps, step.done)
            dve.tensor_reduce(total, part, AXIS_X, ALU.add).then_inc(sums, 1)
            ln_apply(dve, s, 0, X[:, 0])
            dve.wait_ge(summed, 1)
            dve.tensor_scalar(total, psum[:, 6, 0:2], 1.0 / (D * FF2), 1e-6, ALU.mult, ALU.add).then_inc(dve_steps, step.one())
            dve.wait_ge(dve_steps, step.done)
            dve.tensor_scalar(half, total, 0.5, None, ALU.mult).then_inc(dve_steps, step.one())
            dve.tensor_scalar(nhalf, total, -0.5, None, ALU.mult).then_inc(dve_steps, step.one())
            dve.wait_ge(dve_steps, step.done)
            for m in range(2):
                if m:
                    dve.wait_ge(ternaries, 1)
                dve.tensor_scalar(scratch, flat[m], nhalf[:, m:m + 1], None, ALU.is_lt).then_inc(dve_steps, step.one())
                dve.wait_ge(dve_steps, step.done)
                dve.scalar_tensor_tensor(flat[m], flat[m], half[:, m:m + 1], scratch, ALU.is_gt, ALU.subtract).then_inc(ternaries, 1)
            dve.wait_ge(dve_steps, step.done)
            dve.sem_clear(dve_steps)
            for i, more in batches(dve):
                step = Steps()
                for j in range(NT):
                    b = 2 * j
                    dve.wait_ge(B[b].free, B[b].n(s, i) + 1)
                    for m in range(2):
                        dve.bn_stats(st[:, j, m, :], G[:, j, m * 512:(m + 1) * 512]).then_inc(dve_steps, step.one())
                    dve.wait_ge(dve_steps, step.done)
                    dve.memset(pad[:, 0:1], 0.0)
                    dve.bn_aggr(mo[:, j, :], st[:, j].rearrange("p a b -> p (a b)")).then_inc(dve_steps, step.one())
                    dve.wait_ge(dve_steps, step.done)
                    dve.tensor_scalar(var[:, j:j + 1], mo[:, j, 1:2], EPS, None, ALU.add).then_inc(vl.ready, 1)
                if more:
                    ln_stats(dve, s, i + 1, step, X[:, i + 1])
                for j in range(NT):
                    dve.wait_ge(rl.ready, rl.n(s, i, f"f{j}") + 1)
                    dve.tensor_scalar(G[:, j, :], G[:, j, :], mo[:, j, 0:1], rs[:, j:j + 1], ALU.subtract, ALU.mult).then_inc(Gl.ready, 1)
                if more:
                    ln_apply(dve, s, i + 1, X[:, i + 1])
                dve.wait_ge(B[6].ready, B[6].n(s, i) + 1)
                dve.tensor_tensor(X[:, i].rearrange("p a b -> p (a b)"), bank(6), X[:, i].rearrange("p a b -> p (a b)"), ALU.add).then_inc(B[6].free, 1)
                dve.wait_ge(B[6].free, B[6].n(s, i) + 1)
                dve.memset(pad[:, 0:1], 0.0).then_inc(updated, 1)
                dve.wait_ge(dve_steps, step.done)
                dve.sem_clear(dve_steps)
        return dict(tensor=pe, scalar=act, gpsimd=pool, vector=dve)
    FFNS["L2f"] = ternary

    def experts(s):
        NC = FF3 // P
        area = Area((NE + 1) * EXPERT_W)
        hid = [area.take(NC, TOK) for _ in range(2)]
        sg = [area.take(TOK) for _ in range(2)]
        acc = area.take(NT, D)
        sm = Area(0, small)
        logits, top, index, turn = sm.take(NT, NE), sm.take(NT, 8), sm.take(NT, 8), sm.take(NT)
        index_f, weight, share, combine = sm.take(NT, 2), sm.take(NT, 2), sm.take(NT, 2, NE), sm.take(NT, NE)
        index = index.bitcast(mybir.dt.uint32)
        gu = {m: " ".join(f"m{x}" for x in range(m, (NE + 1) * NC, 2)) for m in range(2)}
        plan(s, {0: gu[0], 1: gu[1], 2: gu[0], 3: gu[1], 4: " ".join(f"e{e}" for e in range(0, NE + 1, 2)),
                 5: " ".join(f"e{e}" for e in range(1, NE + 1, 2)), 6: "logits", AHEAD: "T"},
             turn="t", tanh="t")
        turn_l, tanh_l = link("turn"), link("tanh")

        def gate_up(pe, i, e, wt):
            for c in range(NC):
                m = e * NC + c
                for b, n in ((m % 2, "g"), (2 + m % 2, "u")):
                    pe.wait_ge(B[b].free, B[b].n(s, i, f"m{m}"))
                    for k in range(KD):
                        ins = pe.matmul(bank(b, TOK), wt[n][:, k, c * P:(c + 1) * P], hT[:, k, :], start=k == 0, stop=k == KD - 1)
                    ins.then_inc(B[b].ready, 1)

        def down(pe, i, e, wt):
            b = 4 + e % 2
            pe.wait_ge(B[b].free, B[b].n(s, i, f"e{e}"))
            for x in (2, 3):
                m = e * NC + NC - 4 + x
                pe.wait_ge(B[2 + m % 2].free, B[2 + m % 2].n(s, i, f"m{m}") + 1)
            for j in range(NT):
                for c in range(NC):
                    ins = pe.matmul(psum[:, b, j * D:(j + 1) * D], hid[e % 2][:, c, j * P:(j + 1) * P], wt["d"][:, c, :],
                                    start=c == 0, stop=c == NC - 1)
            ins.then_inc(B[b].ready, 1)

        def pe(pe):
            begin(pe, s)
            pe.wait_ge(loaded["base"], LOADS["base"])
            pe.wait_ge(loaded[s], LOADS[s])
            transpose_h(pe, s, 0)
            for i, more in batches(pe):
                need_hT(pe, s, i)
                pe.wait_ge(B[6].free, B[6].n(s, i))
                for j in range(NT):
                    for k in range(KD):
                        ins = pe.matmul(psum[:, 6, j * NE:(j + 1) * NE], hT[:, k, j * P:(j + 1) * P], router[:, k, :],
                                        start=k == 0, stop=k == KD - 1)
                ins.then_inc(B[6].ready, 1)
                for e in range(NE + 1):
                    if e >= EARLY:
                        pe.wait_ge(loaded[f"L3f_expert{e}"], LOADS[f"L3f_expert{e}"])
                    gate_up(pe, i, e, W[s][e])
                    if e:
                        down(pe, i, e - 1, W[s][e - 1])
                if more:
                    transpose_h(pe, s, i + 1)
                down(pe, i, NE, W[s][NE])

        def act(act):
            begin(act, s)
            copy_hT(act, s, 0)
            for i, more in batches(act):
                for m in range((NE + 1) * NC):
                    b = m % 2
                    act.wait_ge(B[b].ready, B[b].n(s, i, f"m{m}") + 1)
                    act.wait_ge(B[2 + b].free, B[2 + b].n(s, i, f"m{m}"))
                    act.activation(sg[b], bank(b, TOK), ACT.Silu).then_inc(B[b].free, 1)
                    if m == 2 * NC - 1:
                        act.wait_ge(turn_l.ready, turn_l.n(s, i) + 1)
                        act.activation(turn, turn, ACT.Tanh, scale=0.5).then_inc(tanh_l.ready, 1)
                if more:
                    copy_hT(act, s, i + 1)

        def pool(pool):
            begin(pool, s)
            ln_power(pool, s, 0)
            for i, more in batches(pool):
                if more:
                    ln_power(pool, s, i + 1)

        def route(dve, i, step):
            dve.wait_ge(B[6].ready, B[6].n(s, i) + 1)
            dve.tensor_copy(logits.rearrange("p a b -> p (a b)"), psum[:, 6, 0:NT * NE]).then_inc(B[6].free, 1)
            dve.wait_ge(B[6].free, B[6].n(s, i) + 1)
            dve.memset(pad[:, 0:1], 0.0)
            for j in range(NT):
                dve.max(top[:, j, :], logits[:, j, :]).then_inc(dve_steps, step.one())
            dve.wait_ge(dve_steps, step.done)
            dve.tensor_tensor(turn, top[:, :, 0], top[:, :, 1], ALU.subtract).then_inc(turn_l.ready, 1)
            for j in range(NT):
                dve.max_index(index[:, j, :], top[:, j, :], logits[:, j, :]).then_inc(dve_steps, step.one())
            dve.wait_ge(dve_steps, step.done)
            dve.tensor_copy(index_f, index[:, :, 0:2]).then_inc(dve_steps, step.one())

        def weigh(dve, i, step):
            dve.wait_ge(tanh_l.ready, tanh_l.n(s, i) + 1)
            dve.tensor_scalar(weight[:, :, 0], turn, 0.5, 0.5, ALU.mult, ALU.add).then_inc(dve_steps, step.one())
            dve.tensor_scalar(weight[:, :, 1], turn, -0.5, 0.5, ALU.mult, ALU.add).then_inc(dve_steps, step.one())
            dve.wait_ge(dve_steps, step.done)
            for j in range(NT):
                for q in range(2):
                    dve.tensor_scalar(share[:, j, q, :], const("iota"), index_f[:, j, q:q + 1], weight[:, j, q:q + 1],
                                      ALU.is_equal, ALU.mult).then_inc(dve_steps, step.one())
            dve.wait_ge(dve_steps, step.done)
            dve.tensor_tensor(combine, share[:, :, 0, :], share[:, :, 1, :], ALU.add).then_inc(dve_steps, step.one())
            dve.wait_ge(dve_steps, step.done)

        def add_expert(dve, i, e):
            b = 4 + e % 2
            if e:
                dve.wait_ge(B[4 + (e - 1) % 2].free, B[4 + (e - 1) % 2].n(s, i, f"e{e - 1}") + 1)
            dve.wait_ge(B[b].ready, B[b].n(s, i, f"e{e}") + 1)
            for j in range(NT):
                y, into = psum[:, b, j * D:(j + 1) * D], X[:, i, j, :] if e == NE else acc[:, j, :]
                if e == 0:
                    ins = dve.tensor_tensor(into, y, X[:, i, j, :], ALU.add)
                else:
                    ins = dve.scalar_tensor_tensor(into, y, combine[:, j, e - 1:e], acc[:, j, :], ALU.mult, ALU.add)
            ins.then_inc(B[b].free, 1)

        def dve(dve):
            step = Steps()
            begin(dve, s)
            ln_stats(dve, s, 0, step, X[:, 0])
            ln_apply(dve, s, 0, X[:, 0])
            dve.wait_ge(dve_steps, step.done)
            dve.sem_clear(dve_steps)
            for i, more in batches(dve):
                step = Steps()
                for e in range(NE + 1):
                    for c in range(NC):
                        m = e * NC + c
                        b = 2 + m % 2
                        dve.wait_ge(B[b].ready, B[b].n(s, i, f"m{m}") + 1)
                        dve.wait_ge(B[b - 2].free, B[b - 2].n(s, i, f"m{m}") + 1)
                        dve.tensor_tensor(hid[e % 2][:, c, :], bank(b, TOK), sg[m % 2], ALU.mult).then_inc(B[b].free, 1)
                    if e == 0:
                        route(dve, i, step)
                    if e == 2:
                        weigh(dve, i, step)
                    if e == 4 and more:
                        ln_stats(dve, s, i + 1, step, X[:, i + 1])
                    if e == 6 and more:
                        ln_apply(dve, s, i + 1, X[:, i + 1])
                    if e:
                        if e == 2:
                            pass
                        add_expert(dve, i, e - 1)
                add_expert(dve, i, NE)
                dve.wait_ge(B[4].free, B[4].n(s, i, f"e{NE}") + 1)
                dve.memset(pad[:, 0:1], 0.0).then_inc(updated, 1)
                dve.wait_ge(dve_steps, step.done)
                dve.sem_clear(dve_steps)
        return dict(tensor=pe, scalar=act, gpsimd=pool, vector=dve)
    FFNS["L3f"] = experts

    def memory(s):
        wt = W[s]
        NC = FF0 // P
        area = Area(WORK1)
        qT, sims = area.take(4, TOK), area.take(NT, 2, PH, NKEYS)
        below = Area(AT_L1A)
        S = [below.take(PROWS, NKEYS) for _ in range(PH)]
        E = [below.take(NEXP) for _ in range(2)]
        assert below.at <= AT_L1A + L1F_W
        G = [area.take(NEXP) for _ in range(NT)]
        C = [area.take(NEXP) for _ in range(NT)]
        CT = area.take(NEXP // P, TOK)
        hid = area.take(NC, TOK)
        sg = [area.take(TOK) for _ in range(2)]
        sm = Area(0, small)
        tx, ty, top = sm.take(PH, TOPK), sm.take(PH, TOPK), sm.take(PH, TOPK)
        grid = sm.take(PH, TOPK, TOPK)
        thr, ntop = sm.take(NT, PH), sm.take(NT, PH)
        shifted, e8 = sm.take(NT, PH, TOPK), sm.take(NT, PH, TOPK)
        z, rz, left = sm.take(NT, PH), sm.take(NT, PH), sm.take(NT, 2)
        heads = " ".join(f"{j}{h}" for j in range(NT) for h in range(PH))
        plan(s, {0: "m0 m2 m4 m6 w0 w1", 1: "m1 m3 m5 m7 w0 w1", 2: "m0 m2 m4 m6", 3: "m1 m3 m5 m7",
                 4: "q s0 c0 c1", 5: "q s1 c0 c1", 6: "Y", AHEAD: "T"},
             shifted="t0 t1", e8="t0 t1", S=heads, exps=heads, picked=heads, G=heads, C="t0 t1")
        shifted_l, e8_l, S_l, E_l, picked_l, G_l, C_l = (link(n) for n in ("shifted", "e8", "S", "exps", "picked", "G", "C"))

        def gate_up(pe, i, m):
            for b, n in ((m % 2, "wg"), (2 + m % 2, "wu")):
                pe.wait_ge(B[b].free, B[b].n(s, i, f"m{m}"))
                for k in range(KD):
                    ins = pe.matmul(bank(b, TOK), wt[n][:, k, m * P:(m + 1) * P], hT[:, k, :], start=k == 0, stop=k == KD - 1)
                ins.then_inc(B[b].ready, 1)

        def pe(pe):
            begin(pe, s)
            pe.wait_ge(loaded["base"], LOADS["base"])
            pe.wait_ge(loaded[s], LOADS[s])
            transpose_h(pe, s, 0)
            for i, more in batches(pe):
                need_hT(pe, s, i)
                for b in (4, 5):
                    pe.wait_ge(B[b].free, B[b].n(s, i, "q"))
                    for x in range(2):
                        c = 2 * (b - 4) + x
                        for k in range(KD):
                            ins = pe.matmul(psum[:, b, x * TOK:(x + 1) * TOK], wt["wq"][:, k, c * P:(c + 1) * P], hT[:, k, :],
                                            start=k == 0, stop=k == KD - 1)
                    ins.then_inc(B[b].ready, 1)
                for m in range(2):
                    gate_up(pe, i, m)
                for b in (4, 5):
                    pe.wait_ge(B[b].free, B[b].n(s, i, "q") + 1)
                for j in range(NT):
                    b = 4 + j
                    pe.wait_ge(B[b].free, B[b].n(s, i, f"s{j}"))
                    for c in range(4):
                        ins = pe.matmul(psum[:, b, c * P:(c + 1) * P], qT[:, c, j * P:(j + 1) * P], wt["keys"][:, c, :],
                                        start=True, stop=True)
                    ins.then_inc(B[b].ready, 1)
                for m in range(2, NC):
                    gate_up(pe, i, m)
                for j in range(NT):
                    for m in range(2):
                        pe.wait_ge(B[m].free, B[m].n(s, i, f"w{j}"))
                        for k in range(KD):
                            ins = pe.matmul(bank(m), hT[:, k, j * P:(j + 1) * P], wt["down"][:, k, m * 512:(m + 1) * 512],
                                            start=k == 0, stop=k == KD - 1)
                        ins.then_inc(B[m].ready, 1)
                if more:
                    transpose_h(pe, s, i + 1)
                pe.wait_ge(B[6].free, B[6].n(s, i))
                for b in (2, 3):
                    pe.wait_ge(B[b].free, B[b].n(s, i, f"m{b + 4}") + 1)
                for j in range(NT):
                    y = psum[:, 6, j * D:(j + 1) * D]
                    for m in range(NC):
                        pe.matmul(y, hid[:, m, j * P:(j + 1) * P], wt["wd"][:, m, :], start=m == 0, stop=False)
                    pe.wait_ge(C_l.ready, C_l.n(s, i, f"t{j}") + 1)
                    for b in (4, 5):
                        pe.wait_ge(B[b].free, B[b].n(s, i, f"c{j}"))
                        for m in range(4):
                            e = (b - 4) * 4 + m
                            ins = pe.transpose(psum[:, b, m * P:(m + 1) * P], C[j][:, e * P:(e + 1) * P], ident)
                        ins.then_inc(B[b].ready, 1)
                    for b in (4, 5):
                        pe.wait_ge(B[b].free, B[b].n(s, i, f"c{j}") + 1)
                        for m in range(4):
                            e = (b - 4) * 4 + m
                            ins = pe.matmul(y, CT[:, e, j * P:(j + 1) * P], wt["up"][:, e, :], start=False, stop=e == NEXP // P - 1)
                ins.then_inc(B[6].ready, 1)

        def act(act):
            begin(act, s)
            act.wait_ge(loaded["base"], LOADS["base"])
            copy_hT(act, s, 0)

            def silu(i, m):
                b = m % 2
                act.wait_ge(B[b].ready, B[b].n(s, i, f"m{m}") + 1)
                act.wait_ge(B[2 + b].free, B[2 + b].n(s, i, f"m{m}"))
                act.activation(sg[b], bank(b, TOK), ACT.Silu, bias=col("L0f_bg", m)).then_inc(B[b].free, 1)

            def exps(i, j, pair):
                if pair == 0:
                    act.wait_ge(shifted_l.ready, shifted_l.n(s, i, f"t{j}") + 1)
                    act.activation(e8[:, j], shifted[:, j], ACT.Exp).then_inc(e8_l.ready, 1)
                for hh in (2 * pair, 2 * pair + 1):
                    act.wait_ge(S_l.ready, S_l.n(s, i, f"{j}{hh}") + 1)
                    if j or hh > 1:
                        act.wait_ge(G_l.ready, G_l.n(s, i, f"{j}{hh}") - 1)
                    act.activation(E[hh % 2], S[hh].rearrange("p a b -> p (a b)"), ACT.Exp, bias=ntop[:, j, hh:hh + 1]).then_inc(E_l.ready, 1)

            def silu_w(i, j):
                for m in range(2):
                    act.wait_ge(B[m].ready, B[m].n(s, i, f"w{j}") + 1)
                    act.activation(C[j][:, m * 512:(m + 1) * 512], bank(m), ACT.Silu).then_inc(B[m].free, 1)

            for i, more in batches(act):
                for b in (4, 5):
                    act.wait_ge(B[b].ready, B[b].n(s, i, "q") + 1)
                    act.activation(qT[:, 2 * (b - 4):2 * (b - 4) + 2, :].rearrange("p a b -> p (a b)"), bank(b), ACT.Copy).then_inc(B[b].free, 1)
                silu(i, 0)
                silu(i, 1)
                for j in range(NT):
                    b = 4 + j
                    act.wait_ge(B[b].ready, B[b].n(s, i, f"s{j}") + 1)
                    act.activation(sims[:, j].rearrange("p a b c -> p (a b c)"), bank(b), ACT.Copy).then_inc(B[b].free, 1)
                silu(i, 2)
                silu(i, 3)
                exps(i, 0, 0)
                silu(i, 4)
                silu(i, 5)
                exps(i, 0, 1)
                silu(i, 6)
                silu(i, 7)
                exps(i, 1, 0)
                silu_w(i, 0)
                exps(i, 1, 1)
                silu_w(i, 1)
                if more:
                    copy_hT(act, s, i + 1)
                for j in range(NT):
                    for b in (4, 5):
                        act.wait_ge(B[b].ready, B[b].n(s, i, f"c{j}") + 1)
                        act.activation(CT[:, 4 * (b - 4):4 * (b - 4) + 4, j * P:(j + 1) * P],
                                       bank(b).rearrange("p (a b) -> p a b", a=4), ACT.Copy).then_inc(B[b].free, 1)

        def pool(pool):
            begin(pool, s)
            ln_power(pool, s, 0)
            for i, more in batches(pool):
                for j in range(NT):
                    pool.wait_ge(B[4 + j].free, B[4 + j].n(s, i, f"s{j}") + 1)
                    for hh in range(PH):
                        if j:
                            pool.wait_ge(picked_l.ready, picked_l.n(s, i, f"{j - 1}{hh}") + 1)
                        x = sims[:, j, 0, hh, 0:PROWS].unsqueeze(2).broadcast_to([P, PROWS, NKEYS])
                        y = sims[:, j, 1, hh, :].unsqueeze(1).broadcast_to([P, PROWS, NKEYS])
                        pool.tensor_tensor(S[hh], x, y, ALU.add).then_inc(S_l.ready, 1)
                    if more and j == 0:
                        ln_power(pool, s, i + 1)

        def dve(dve):
            step = Steps()
            begin(dve, s)
            ln_stats(dve, s, 0, step, X[:, 0])
            ln_apply(dve, s, 0, X[:, 0])
            dve.wait_ge(dve_steps, step.done)
            dve.sem_clear(dve_steps)

            def hidden(i, m):
                b = 2 + m % 2
                dve.wait_ge(B[b].ready, B[b].n(s, i, f"m{m}") + 1)
                dve.wait_ge(B[b - 2].free, B[b - 2].n(s, i, f"m{m}") + 1)
                dve.scalar_tensor_tensor(hid[:, m, :], bank(b, TOK), col("L0f_bu", m), sg[m % 2], ALU.add, ALU.mult).then_inc(B[b].free, 1)

            def select(i, j, step):
                dve.wait_ge(B[4 + j].free, B[4 + j].n(s, i, f"s{j}") + 1)
                dve.memset(pad[:, 0:1], 0.0)
                for hh in range(PH):
                    dve.max(tx[:, hh, :], sims[:, j, 0, hh, :]).then_inc(dve_steps, step.one())
                    dve.max(ty[:, hh, :], sims[:, j, 1, hh, :]).then_inc(dve_steps, step.one())
                dve.wait_ge(dve_steps, step.done)
                dve.tensor_tensor(grid, tx.unsqueeze(3).broadcast_to([P, PH, TOPK, TOPK]),
                                  ty.unsqueeze(2).broadcast_to([P, PH, TOPK, TOPK]), ALU.add).then_inc(dve_steps, step.one())
                dve.wait_ge(dve_steps, step.done)
                dve.memset(pad[:, 0:1], 0.0)
                for hh in range(PH):
                    dve.max(top[:, hh, :], grid[:, hh].rearrange("p a b -> p (a b)")).then_inc(dve_steps, step.one())
                dve.wait_ge(dve_steps, step.done)
                dve.tensor_scalar(ntop[:, j, :], top[:, :, 0], -1.0, None, ALU.mult).then_inc(dve_steps, step.one())
                dve.tensor_copy(thr[:, j, :], top[:, :, TOPK - 1]).then_inc(dve_steps, step.one())
                dve.wait_ge(dve_steps, step.done)
                dve.tensor_tensor(shifted[:, j], top, ntop[:, j, :].unsqueeze(2).broadcast_to([P, PH, TOPK]),
                                  ALU.add).then_inc(shifted_l.ready, 1)

            def normalise(i, j, step):
                dve.wait_ge(e8_l.ready, e8_l.n(s, i, f"t{j}") + 1)
                dve.tensor_reduce(z[:, j, :], e8[:, j], AXIS_X, ALU.add).then_inc(dve_steps, step.one())
                dve.wait_ge(dve_steps, step.done)
                dve.reciprocal(rz[:, j, :], z[:, j, :]).then_inc(dve_steps, step.one())

            def accumulate(i, j, hh, step):
                at = f"{j}{hh}"
                dve.wait_ge(E_l.ready, E_l.n(s, i, at) + 1)
                dve.scalar_tensor_tensor(E[hh % 2], S[hh].rearrange("p a b -> p (a b)"), thr[:, j, hh:hh + 1], E[hh % 2],
                                         ALU.is_ge, ALU.mult).then_inc(picked_l.ready, 1)
                dve.wait_ge(picked_l.ready, picked_l.n(s, i, at) + 1)
                if hh == 0:
                    dve.wait_ge(dve_steps, step.done)
                    dve.tensor_scalar(G[j], E[hh % 2], rz[:, j, hh:hh + 1], None, ALU.mult).then_inc(G_l.ready, 1)
                    return
                dve.wait_ge(G_l.ready, G_l.n(s, i, at))
                last = hh == PH - 1
                dve.scalar_tensor_tensor(G[j], E[hh % 2], rz[:, j, hh:hh + 1], G[j], ALU.mult, ALU.add,
                                         accum_out=left[:, j, 0:1] if last else None).then_inc(G_l.ready, 1)
                if last:
                    dve.wait_ge(G_l.ready, G_l.n(s, i, at) + 1)
                    dve.tensor_scalar(left[:, j, 1:2], left[:, j, 0:1], -1.0, float(PH), ALU.mult, ALU.add).then_inc(dve_steps, step.one())
                    dve.wait_ge(dve_steps, step.done)
                    dve.tensor_tensor(G[j][:, NEXP - 1:NEXP], G[j][:, NEXP - 1:NEXP], left[:, j, 1:2], ALU.add).then_inc(dve_steps, step.one())

            def combine(i, j, step):
                dve.wait_ge(B[1].free, B[1].n(s, i, f"w{j}") + 1)
                dve.wait_ge(B[0].free, B[0].n(s, i, f"w{j}") + 1)
                dve.wait_ge(dve_steps, step.done)
                dve.tensor_tensor(C[j], C[j], G[j], ALU.mult).then_inc(C_l.ready, 1)

            for i, more in batches(dve):
                step = Steps()
                for m in range(2):
                    hidden(i, m)
                select(i, 0, step)
                for m in range(2, 4):
                    hidden(i, m)
                normalise(i, 0, step)
                accumulate(i, 0, 0, step)
                accumulate(i, 0, 1, step)
                for m in range(4, 6):
                    hidden(i, m)
                accumulate(i, 0, 2, step)
                accumulate(i, 0, 3, step)
                if more:
                    ln_stats(dve, s, i + 1, step, X[:, i + 1])
                for m in range(6, 8):
                    hidden(i, m)
                select(i, 1, step)
                normalise(i, 1, step)
                accumulate(i, 1, 0, step)
                accumulate(i, 1, 1, step)
                if more:
                    ln_apply(dve, s, i + 1, X[:, i + 1])
                combine(i, 0, step)
                accumulate(i, 1, 2, step)
                accumulate(i, 1, 3, step)
                combine(i, 1, step)
                dve.wait_ge(B[6].ready, B[6].n(s, i) + 1)
                x = X[:, i].rearrange("p a b -> p (a b)")
                dve.tensor_tensor(x, bank(6), x, ALU.add).then_inc(B[6].free, 1)
                dve.wait_ge(B[6].free, B[6].n(s, i) + 1)
                dve.tensor_tensor(X[:, i], X[:, i], row(s + "_bd").unsqueeze(1).broadcast_to([P, NT, D]), ALU.add).then_inc(updated, 1)
                dve.wait_ge(dve_steps, step.done)
                dve.sem_clear(dve_steps)
        return dict(tensor=pe, scalar=act, gpsimd=pool, vector=dve)
    FFNS["L0f"] = memory

    def local(s):
        NI = INNER // P
        HALF = WD // 2
        area = Area(WORK2)
        cos = [{n: area.take(NT, WD) for n in "qk"} for _ in range(2)]
        sin = [{n: area.take(NT, WD) for n in "qk"} for _ in range(2)]
        sm = Area(0, small)
        tables = sem("rotary_tables")
        steps = [Steps()]
        HEADS_OF = [[0, 1, 2, 3], [4, 5, 6, 7], [0, 1], [2, 3], [4, 5], [6, 7]]
        GROUP_BANK = [2, 3, 1, 2, 3, 1]

        def chunk(m):
            return P if m < NHC - 1 else HREM

        def both_layers(uses):
            return " ".join(u + l for l in "ab" for u in uses.split())

        def stream(x):
            f = front[x]
            c0 = 4 * x
            b = B[c0:c0 + 4]
            h, hT = f.h, f.hT
            at = area.at
            qk0, turned0, other0 = (area.take(2, WH, WD) for _ in range(3))
            mlp = Area(at)
            hid, gel, hs, hsT = mlp.take(NHC, TOK), mlp.take(2, TOK), mlp.take(NT, D), mlp.take(KD, TOK)
            assert mlp.at <= area.at
            v = area.take(NT, INNER)
            at = area.at
            qT, kT = area.take(NI, TOK), area.take(NI, TOK)
            PT = view(at, (2 * WH, P))
            at = area.at
            Pj = [area.take(WH, P), area.take(WH, 2 * P)]
            turned1, qk1, other1 = (view(at + k * WH * P, (2, WH, WD)) for k in range(3))
            qk, turned, other = (qk0, qk1), (turned0, turned1), (other0, other1)
            o, oT = view(at, (NT, INNER)), view(at + WH * P, (NI, TOK))
            z1 = area.take(NT, D)
            ssq, rn = sm.take(NT, 2 * WH), sm.take(NT, 2 * WH)
            mx, nmax, den, rden = sm.take(NT, WH), sm.take(NT, WH), sm.take(NT, WH), sm.take(NT, WH)
            st, mo, var, rs = sm.take(NT, 6), sm.take(NT, 2), sm.take(NT), sm.take(NT)
            f.plan(s, nb // 2, h_uses="ha hb")
            plan_uses(s, nb // 2, {
                c0: both_layers("q0 q1 S0 S1 O0 O1 sh g0 g2 g4 Y2"),
                c0 + 1: both_layers("k0 k1 S0 S1 p2 p5 o0 hf g1 g3 g5"),
                c0 + 2: both_layers("v0 v1 tq0 tq1 S1 p0 p3 o1 g0 g2 g4"),
                c0 + 3: both_layers("T tk0 tk1 S1 p1 p4 Y g1 g3 g5")},
                **{f"{n}{x}": both_layers("0 1") for n in ("squares", "norms", "inverse_norms", "other", "rotated", "scaled", "nmax", "E")},
                **{f"{n}{x}": "a b" for n in ("z1", "hs_variance", "hs_rstd", "hs")})
            sq_l, ssq_l, rn_l, other_l, rot_l, scaled_l, nmax_l, E_l, z1_l, var_l, rs_l, hs_l = (link(f"{n}{x}") for n in (
                "squares", "norms", "inverse_norms", "other", "rotated", "scaled", "nmax", "E", "z1",
                "hs_variance", "hs_rstd", "hs"))

            def free(eng, k, i, use):
                eng.wait_ge(b[k].free, b[k].n(s, i, use))

            def ready(eng, k, i, use):
                eng.wait_ge(b[k].ready, b[k].n(s, i, use) + 1)

            def taken(eng, k, i, use):
                eng.wait_ge(b[k].free, b[k].n(s, i, use) + 1)

            def pe_head(pe, i, l):
                wt, L = W["L1" + l], l
                yield
                free(pe, 3, i, "T" + L)
                pe.wait_ge(f.h_l.ready, f.h_l.n(s, i, "h" + L) + 1)
                for k in range(KD):
                    for j in range(NT):
                        ins = pe.transpose(psum[:, c0 + 3, k * TOK + j * P:k * TOK + (j + 1) * P], h[:, j, k * P:(k + 1) * P], ident)
                ins.then_inc(b[3].ready, 1)
                yield
                taken(pe, 3, i, "T" + L)
                for j in range(NT):
                    for c, n in enumerate("qkv"):
                        free(pe, c, i, f"{n}{j}{L}")
                        for k in range(KD):
                            ins = pe.matmul(bank(c0 + c), hT[:, k, j * P:(j + 1) * P], wt["wqkv"][:, k, c * INNER:(c + 1) * INNER],
                                            start=k == 0, stop=k == KD - 1)
                        ins.then_inc(b[c].ready, 1)
                    yield
                yield
                for j in range(NT):
                    pe.wait_ge(scaled_l.ready, scaled_l.n(s, i, f"{j}{L}") + 1)
                    for c, n in ((2, "tq"), (3, "tk")):
                        free(pe, c, i, f"{n}{j}{L}")
                        src = turned[j][:, c - 2].rearrange("p h d -> p (h d)")
                        for m in range(NI):
                            ins = pe.transpose(psum[:, c0 + c, m * P:(m + 1) * P], src[:, m * P:(m + 1) * P], ident)
                        ins.then_inc(b[c].ready, 1)
                    yield
                for odd in range(2):
                    free(pe, odd, i, "S0" + L)
                for c in (2, 3):
                    free(pe, c, i, "S1" + L)
                for odd in range(2):
                    r = slice(odd * WD, (odd + 1) * WD)
                    for m in range(NI):
                        ins = pe.matmul(psum[:, c0 + odd, m * P:(m + 1) * P], qT[r, m, 0:P], kT[r, m, 0:P], start=True, stop=True)
                    ins.then_inc(b[odd].ready, 1)

                def scores1(odd):
                    r = slice(odd * WD, (odd + 1) * WD)
                    for m in range(NI):
                        c = (0 if odd else 2) + m // 2
                        ins = pe.matmul(psum[:, c0 + c, (m % 2) * 2 * P:(m % 2 + 1) * 2 * P], qT[r, m, P:2 * P], kT[r, m, :], start=True, stop=True)
                        if m % 2:
                            ins.then_inc(b[c].ready, 1)
                scores1(0)
                yield
                for c in (0, 1):
                    free(pe, c, i, "S1" + L)
                scores1(1)
                yield

                def turn(g):
                    c = GROUP_BANK[g]
                    free(pe, c, i, f"p{g}{L}")
                    blocks = [Pj[0][:, hh, :] for hh in HEADS_OF[g]] if g < 2 else \
                        [Pj[1][:, hh, kb * P:(kb + 1) * P] for hh in HEADS_OF[g] for kb in range(2)]
                    for k, block in enumerate(blocks):
                        ins = pe.transpose(psum[:, c0 + c, k * P:(k + 1) * P], block, ident)
                    ins.then_inc(b[c].ready, 1)

                pe.wait_ge(E_l.ready, E_l.n(s, i, "0" + L) + 1)
                turn(0)
                turn(1)
                yield
                free(pe, 0, i, "O0" + L)
                for g in (0, 1):
                    taken(pe, GROUP_BANK[g], i, f"p{g}{L}")
                for hh in range(WH):
                    ins = pe.matmul(psum[:, c0, hh * WD:(hh + 1) * WD], PT[:, hh, :], v[:, 0, hh * WD:(hh + 1) * WD], start=True, stop=True)
                ins.then_inc(b[0].ready, 1)
                pe.wait_ge(E_l.ready, E_l.n(s, i, "1" + L) + 1)
                for g in (2, 3, 4, 5):
                    turn(g)
                yield
                free(pe, 0, i, "O1" + L)
                for g in (3, 4, 5):
                    taken(pe, GROUP_BANK[g], i, f"p{g}{L}")
                for hh in range(WH):
                    for kb in range(2):
                        ins = pe.matmul(psum[:, c0, hh * WD:(hh + 1) * WD], PT[:, 2 * hh + kb, :], v[:, kb, hh * WD:(hh + 1) * WD],
                                        start=kb == 0, stop=kb == 1)
                ins.then_inc(b[0].ready, 1)
                yield
                for j in range(NT):
                    taken(pe, 0, i, f"O{j}{L}")
                    free(pe, 1 + j, i, f"o{j}{L}")
                    for m in range(NI):
                        ins = pe.transpose(psum[:, c0 + 1 + j, m * P:(m + 1) * P], o[:, j, m * P:(m + 1) * P], ident)
                    ins.then_inc(b[1 + j].ready, 1)
                yield

            def pe_tail(pe, i, l):
                wt, L = W["L1" + l], l
                free(pe, 3, i, "Y" + L)
                for j in range(NT):
                    taken(pe, 1 + j, i, f"o{j}{L}")
                    for m in range(NI):
                        ins = pe.matmul(psum[:, c0 + 3, j * D:(j + 1) * D], oT[:, m, j * P:(j + 1) * P], wt["wo"][:, m, :],
                                        start=m == 0, stop=m == NI - 1)
                ins.then_inc(b[3].ready, 1)
                yield
                pe.wait_ge(z1_l.ready, z1_l.n(s, i, L) + 1)
                free(pe, 0, i, "sh" + L)
                for j in range(NT):
                    out_ = psum[:, c0, j * P:(j + 1) * P]
                    ins = pe.matmul(out_, const("shift"), z1[:, j, P:D], start=True, stop=j == 0)
                    if j:
                        ins = pe.matmul(out_, const("edge"), z1[:, j - 1, P:D], start=False, stop=True)
                ins.then_inc(b[0].ready, 1)
                yield
                pe.wait_ge(hs_l.ready, hs_l.n(s, i, L) + 1)
                free(pe, 1, i, "hf" + L)
                for k in range(KD):
                    for j in range(NT):
                        ins = pe.transpose(psum[:, c0 + 1, k * TOK + j * P:k * TOK + (j + 1) * P], hs[:, j, k * P:(k + 1) * P], ident)
                ins.then_inc(b[1].ready, 1)
                yield
                taken(pe, 1, i, "hf" + L)
                for m in range(NHC):
                    M = chunk(m)
                    for c, at in ((m % 2, HID), (2 + m % 2, 0)):
                        free(pe, c, i, f"g{m}{L}")
                        for k in range(KD):
                            ins = pe.matmul(psum[0:M, c0 + c, 0:TOK], wt["w1"][:, k, at + m * P:at + m * P + M], hsT[:, k, :],
                                            start=k == 0, stop=k == KD - 1)
                        ins.then_inc(b[c].ready, 1)
                    if m % 2:
                        yield
                free(pe, 0, i, "Y2" + L)
                for c in (2, 3):
                    taken(pe, c, i, f"g{c + 2}{L}")
                for j in range(NT):
                    for m in range(NHC):
                        M = chunk(m)
                        ins = pe.matmul(psum[:, c0, j * D:(j + 1) * D], hid[0:M, m, j * P:(j + 1) * P], wt["w2"][0:M, m, :],
                                        start=m == 0, stop=m == NHC - 1)
                ins.then_inc(b[0].ready, 1)
                yield

            def act_head(act, i, l):
                L = l
                yield
                ready(act, 3, i, "T" + L)
                act.activation(hT[:, 0, :], psum[:, c0 + 3, 0:TOK], ACT.Copy)
                act.activation(hT[:, 1, 1:TOK], psum[:, c0 + 3, TOK:2 * TOK - 1], ACT.Copy).then_inc(b[3].free, 1)
                yield
                for j in range(NT):
                    for c in range(2):
                        ready(act, c, i, f"{'qk'[c]}{j}{L}")
                        act.activation(qk[j][:, c].rearrange("p h d -> p (h d)"), bank(c0 + c), ACT.Copy).then_inc(b[c].free, 1)
                    ready(act, 2, i, f"v{j}{L}")
                    act.activation(v[:, j, :], bank(c0 + 2), ACT.Copy).then_inc(b[2].free, 1)
                    for c in range(2):
                        taken(act, c, i, f"{'qk'[c]}{j}{L}")
                    act.activation(other[j].rearrange("p a b c -> p (a b c)"), qk[j].rearrange("p a b c -> p (a b c)"),
                                   ACT.Square).then_inc(sq_l.ready, 1)
                    yield
                yield
                for j in range(NT):
                    for c, n, dst in ((2, "tq", qT), (3, "tk", kT)):
                        ready(act, c, i, f"{n}{j}{L}")
                        act.activation(dst[:, :, j * P:(j + 1) * P], bank(c0 + c).rearrange("p (a b) -> p a b", a=NI), ACT.Copy).then_inc(b[c].free, 1)
                    yield
                for j in range(NT):
                    act.wait_ge(nmax_l.ready, nmax_l.n(s, i, f"{j}{L}") + 1)
                    for hh in range(WH):
                        ins = act.activation(Pj[j][:, hh, :], Pj[j][:, hh, :], ACT.Exp, scale=QK_SCALE, bias=nmax[:, j, hh:hh + 1],
                                             accum_out=den[:, j, hh:hh + 1])
                    ins.then_inc(E_l.ready, 1)
                    yield
                for groups in ((0, 1), (2, 3, 4, 5)):
                    for g in groups:
                        c, to = GROUP_BANK[g], 4 * (g if g < 2 else g - 2)
                        ready(act, c, i, f"p{g}{L}")
                        act.activation(PT[:, to:to + 4, :].rearrange("p a b -> p (a b)"), bank(c0 + c), ACT.Copy).then_inc(b[c].free, 1)
                    yield
                yield
                for j in range(NT):
                    ready(act, 1 + j, i, f"o{j}{L}")
                    act.activation(oT[:, :, j * P:(j + 1) * P], bank(c0 + 1 + j).rearrange("p (a b) -> p a b", a=NI), ACT.Copy).then_inc(b[1 + j].free, 1)
                yield

            def act_tail(act, i, l):
                L, name = l, "L1" + l
                yield
                yield
                ready(act, 1, i, "hf" + L)
                for k in range(KD):
                    ins = act.activation(hsT[:, k, :], psum[:, c0 + 1, k * TOK:(k + 1) * TOK], ACT.Identity,
                                         scale=col(name + "_g", k), bias=col(name + "_b", k))
                ins.then_inc(b[1].free, 1)
                yield
                for m in range(NHC):
                    M, c = chunk(m), m % 2
                    k = COL_AT[name + "_b1g"][0] + m
                    ready(act, c, i, f"g{m}{L}")
                    free(act, 2 + c, i, f"g{m}{L}")
                    act.activation(gel[0:M, c, :], psum[0:M, c0 + c, 0:TOK], ACT.Gelu, bias=cols[0:M, k:k + 1]).then_inc(b[c].free, 1)
                    if m % 2:
                        yield
                yield

            def pool_head(pool, i, l):
                L = l
                if l == "a":
                    f.ln_power(pool, s, i)
                yield
                yield
                yield
                for j in range(NT):
                    pool.wait_ge(ssq_l.ready, ssq_l.n(s, i, f"{j}{L}") + 1)
                    pool.tensor_tensor(rn[:, j, :], ssq[:, j, :], minus_half[:, 0:2 * WH], ALU.pow).then_inc(rn_l.ready, 1)
                    for c in range(2):
                        taken(pool, c, i, f"{'qk'[c]}{j}{L}")
                        n = "qk"[c]
                        for a_, b_ in ((slice(0, HALF), slice(HALF, WD)), (slice(HALF, WD), slice(0, HALF))):
                            ins = pool.tensor_tensor(other[j][:, c, :, a_], qk[j][:, c, :, b_],
                                                     sin["ab".index(l)][n][:, j, a_].unsqueeze(1).broadcast_to([P, WH, HALF]), ALU.mult)
                    ins.then_inc(other_l.ready, 1)
                    yield
                for _ in range(8):
                    yield

            def pool_tail(pool, i, l):
                L = l
                yield
                pool.wait_ge(var_l.ready, var_l.n(s, i, L) + 1)
                pool.tensor_tensor(rs, var, minus_half[:, 0:NT], ALU.pow).then_inc(rs_l.ready, 1)
                for _ in range(6):
                    yield

            def dve_head(dve, i, l):
                L, step = l, steps[0]
                if l == "a":
                    f.ln_stats(dve, s, i, step, XR[:, i, x])
                    f.ln_apply(dve, s, i, XR[:, i, x], "Ta")
                yield
                yield
                yield

                def turn(j):
                    dve.wait_ge(sq_l.ready, sq_l.n(s, i, f"{j}{L}") + 1)
                    dve.tensor_reduce(ssq[:, j, :], other[j].rearrange("p a b c -> p (a b) c"), AXIS_X, ALU.add).then_inc(dve_steps, step.one())
                    dve.wait_ge(dve_steps, step.done)
                    dve.tensor_scalar(ssq[:, j, :], ssq[:, j, :], 1e-24, None, ALU.max).then_inc(ssq_l.ready, 1)
                    for c, n in enumerate("qk"):
                        dve.tensor_tensor(turned[j][:, c], qk[j][:, c],
                                          cos["ab".index(l)][n][:, j].unsqueeze(1).broadcast_to([P, WH, WD]), ALU.mult).then_inc(dve_steps, step.one())

                def scale(j):
                    dve.wait_ge(other_l.ready, other_l.n(s, i, f"{j}{L}") + 1)
                    dve.wait_ge(dve_steps, step.done)
                    flat = turned[j].rearrange("p a b c -> p (a b c)")
                    dve.tensor_tensor(flat, flat, other[j].rearrange("p a b c -> p (a b c)"), ALU.add).then_inc(rot_l.ready, 1)
                    dve.wait_ge(rot_l.ready, rot_l.n(s, i, f"{j}{L}") + 1)
                    dve.wait_ge(rn_l.ready, rn_l.n(s, i, f"{j}{L}") + 1)
                    t16 = turned[j].rearrange("p a b c -> p (a b) c")
                    dve.tensor_tensor(t16, t16, rn[:, j, :].unsqueeze(2).broadcast_to([P, 2 * WH, WD]), ALU.mult).then_inc(scaled_l.ready, 1)

                turn(0)
                yield
                turn(1)
                scale(0)
                yield
                scale(1)
                yield
                yield
                for j in range(NT):
                    held = [(0, [0, 2, 4, 6]), (1, [1, 3, 5, 7])] if j == 0 else \
                        [(2, [0, 2]), (3, [4, 6]), (0, [1, 3]), (1, [5, 7])]
                    mask, n = (const("band"), 2 * P) if j else (const("causal"), P)
                    for c, heads in held:
                        ready(dve, c, i, f"S{j}{L}")
                        dve.memset(pad[:, 4 * x + c:4 * x + c + 1], 0.0)
                        for k, hh in enumerate(heads):
                            ins = dve.tensor_tensor_reduce(out=Pj[j][:, hh, :], in0=psum[:, c0 + c, k * n:(k + 1) * n], in1=mask,
                                                           scale=1.0, scalar=MASKED, op0=ALU.add, op1=ALU.max,
                                                           accum_out=mx[:, j, hh:hh + 1])
                        ins.then_inc(b[c].free, 1)
                    for c, _ in held:
                        taken(dve, c, i, f"S{j}{L}")
                    dve.tensor_scalar(nmax[:, j, :], mx[:, j, :], -QK_SCALE, None, ALU.mult).then_inc(nmax_l.ready, 1)
                    yield
                yield
                for j in range(NT):
                    dve.wait_ge(E_l.ready, E_l.n(s, i, f"{j}{L}") + 1)
                    dve.reciprocal(rden[:, j, :], den[:, j, :]).then_inc(dve_steps, step.one())
                    dve.wait_ge(dve_steps, step.done)
                    ready(dve, 0, i, f"O{j}{L}")
                    dve.tensor_tensor(o[:, j, :].rearrange("p (h d) -> p h d", d=WD), bank(c0).rearrange("p (h d) -> p h d", d=WD),
                                      rden[:, j, :].unsqueeze(2).broadcast_to([P, WH, WD]), ALU.mult).then_inc(b[0].free, 1)
                    yield
                yield

            def dve_tail(dve, i, l):
                L, name, step = l, "L1" + l, steps[0]
                zf, hf = z1.rearrange("p a b -> p (a b)"), h[:].rearrange("p a b -> p (a b)")
                ready(dve, 3, i, "Y" + L)
                dve.tensor_tensor(zf, bank(c0 + 3), hf, ALU.add).then_inc(b[3].free, 1)
                taken(dve, 3, i, "Y" + L)
                dve.tensor_copy(hs[:, :, 0:P], z1[:, :, 0:P]).then_inc(z1_l.ready, 1)
                yield
                ready(dve, 0, i, "sh" + L)
                dve.tensor_copy(hs[:, :, P:D], psum[:, c0, 0:NT * P].rearrange("p (a b) -> p a b", a=NT)).then_inc(b[0].free, 1)
                taken(dve, 0, i, "sh" + L)
                dve.wait_ge(z1_l.ready, z1_l.n(s, i, L) + 1)
                for j in range(NT):
                    dve.bn_stats(st[:, j, :], hs[:, j, :]).then_inc(dve_steps, step.one())
                dve.wait_ge(dve_steps, step.done)
                for j in range(NT):
                    dve.bn_aggr(mo[:, j, :], st[:, j, :]).then_inc(dve_steps, step.one())
                dve.wait_ge(dve_steps, step.done)
                dve.tensor_scalar(var, mo[:, :, 1], EPS, None, ALU.add).then_inc(var_l.ready, 1)
                dve.wait_ge(rs_l.ready, rs_l.n(s, i, L) + 1)
                for j in range(NT):
                    ins = dve.tensor_scalar(hs[:, j, :], hs[:, j, :], mo[:, j, 0:1], rs[:, j:j + 1], ALU.subtract, ALU.mult)
                ins.then_inc(hs_l.ready, 1)
                yield
                yield
                for m in range(NHC):
                    M, c = chunk(m), 2 + m % 2
                    ready(dve, c, i, f"g{m}{L}")
                    taken(dve, c - 2, i, f"g{m}{L}")
                    k = COL_AT[name + "_b1a"][0] + m
                    dve.scalar_tensor_tensor(hid[0:M, m, :], psum[0:M, c0 + c, 0:TOK], cols[0:M, k:k + 1], gel[0:M, m % 2, :],
                                             ALU.add, ALU.mult).then_inc(b[c].free, 1)
                    if m % 2:
                        yield
                ready(dve, 0, i, "Y2" + L)
                dve.tensor_tensor(zf, bank(c0), zf, ALU.add).then_inc(b[0].free, 1)
                taken(dve, 0, i, "Y2" + L)
                b2 = row(name + "_b2").unsqueeze(1).broadcast_to([P, NT, D])
                if l == "a":
                    dve.tensor_tensor(h[:], z1, b2, ALU.add).then_inc(f.h_l.ready, 1)
                else:
                    dve.tensor_tensor(z1, z1, b2, ALU.add).then_inc(dve_steps, step.one())
                    dve.wait_ge(dve_steps, step.done)
                    dve.tensor_tensor(XR[:, i, x], z1, XR[:, i, x], ALU.add).then_inc(updated, 1)
                yield
            return dict(pe_head=pe_head, pe_tail=pe_tail, act_head=act_head, act_tail=act_tail,
                        pool_head=pool_head, pool_tail=pool_tail, dve_head=dve_head, dve_tail=dve_tail)

        pair = [stream(x) for x in range(2)]

        def first(name, eng):
            for _ in pair[1][name + "_head"](eng, 0, "a"):
                pass

        def both(name, eng, i, more):
            def leading():
                head, tail = pair[1][name + "_head"], pair[1][name + "_tail"]
                yield from tail(eng, i, "a")
                yield from head(eng, i, "b")
                yield from tail(eng, i, "b")
                if more:
                    yield from head(eng, i + 1, "a")

            def following():
                head, tail = pair[0][name + "_head"], pair[0][name + "_tail"]
                for l in "ab":
                    yield from head(eng, i, l)
                    yield from tail(eng, i, l)
            by_turns(leading(), following())

        def pe(pe):
            begin(pe, s)
            pe.wait_ge(loaded["base"], LOADS["base"])
            pe.wait_ge(loaded[s], LOADS[s])
            first("pe", pe)
            for i, more in rounds(pe):
                both("pe", pe, i, more)

        def act(act):
            begin(act, s)
            act.wait_ge(loaded["base"], LOADS["base"])
            for f in front:
                act.activation(f.hT[:, 1, 0:1], pad_act[:, 0:1], ACT.Copy)
            first("act", act)
            for i, more in rounds(act):
                both("act", act, i, more)

        def pool(pool):
            begin(pool, s)
            pool.wait_ge(tables, 1)
            first("pool", pool)
            for i, more in rounds(pool):
                both("pool", pool, i, more)

        def dve(dve):
            steps[0] = step = Steps()
            begin(dve, s)
            dve.wait_ge(loaded["base"], LOADS["base"])
            for l, name in enumerate(("L1a", "L1b")):
                for n in "qk":
                    scale = row(f"{name}_{n}s")
                    c, t = (const(f"{k}_{n}").rearrange("p (j d) -> p j d", j=NT) for k in ("cos", "sin"))
                    dve.tensor_tensor(cos[l][n], c, scale.unsqueeze(1).broadcast_to([P, NT, WD]), ALU.mult).then_inc(dve_steps, step.one())
                    for a_, b_ in ((slice(0, HALF), slice(HALF, WD)), (slice(HALF, WD), slice(0, HALF))):
                        ins = dve.tensor_tensor(sin[l][n][:, :, a_], t[:, :, a_], scale[:, b_].unsqueeze(1).broadcast_to([P, NT, HALF]), ALU.mult)
            ins.then_inc(tables, 1)
            first("dve", dve)
            dve.wait_ge(dve_steps, step.done)
            dve.sem_clear(dve_steps)
            for i, more in rounds(dve):
                steps[0] = step = Steps()
                both("dve", dve, i, more)
                dve.wait_ge(dve_steps, step.done)
                dve.sem_clear(dve_steps)
        return dict(tensor=pe, scalar=act, gpsimd=pool, vector=dve)
    FFNS["L1f"] = local

    MAKE = dict(L0x=cross, L1x=single, L2x=cross, L3x=cross)
    for f in ("L0f", "L1f", "L2f", "L3f"):
        MAKE[f] = FFNS[f] if f in FFNS else None
    parts = [MAKE[s](s) for s in stages]
    block = ctx.enter_context(nc.Block())

    @block.sync
    def _(sp):
        for l in B + list(links.values()):
            for sm in l.sems:
                sp.sem_inc(sm, 1)
        x = a["x"].rearrange("(b t p) d -> b p t d", p=P, t=NT)
        for b in range(nb):
            sp.dma_start(X[:, b], x[b]).then_inc(loaded["base"], 16)
        sp.dma_start(consts[:], a["consts"]).then_inc(loaded["base"], 16)
        sp.dma_start(cols[:], a["cols"]).then_inc(loaded["base"], 16)
        sp.dma_start(rows[:], a["rows"].partition_broadcast(P)).then_inc(loaded["base"], 16)
        sp.dma_start(mask_bytes[:], a["mask"].rearrange("(j p) k -> p j k", p=P)).then_inc(loaded["base"], 16)

        for s, part in zip(stages, parts):
            if "sync" in part:
                part["sync"](sp)
        sp.wait_ge(updated, len(stages) * nb)
        for b in range(nb):
            sp.dma_start(out.rearrange("(b t p) d -> b p t d", p=P, t=NT)[b], X[:, b]).then_inc(stored, 16)
        sp.wait_ge(stored, 16 * nb)

    @block.gpsimd
    def _(pool):
        for s, part in zip(stages, parts):
            load_weights(pool, s)
            part["gpsimd"](pool)

    @block.scalar
    def _(act):
        act.wait_ge(made, 1)
        for part in parts:
            part["scalar"](act)

    @block.tensor
    def _(pe):
        for part in parts:
            part["tensor"](pe)

    @block.vector
    def _(dve):
        dve.memset(minus_half[:], -0.5)
        dve.memset(pad_act[:], 0.0)
        dve.memset(pad[:], 0.0).then_inc(made, 1)
        dve.wait_ge(loaded["base"], LOADS["base"])
        for part in parts:
            part["vector"](dve)


def layout(inputs):
    import numpy as np

    g = {k: np.asarray(v) for k, v in inputs.items()}
    a = {"x": g["x"].reshape(-1, D), "ctx": g["ctx_1024"],
         "mask": g["mask_1x1xSxS2_bk0"].reshape(TOK, S2)}
    for s, names in (("L0x", ("L0_xattn_Wq", "L0_xattn_Wk", "L0_xattn_Wv", "L0_xattn_Wo")),
                     ("L2x", ("L2_xattn_W_q", "L2_xattn_W_k", "L2_xattn_W_v", "L2_xattn_W_o")),
                     ("L3x", ("L3_xattn_wq", "L3_xattn_wk", "L3_xattn_wv", "L3_xattn_wo"))):
        for n, name in zip(("wq", "wk", "wv", "wo"), names):
            a[f"{s}_{n}"] = g[name]
    for n in "qkv":
        a[f"L1x_w{n}"] = g[f"L1_xattn_W{n}"].T
    a["L0f_wg"], a["L0f_wu"], a["L0f_wd"], a["L0f_wq"] = (g[f"L0_ffn_{n}"] for n in ("Wg", "Wu", "Wd", "Wq"))
    a["L0f_keys"] = g["L0_ffn_keys"].transpose(2, 0, 3, 1).reshape(4, P, NKEYS)
    a["L0f_down"], a["L0f_up"] = g["L0_ffn_down_embed"].T, g["L0_ffn_up_embed"]
    for l, s in enumerate(("L1a", "L1b")):
        for n in ("wqkv", "wo", "w1", "w2"):
            a[f"{s}_{n}"] = g[f"L1_ffn_{n}"][l]
    a["L2f_fc"], a["L2f_proj"] = g["L2_ffn_W_fc"].T, g["L2_ffn_W_proj"].T
    a["L3f_router"] = g["L3_ffn_router_w"].T
    for n in "gud":
        shared, routed = g[f"L3_ffn_s{n}"], g[f"L3_ffn_e{n}"]
        a[f"L3f_{n}"] = np.concatenate([shared[None], routed]).transpose(0, 2, 1)

    def column(v, k):
        return np.concatenate([v, np.zeros(k * P - v.size, v.dtype)]).reshape(k, P).T

    c = {f"{s}_b{n}": g[f"{s[:2]}_xattn_b{n}"] for s in ("L0x", "L1x", "L3x") for n in "qk"}
    c.update(L0f_bg=g["L0_ffn_bg"], L0f_bu=g["L0_ffn_bu"], L2f_w=g["L2_ffn_ln_w"], L2f_b=g["L2_ffn_ln_b"])
    r = {f"{s}_b{n}": g[f"{s[:2]}_xattn_b{n}"] for s in ("L0x", "L3x") for n in "vo"}
    r.update(L0f_bd=g["L0_ffn_bd"], L1x_bv=g["L1_xattn_bv"])
    for l, s in enumerate(("L1a", "L1b")):
        b1 = g["L1_ffn_b1"][l]
        c.update({f"{s}_g": g["L1_ffn_ln_g"][l], f"{s}_b": g["L1_ffn_ln_b"][l], f"{s}_b1a": b1[:HID], f"{s}_b1g": b1[HID:]})
        r.update({f"{s}_b2": g["L1_ffn_b2"][l], f"{s}_qs": g["L1_ffn_q_scale"][l], f"{s}_ks": g["L1_ffn_k_scale"][l]})
    a["cols"] = np.concatenate([column(c[n], k) for n, k in COLS.items()], axis=1)
    a["rows"] = np.concatenate([r[n] for n in ROWS])
    a["consts"] = constants()
    return {k: np.ascontiguousarray(v) for k, v in a.items()}


def constants():
    import numpy as np

    p, f32 = np.arange(P)[:, None], np.float32
    q, j = p, np.arange(P)[None, :]
    j2 = np.arange(2 * P)[None, :]
    half = np.arange(0, WD, 2, dtype=f32)
    inv_freq = (f32(1.0) / f32(10000.0) ** (half / f32(WD))).astype(f32)
    t = np.arange(TOK, dtype=f32)
    freqs = t[:, None] * inv_freq[None, :]
    freqs = np.concatenate([freqs, freqs], axis=-1)
    base = (half + f32(0.4 * WD)) / f32(1.4 * WD)
    power = (t - f32(TOK // 2)) / f32(P // 2)
    scale = base[None, :] ** power[:, None]
    scale = np.concatenate([scale, scale], axis=-1)
    cos, sin = np.cos(freqs), np.sin(freqs)
    sin = sin * np.where(np.arange(WD) < WD // 2, -1, 1)

    def tokens(v):
        return v.reshape(NT, P, WD).transpose(1, 0, 2).reshape(P, NT * WD)

    c = dict(iota=np.broadcast_to(np.arange(NE), (P, NE)), ident=np.eye(P), headmask=p // HD == np.arange(P // HD)[None, :],
             causal=np.where(j > q, MASKED, 0), band=np.where((j2 > P + q) | (j2 < q), MASKED, 0),
             shift=j == p + 1, edge=(p == P - 1) & (j == 0),
             cos_q=tokens(cos * scale), sin_q=tokens(sin * scale),
             cos_k=tokens(cos / scale), sin_k=tokens(sin / scale))
    return np.concatenate([c[n].astype(f32) for n in CONSTS], axis=1)


def kernel(**inputs):
    import numpy as np
    import concourse.bacc as bacc
    from concourse.bass_utils import run_bass_kernel_spmd

    nc = bacc.Bacc("TRN2", target_bir_lowering=False, num_devices=1)
    arrays = layout(inputs)
    a = {n: nc.dram_tensor(f"in_{n}", v.shape, U8 if v.dtype == bool else F32, kind="ExternalInput").ap()
         for n, v in arrays.items()}
    out = nc.dram_tensor("out", (NB * TOK, D), F32, kind="ExternalOutput").ap()
    build(nc, a, out)
    r = run_bass_kernel_spmd(nc, [{f"in_{n}": v for n, v in arrays.items()}], core_ids=[0])
    return r.results[0]["out"].reshape(NB, TOK, D)
```

```python
import concourse.bass as bass
from concourse import mybir
from contextlib import ExitStack

F32 = mybir.dt.float32
U8 = mybir.dt.uint8
ALU = mybir.AluOpType
ACT = mybir.ActivationFunctionType
AXIS_X = mybir.AxisListType.X

P = 128
D = 256
KD = D // P
NB = 16
TOK = 256
NT = TOK // P
S2 = 77
H = 16
HD = D // H
GRP = 4
EPS = 1e-5

FF0 = 1024
NEXP = 1024
PH = 4
NKEYS = 64
TOPK = 8
PROWS = NEXP // NKEYS

WH = 8
WD = 64
INNER = WH * WD
HID = 682
NHC = 6
HREM = HID - 5 * P
QK_SCALE = 8.0
MASKED = -1e30

FF2 = 1024
NE = 8
FF3 = 512

STAGES = ["L0", "L1x", "L1f", "L2x", "L2f", "L3"]

COLS = dict(L0x_bq=2, L0x_bk=2, L0f_bg=8, L0f_bu=8, L1x_bq=2, L1x_bk=2,
            L1a_g=2, L1a_b=2, L1a_b1a=6, L1a_b1g=6, L1b_g=2, L1b_b=2, L1b_b1a=6, L1b_b1g=6,
            L2f_w=8, L2f_b=8, L3x_bq=2, L3x_bk=2)
ROWS = dict(L0x_bv=D, L0x_bo=D, L0f_bd=D, L1x_bv=D, L1a_b2=D, L1b_b2=D, L1a_qs=WD, L1a_ks=WD,
            L1b_qs=WD, L1b_ks=WD, L3x_bv=D, L3x_bo=D)
CONSTS = dict(iota=NE, ident=P, headmask=P // HD, causal=P, band=2 * P, shift=P, edge=P,
              cos_q=NT * WD, sin_q=NT * WD, cos_k=NT * WD, sin_k=NT * WD)


def places(sizes):
    at, out = 0, {}
    for name, n in sizes.items():
        out[name] = (at, at + n)
        at += n
    return out, at


COL_AT, NCOLS = places(COLS)
ROW_AT, NROWS = places(ROWS)
CONST_AT, NCONSTS = places(CONSTS)

ATTN_W = 4 * KD * D
L1X_W = 3 * KD * D
L1F_W = KD * 3 * INNER + (INNER // P) * D + KD * 2 * HID + NHC * D
L0F_W = 3 * KD * FF0 + KD * 4 * P + 4 * 2 * NKEYS + 2 * KD * NEXP
EXPERT_W = 3 * KD * FF3
ARENA = 38400
AT_L1A = 0
AT_L0F = L1F_W
AT_L1B = AT_L0F
AT_L0X = AT_L0F + L0F_W
AT_L1X = AT_L0X
WORK1 = AT_L0X + ATTN_W
WORK2 = AT_L1B + L1F_W
AT_EXPERT = 0
EARLY = 2
AT_L2X = EARLY * EXPERT_W
AT_L2F = AT_L2X + ATTN_W
WORK3 = AT_L2F + 2 * KD * FF2
AT_L3X = (NE + 1) * EXPERT_W
WORK_L3 = AT_L3X + ATTN_W


class Link:

    def __init__(self, make, name, kinds=("ready",)):
        self.sems = [make(f"{name}_{kind}") for kind in kinds]
        self.ready, self.free = self.sems[0], self.sems[-1]
        self.base, self.uses, self.total = {}, {}, 1

    def plan(self, stage, uses, rounds):
        self.uses[stage] = uses.split()
        self.base[stage] = self.total
        self.total += rounds * len(self.uses[stage])

    def n(self, stage, round_, use=None):
        uses = self.uses[stage]
        return self.base[stage] + round_ * len(uses) + (uses.index(use) if use else 0)


class Steps:

    def __init__(self):
        self.done = 0

    def one(self):
        self.done += 1
        return 1


def build(nc, a, out, nb=NB):
    with ExitStack() as ctx:
        program(nc, a, out, nb, ctx)


def program(nc, a, out, nb, ctx):
    def sem(name):
        return ctx.enter_context(nc.semaphore(name))

    def sbuf(name, shape, dt=F32):
        return ctx.enter_context(nc.sbuf_tensor(name, shape, dt))

    X = sbuf("X", [P, nb, NT, D])
    arena = sbuf("arena", [P, ARENA])
    cols = sbuf("cols", [P, NCOLS])
    rows = sbuf("rows", [P, NROWS])
    consts = sbuf("consts", [P, NCONSTS])
    minus_half = sbuf("minus_half", [P, 2 * NT * WH])
    pad = sbuf("pad", [P, 8])
    pad_act = sbuf("pad_act", [P, 2])
    router = sbuf("router", [P, KD, NE])
    mask_bytes = sbuf("mask_bytes", [P, NT, S2], U8)
    small = sbuf("small", [P, 690])
    psum = ctx.enter_context(nc.psum_tensor("psum", [P, 8, 512], F32))

    def view(at, shape, base=arena, parts=P):
        n = 1
        for s in shape:
            n *= s
        v = base[0:parts, at:at + n]
        if len(shape) == 1:
            return v
        names = "abcd"[:len(shape)]
        return v.rearrange(f"p ({' '.join(names)}) -> p {' '.join(names)}", **dict(zip(names[1:], shape[1:])))

    class Area:

        def __init__(self, at, base=arena):
            self.at, self.base = at, base

        def take(self, *shape, parts=P):
            v = view(self.at, shape, base=self.base, parts=parts)
            n = 1
            for s in shape:
                n *= s
            self.at += n
            assert self.at <= self.base.shape[1], self.at
            return v

    def col(name, k=0):
        return cols[:, COL_AT[name][0] + k:COL_AT[name][0] + k + 1]

    def row(name):
        return rows[:, slice(*ROW_AT[name])]

    def const(name):
        return consts[:, slice(*CONST_AT[name])]

    ident = const("ident")

    def bank(b, n=512, parts=P):
        return psum[0:parts, b, 0:n]

    def attn_weights(at):
        area = Area(at)
        return {n: area.take(KD, D) for n in ("wq", "wk", "wv", "wo")}

    W = {"L0x": attn_weights(AT_L0X), "L2x": attn_weights(AT_L2X), "L3x": attn_weights(AT_L3X)}
    area = Area(AT_L1X)
    W["L1x"] = {n: area.take(KD, D) for n in ("wq", "wk", "wv")}
    area = Area(AT_L0F)
    W["L0f"] = dict(wg=area.take(KD, FF0), wu=area.take(KD, FF0), wd=area.take(FF0 // P, D),
                    wq=area.take(KD, 4 * P), keys=area.take(4, 2 * NKEYS),
                    down=area.take(KD, NEXP), up=area.take(NEXP // P, D))
    for s, at in (("L1a", AT_L1A), ("L1b", AT_L1B)):
        area = Area(at)
        W[s] = dict(wqkv=area.take(KD, 3 * INNER), wo=area.take(INNER // P, D),
                    w1=area.take(KD, 2 * HID), w2=area.take(NHC, D))
    area = Area(AT_L2F)
    W["L2f"] = dict(fc=area.take(KD, FF2), proj=area.take(FF2 // P, D))
    area = Area(AT_EXPERT)
    W["L3f"] = [dict(g=area.take(KD, FF3), u=area.take(KD, FF3), d=area.take(FF3 // P, D)) for _ in range(NE + 1)]

    LATE = {f"L3f_expert{e}": e for e in range(EARLY, NE + 1)}
    loaded = {s: sem(f"loaded_{s}") for s in ["base", "rest", "L0x", "L0f", "L1x", "L1f", "L2x", "L2f", "L3x", "L3f"] + list(LATE)}
    made = sem("made")
    updated = sem("updated")
    stored = sem("stored")
    dve_steps = sem("dve_steps")
    B = [Link(sem, f"bank{b}", ("ready", "free")) for b in range(8)]
    links = {}

    def link(name):
        if name not in links:
            links[name] = Link(sem, name)
        return links[name]

    number = {s: n for n, s in enumerate(STAGES)}

    def begin(eng, s):
        eng.wait_ge(updated, number[s] * nb)

    def rounds(eng):
        if nb > 2:
            with eng.Fori(0, nb // 2 - 1) as i:
                yield i, True
        yield nb // 2 - 1, False

    def by_turns(*programs):
        live = list(programs)
        while live:
            for p in list(live):
                try:
                    next(p)
                except StopIteration:
                    live.remove(p)

    def halves_first(pair, name, eng):
        for _ in pair[1][name + "_head"](eng, 0):
            pass

    def halves(pair, name, eng, i, more):
        def leading():
            yield from pair[1][name + "_tail"](eng, i)
            if more:
                yield from pair[1][name + "_head"](eng, i + 1)

        def following():
            yield from pair[0][name + "_head"](eng, i)
            yield from pair[0][name + "_tail"](eng, i)
        by_turns(following(), leading())

    def plan_uses(s, n, banks, **others):
        for b, uses in banks.items():
            B[b].plan(s, uses, n)
        for name, uses in others.items():
            link(name).plan(s, uses, n)

    zeroed = sem("zeroed")

    def weight_loads(s):
        if s in LATE:
            return expert_loads(LATE[s])
        if s == "L3f":
            return [p for e in range(min(EARLY, NE + 1)) for p in expert_loads(e)] + [(router[:], chunks(a["L3f_router"]))]
        if s == "L1f":
            return weight_loads("L1a") + weight_loads("L1b")
        out = []
        for n, dst in W[s].items():
            src = a[f"{s}_{n}"]
            if n == "w2":
                out.append((dst[:, 0:NHC - 1, :], chunks(src[0:(NHC - 1) * P])))
                out.append((dst[0:HREM, NHC - 1, :], src[(NHC - 1) * P:HID]))
            elif n == "keys":
                for q in range(2):
                    r = slice(q * NKEYS, (q + 1) * NKEYS)
                    out.append((dst[r, :, r], src[:, r, :].rearrange("c p k -> p c k")))
            else:
                out.append((dst, chunks(src)))
        return out

    def chunks(src):
        return src.rearrange("(c p) n -> p c n", p=P)

    def expert_loads(e):
        return [(W["L3f"][e][n], chunks(a[f"L3f_{n}"][e])) for n in ("g", "u", "d")]

    LOADED_FOR = {"L0": {"L0x": None, "L0f": None}, "L1x": {"L1x": "L0"}, "L1f": {"L1f": "L0"},
                  "L2x": {"L2x": "L1f"}, "L2f": {"L2f": "L1f"},
                  "L3": {"L3x": "L1f", "L3f": "L1f", **{n: "L2f" for n in LATE}}}
    LOADS = {n: 16 * len(weight_loads(n)) for groups in LOADED_FOR.values() for n in groups}
    LOADS["base"] = 16 * (2 + 4)
    LOADS["rest"] = 16 * (nb - 2)
    WHEN = {}
    for groups in LOADED_FOR.values():
        for n, after in groups.items():
            k = STAGES.index(after) + 1 if after else 0
            WHEN.setdefault(STAGES[k], []).append((n, k))

    def load_weights(sp, at):
        for n, k in WHEN.get(at, []):
            if k:
                sp.wait_ge(updated, k * nb)
            if n == "L0f":
                sp.wait_ge(zeroed, 1)
            for dst, src in weight_loads(n):
                sp.dma_start(dst, src).then_inc(loaded[n], 16)

    class Front:

        def __init__(self, x):
            self.bank_at = 4 * x + 3
            self.bank = B[self.bank_at]
            self.h = sbuf(f"h{x}", [P, NT, D])
            self.hT = sbuf(f"hT{x}", [P, KD, TOK])
            self.stats = sbuf(f"stats{x}", [P, NT, 6])
            self.moments = sbuf(f"moments{x}", [P, NT, 2])
            self.variance = sbuf(f"variance{x}", [P, NT])
            self.rstd = sbuf(f"rstd{x}", [P, NT])
            self.variance_l, self.rstd_l, self.h_l = link(f"variance{x}"), link(f"rstd{x}"), link(f"h{x}")

        def plan(self, s, n, uses="h", h_uses="h"):
            self.h_l.plan(s, h_uses, n)
            for l in (self.variance_l, self.rstd_l):
                l.plan(s, uses, n)

        def ln_stats(self, dve, s, i, step, src):
            for j in range(NT):
                dve.bn_stats(self.stats[:, j, :], src[:, j, :]).then_inc(dve_steps, step.one())
            dve.wait_ge(dve_steps, step.done)
            for j in range(NT):
                dve.bn_aggr(self.moments[:, j, :], self.stats[:, j, :]).then_inc(dve_steps, step.one())
            dve.wait_ge(dve_steps, step.done)
            dve.tensor_scalar(self.variance[:], self.moments[:, :, 1], EPS, None, ALU.add).then_inc(self.variance_l.ready, 1)

        def ln_apply(self, dve, s, i, src, use="T"):
            dve.wait_ge(self.rstd_l.ready, self.rstd_l.n(s, i) + 1)
            dve.wait_ge(self.bank.ready, self.bank.n(s, i, use))
            for j in range(NT):
                ins = dve.tensor_scalar(self.h[:, j, :], src[:, j, :], self.moments[:, j, 0:1], self.rstd[:, j:j + 1],
                                        ALU.subtract, ALU.mult)
            ins.then_inc(self.h_l.ready, 1)

        def ln_power(self, pool, s, i):
            pool.wait_ge(self.variance_l.ready, self.variance_l.n(s, i) + 1)
            pool.tensor_tensor(self.rstd[:], self.variance[:], minus_half[:, 0:NT], ALU.pow).then_inc(self.rstd_l.ready, 1)

        def transpose_h(self, pe, s, i):
            b = self.bank
            pe.wait_ge(b.free, b.n(s, i, "T"))
            pe.wait_ge(self.h_l.ready, self.h_l.n(s, i) + 1)
            for k in range(KD):
                for j in range(NT):
                    ins = pe.transpose(psum[:, self.bank_at, k * TOK + j * P:k * TOK + (j + 1) * P],
                                       self.h[:, j, k * P:(k + 1) * P], ident)
            ins.then_inc(b.ready, 1)

        def copy_hT(self, act, s, i):
            b = self.bank
            act.wait_ge(b.ready, b.n(s, i, "T") + 1)
            act.activation(self.hT[:].rearrange("p a b -> p (a b)"), bank(self.bank_at), ACT.Copy).then_inc(b.free, 1)

        def need_hT(self, pe, s, i):
            pe.wait_ge(self.bank.free, self.bank.n(s, i, "T") + 1)

    front = [Front(x) for x in range(2)]
    whole = front[1]
    hT = whole.hT
    ln_stats, ln_apply, ln_power = whole.ln_stats, whole.ln_apply, whole.ln_power
    transpose_h, copy_hT, need_hT = whole.transpose_h, whole.copy_hT, whole.need_hT
    XR = X[:].rearrange("p (r x) t d -> p r x t d", x=2)
    contexts = a["ctx"].rearrange("(r x) s d -> r x s d", x=2)

    def cross_stream(s, x, area, sm, steps, n, X_of, context_of, done, masks=None):
        biased, masked = s != "L2x", s == "L2x"
        wt = W[s]
        NG = H // GRP
        keep, fill = masks or (None, None)
        f = front[x]
        c0 = 4 * x
        t, Ob, ahead = (B[c0], B[c0 + 1]), B[c0 + 2], B[c0 + 3]
        Sb = t[0]
        context, contextT, KT = area.take(D, parts=S2), area.take(KD, S2), area.take(KD, S2)
        Kd, V, QT = area.take(H, S2), area.take(H, HD + 1, parts=S2), area.take(KD, TOK)
        at = area.at
        Pj = [area.take(H, S2) for _ in range(NT)]
        O, OT = view(at, (NT, D)), view(at + NT * D, (KD, TOK))
        PT = area.take(H, P, parts=S2)
        nmax, rden = sm.take(NT, H), sm.take(NT, H)
        f.plan(s, n)
        plan_uses(s, n, {c0: "Q S0 S1 t00 t02 t10 t12 OT", c0 + 1: "t01 t03 t11 t13 Y", c0 + 2: "O0 O1",
                               c0 + 3: "T c K V"},
                  **{f"context{x}": "c", f"Kd{x}": "K", f"P{x}": "S0 S1" if masked else "", f"E{x}": "S0 S1"})
        Pl, El, Kdl, context_l = (link(f"{n}{x}") for n in ("P", "E", "Kd", "context"))
        scores = psum[:, c0:c0 + 4, 0:GRP * S2].rearrange("p g (h k) -> p g h k", k=S2)

        def sync_first(sp):
            sp.dma_start(context, context_of(0)).then_inc(context_l.ready, 16)

        def sync_next(sp, i):
            sp.wait_ge(ahead.ready, ahead.n(s, i - 1, "c") + 1)
            sp.dma_start(context, context_of(i)).then_inc(context_l.ready, 16)

        def context_pe(pe, i):
            pe.wait_ge(context_l.ready, 16 * context_l.n(s, i) + 1)
            pe.wait_ge(ahead.free, ahead.n(s, i, "c"))
            for k in range(KD):
                ins = pe.transpose(psum[:, c0 + 3, k * S2:(k + 1) * S2], context[:, k * P:(k + 1) * P],
                                   ident[0:S2, 0:S2])
            ins.then_inc(ahead.ready, 1)

        def keys_pe(pe, i):
            pe.wait_ge(ahead.free, ahead.n(s, i, "K"))
            for m in range(KD):
                for k in range(KD):
                    ins = pe.matmul(psum[:, c0 + 3, m * S2:(m + 1) * S2], wt["wk"][:, k, m * P:(m + 1) * P],
                                    contextT[:, k, :], start=k == 0, stop=k == KD - 1)
            ins.then_inc(ahead.ready, 1)

        def values_pe(pe, i):
            pe.wait_ge(ahead.free, ahead.n(s, i, "V"))
            for k in range(KD):
                ins = pe.matmul(psum[0:S2, c0 + 3, 0:D], contextT[:, k, :], wt["wv"][:, k, :],
                                start=k == 0, stop=k == KD - 1)
            ins.then_inc(ahead.ready, 1)

        def scores_pe(pe, i, j):
            pe.wait_ge(Sb.free, Sb.n(s, i, f"S{j}"))
            for g in range(NG):
                k = g * GRP * HD // P
                ins = pe.matmul(psum[:, c0 + g, 0:GRP * S2], QT[:, k, j * P:(j + 1) * P],
                                Kd[:, g * GRP:(g + 1) * GRP, :].rearrange("p h k -> p (h k)"), start=True, stop=True)
            ins.then_inc(Sb.ready, 1)

        def turn_pe(pe, i, j):
            pe.wait_ge(El.ready, El.n(s, i, f"S{j}") + 1)
            for g in range(NG):
                b = t[g % 2]
                pe.wait_ge(b.free, b.n(s, i, f"t{j}{g}"))
                for q in range(GRP):
                    ins = pe.transpose(psum[0:S2, c0 + g % 2, q * P:(q + 1) * P], Pj[j][:, g * GRP + q, :], ident)
                ins.then_inc(b.ready, 1)

        def mix_pe(pe, i, j):
            pe.wait_ge(Ob.free, Ob.n(s, i, f"O{j}"))
            for g in (2, 3):
                pe.wait_ge(t[g % 2].free, t[g % 2].n(s, i, f"t{j}{g}") + 1)
            for hh in range(H):
                ins = pe.matmul(psum[:, c0 + 2, hh * (HD + 1):(hh + 1) * (HD + 1)], PT[:, hh, :],
                                V[:, hh, :], start=True, stop=True)
            ins.then_inc(Ob.ready, 1)

        def pe_first(pe):
            f.transpose_h(pe, s, 0)
            context_pe(pe, 0)
            yield
            keys_pe(pe, 0)
            yield
            values_pe(pe, 0)
            yield

        def pe_scores(pe, i):
            f.need_hT(pe, s, i)
            pe.wait_ge(Sb.free, Sb.n(s, i, "Q"))
            for m in range(KD):
                for k in range(KD):
                    ins = pe.matmul(psum[:, c0, m * TOK:(m + 1) * TOK], wt["wq"][:, k, m * P:(m + 1) * P],
                                    f.hT[:, k, :], start=k == 0, stop=k == KD - 1)
            ins.then_inc(Sb.ready, 1)
            yield
            pe.wait_ge(Kdl.ready, Kdl.n(s, i) + 1)
            pe.wait_ge(t[1].free, t[1].n(s, i))
            pe.wait_ge(Ob.free, Ob.n(s, i))
            pe.wait_ge(ahead.free, ahead.n(s, i, "V") + 1)
            scores_pe(pe, i, 0)
            yield
            scores_pe(pe, i, 1)
            yield

        def pe_values(pe, i, more):
            pe.wait_ge(Sb.free, Sb.n(s, i, "S1") + 1)
            turn_pe(pe, i, 0)
            yield
            mix_pe(pe, i, 0)
            turn_pe(pe, i, 1)
            if more:
                f.transpose_h(pe, s, i + 1)
                context_pe(pe, i + 1)
            yield
            mix_pe(pe, i, 1)
            if more:
                keys_pe(pe, i + 1)
            yield
            if more:
                values_pe(pe, i + 1)
            pe.wait_ge(Ob.free, Ob.n(s, i, "O1") + 1)
            pe.wait_ge(Sb.free, Sb.n(s, i, "OT"))
            for k in range(KD):
                for j in range(NT):
                    ins = pe.transpose(psum[:, c0, k * TOK + j * P:k * TOK + (j + 1) * P], O[:, j, k * P:(k + 1) * P], ident)
            ins.then_inc(Sb.ready, 1)
            yield
            pe.wait_ge(t[1].free, t[1].n(s, i, "Y"))
            pe.wait_ge(Sb.free, Sb.n(s, i, "OT") + 1)
            for j in range(NT):
                for k in range(KD):
                    ins = pe.matmul(psum[:, c0 + 1, j * D:(j + 1) * D], OT[:, k, j * P:(j + 1) * P], wt["wo"][:, k, :],
                                    start=k == 0, stop=k == KD - 1)
            ins.then_inc(t[1].ready, 1)
            yield

        def context_act(act, i):
            act.wait_ge(ahead.ready, ahead.n(s, i, "c") + 1)
            act.activation(contextT.rearrange("p a b -> p (a b)"), psum[:, c0 + 3, 0:KD * S2],
                           ACT.Copy).then_inc(ahead.free, 1)

        def keys_act(act, i):
            act.wait_ge(ahead.ready, ahead.n(s, i, "K") + 1)
            act.wait_ge(Kdl.ready, Kdl.n(s, i))
            for m in range(KD):
                src = psum[:, c0 + 3, m * S2:(m + 1) * S2]
                if biased:
                    ins = act.activation(KT[:, m, :], src, ACT.Identity, bias=col(s + "_bk", m))
                else:
                    ins = act.activation(KT[:, m, :], src, ACT.Copy)
            ins.then_inc(ahead.free, 1)

        def act_first(act):
            f.copy_hT(act, s, 0)
            context_act(act, 0)
            yield
            keys_act(act, 0)
            yield

        def act_scores(act, i):
            act.wait_ge(Sb.ready, Sb.n(s, i, "Q") + 1)
            for m in range(KD):
                src = psum[:, c0, m * TOK:(m + 1) * TOK]
                if biased:
                    ins = act.activation(QT[:, m, :], src, ACT.Identity, bias=col(s + "_bq", m))
                else:
                    ins = act.activation(QT[:, m, :], src, ACT.Copy)
            ins.then_inc(Sb.free, 1)
            yield
            for j in range(NT):
                if masked:
                    act.wait_ge(Pl.ready, Pl.n(s, i, f"S{j}") + 1)
                else:
                    act.wait_ge(Sb.free, Sb.n(s, i, f"S{j}") + 1)
                p = Pj[j].rearrange("p a b -> p (a b)")
                act.activation(p, p, ACT.Exp, scale=HD ** -0.5).then_inc(El.ready, 1)
                yield

        def act_values(act, i, more):
            for j in range(NT):
                for g in range(NG):
                    b = t[g % 2]
                    act.wait_ge(b.ready, b.n(s, i, f"t{j}{g}") + 1)
                    act.activation(PT[:, g * GRP:(g + 1) * GRP, :].rearrange("p a b -> p (a b)"),
                                   bank(c0 + g % 2, parts=S2), ACT.Copy).then_inc(b.free, 1)
                if more and j:
                    f.copy_hT(act, s, i + 1)
                    context_act(act, i + 1)
                yield
            if more:
                keys_act(act, i + 1)
            yield
            act.wait_ge(Sb.ready, Sb.n(s, i, "OT") + 1)
            act.activation(OT.rearrange("p a b -> p (a b)"), bank(c0), ACT.Copy).then_inc(Sb.free, 1)
            yield
            yield

        def spread(pool, i):
            pool.wait_ge(ahead.free, ahead.n(s, i, "K") + 1)
            for m in range(KD):
                n = P // HD
                ins = pool.tensor_tensor(Kd[:, m * n:(m + 1) * n, :], KT[:, m, :].unsqueeze(1).broadcast_to([P, n, S2]),
                                         const("headmask").unsqueeze(2).broadcast_to([P, n, S2]), ALU.mult)
            ins.then_inc(Kdl.ready, 1)

        def pool_first(pool):
            f.ln_power(pool, s, 0)
            yield
            spread(pool, 0)
            yield

        def pool_scores(pool, i):
            for _ in range(3):
                yield

        def pool_values(pool, i, more):
            if more:
                f.ln_power(pool, s, i + 1)
            yield
            yield
            yield
            if more:
                spread(pool, i + 1)
            yield
            yield

        def values_dve(dve, i):
            dve.wait_ge(ahead.ready, ahead.n(s, i, "V") + 1)
            src = psum[0:S2, c0 + 3, 0:D].rearrange("p (h d) -> p h d", d=HD)
            if biased:
                bv = rows[0:S2, slice(*ROW_AT[s + "_bv"])].rearrange("p (h d) -> p h d", d=HD)
                dve.tensor_tensor(V[:, :, 0:HD], src, bv, ALU.add).then_inc(ahead.free, 1)
            else:
                dve.tensor_copy(V[:, :, 0:HD], src).then_inc(ahead.free, 1)

        def dve_first(dve):
            step = steps[0]
            dve.memset(V[:, :, HD:HD + 1], 1.0)
            f.ln_stats(dve, s, 0, step, X_of(0))
            yield
            f.ln_apply(dve, s, 0, X_of(0))
            yield
            values_dve(dve, 0)
            yield

        def dve_scores(dve, i):
            step = steps[0]
            yield
            for j in range(NT):
                dve.wait_ge(Sb.ready, Sb.n(s, i, f"S{j}") + 1)
                p = Pj[j].rearrange("p (g h) k -> p g h k", h=GRP)
                src = scores
                if masked:
                    bc = [m[:, j, :].unsqueeze(1).unsqueeze(1).broadcast_to([P, NG, GRP, S2]) for m in (keep, fill)]
                    dve.tensor_tensor(p, scores, bc[0], ALU.mult).then_inc(Sb.free, 1)
                    dve.wait_ge(Sb.free, Sb.n(s, i, f"S{j}") + 1)
                    dve.tensor_tensor(p, p, bc[1], ALU.add).then_inc(dve_steps, step.one())
                    dve.wait_ge(dve_steps, step.done)
                    src = p
                dve.tensor_reduce(nmax[:, j, :], src, AXIS_X, ALU.max, negate=True).then_inc(dve_steps, step.one())
                dve.wait_ge(dve_steps, step.done)
                nm = nmax[:, j, :].rearrange("p (g h) -> p g h", h=GRP).unsqueeze(3).broadcast_to([P, NG, GRP, S2])
                dve.tensor_tensor(p, src, nm, ALU.add).then_inc(Pl.ready if masked else Sb.free, 1)
                yield

        def dve_values(dve, i, more):
            step = steps[0]
            if more:
                f.ln_stats(dve, s, i + 1, step, X_of(i + 1))
                f.ln_apply(dve, s, i + 1, X_of(i + 1))
            yield
            for j in range(NT):
                dve.wait_ge(Ob.ready, Ob.n(s, i, f"O{j}") + 1)
                o = psum[:, c0 + 2, 0:H * (HD + 1)].rearrange("p (h d) -> p h d", d=HD + 1)
                dve.reciprocal(rden[:, j, :], o[:, :, HD]).then_inc(dve_steps, step.one())
                dve.wait_ge(dve_steps, step.done)
                dve.tensor_tensor(O[:, j, :].rearrange("p (h d) -> p h d", d=HD), o[:, :, 0:HD],
                                  rden[:, j, :].unsqueeze(2).broadcast_to([P, H, HD]), ALU.mult).then_inc(Ob.free, 1)
                yield
            if more:
                values_dve(dve, i + 1)
            yield
            dve.wait_ge(t[1].ready, t[1].n(s, i, "Y") + 1)
            xt = X_of(i).rearrange("p t d -> p (t d)")
            dve.tensor_tensor(xt, bank(c0 + 1), xt, ALU.add).then_inc(t[1].free, 1)
            dve.wait_ge(t[1].free, t[1].n(s, i, "Y") + 1)
            if biased:
                dve.tensor_tensor(X_of(i), X_of(i), row(s + "_bo").unsqueeze(1).broadcast_to([P, NT, D]),
                                  ALU.add).then_inc(done, 1)
            else:
                dve.memset(pad[:, x:x + 1], 0.0).then_inc(done, 1)
            yield

        return dict(pe_first=pe_first, pe_scores=pe_scores, pe_values=pe_values,
                    act_first=act_first, act_scores=act_scores, act_values=act_values,
                    pool_first=pool_first, pool_scores=pool_scores, pool_values=pool_values,
                    dve_first=dve_first, dve_scores=dve_scores, dve_values=dve_values,
                    sync_first=sync_first, sync_next=sync_next)

    def cross(s):
        area = Area(WORK3)
        sm = Area(0, small)
        keep, fill = sm.take(NT, S2), sm.take(NT, S2)
        steps = [Steps()]
        pair = [cross_stream(s, x, area, sm, steps, nb // 2, lambda i, x=x: XR[:, i, x], lambda i, x=x: contexts[i, x],
                             updated, (keep, fill)) for x in range(2)]

        def first(name, eng):
            by_turns(*(p[name + "_first"](eng) for p in pair))
            for _ in pair[1][name + "_scores"](eng, 0):
                pass

        def both(name, eng, i, more):
            def leading():
                yield from pair[1][name + "_values"](eng, i, more)
                if more:
                    yield from pair[1][name + "_scores"](eng, i + 1)

            def following():
                yield from pair[0][name + "_scores"](eng, i)
                yield from pair[0][name + "_values"](eng, i, more)
            by_turns(leading(), following())

        def sp(sp):
            begin(sp, s)
            for p in pair:
                p["sync_first"](sp)
            load_weights(sp, s)
            if nb > 2:
                with sp.Fori(1, nb // 2) as i:
                    for p in pair:
                        p["sync_next"](sp, i)

        def pe(pe):
            begin(pe, s)
            pe.wait_ge(loaded["base"], LOADS["base"])
            pe.wait_ge(made, 1)
            pe.wait_ge(loaded[s], LOADS[s])
            first("pe", pe)
            for i, more in rounds(pe):
                both("pe", pe, i, more)

        def act(act):
            begin(act, s)
            act.wait_ge(loaded["base"], LOADS["base"])
            first("act", act)
            for i, more in rounds(act):
                both("act", act, i, more)

        def pool(pool):
            begin(pool, s)
            pool.wait_ge(loaded["base"], LOADS["base"])
            pool.wait_ge(made, 1)
            first("pool", pool)
            for i, more in rounds(pool):
                both("pool", pool, i, more)

        def dve(dve):
            begin(dve, s)
            steps[0] = step = Steps()
            dve.tensor_copy(keep, mask_bytes[:]).then_inc(dve_steps, step.one())
            dve.wait_ge(dve_steps, step.done)
            dve.tensor_scalar(fill, keep, 1.0, 1e9 * HD ** 0.5, ALU.subtract, ALU.mult).then_inc(dve_steps, step.one())
            first("dve", dve)
            dve.wait_ge(dve_steps, step.done)
            dve.sem_clear(dve_steps)
            for i, more in rounds(dve):
                steps[0] = step = Steps()
                both("dve", dve, i, more)
                dve.wait_ge(dve_steps, step.done)
                dve.sem_clear(dve_steps)
        return dict(sync=sp, tensor=pe, scalar=act, gpsimd=pool, vector=dve)

    def single(s):
        wt = W[s]
        area = Area(WORK1)
        sm = Area(0, small)
        steps = [Steps()]

        def stream(x):
            f = front[x]
            c0 = 4 * x
            b = B[c0:c0 + 4]
            context, contextT, KT = area.take(D, parts=S2), area.take(KD, S2), area.take(KD, S2)
            V, QT = area.take(D, parts=S2), area.take(KD, TOK)
            E, ET = area.take(NT, S2), area.take(NT, P, parts=S2)
            mx, nmax, den, rden = (sm.take(NT) for _ in range(4))
            f.plan(s, nb // 2)
            plan_uses(s, nb // 2, {c0: "Q t", c0 + 1: "c K V", c0 + 2: "S O", c0 + 3: "T"},
                      **{f"context{x}": "c", f"nmax{x}": "S", f"E{x}": "S"})
            context_l, nl, El = link(f"context{x}"), link(f"nmax{x}"), link(f"E{x}")

            def free(eng, k, i, use):
                eng.wait_ge(b[k].free, b[k].n(s, i, use))

            def ready(eng, k, i, use):
                eng.wait_ge(b[k].ready, b[k].n(s, i, use) + 1)

            def taken(eng, k, i, use):
                eng.wait_ge(b[k].free, b[k].n(s, i, use) + 1)

            def sync_first(sp):
                sp.dma_start(context, contexts[0, x]).then_inc(context_l.ready, 16)

            def sync_next(sp, i):
                sp.wait_ge(b[1].ready, b[1].n(s, i - 1, "c") + 1)
                sp.dma_start(context, contexts[i, x]).then_inc(context_l.ready, 16)

            def pe_head(pe, i):
                pe.wait_ge(context_l.ready, 16 * context_l.n(s, i) + 1)
                free(pe, 1, i, "c")
                for k in range(KD):
                    ins = pe.transpose(psum[:, c0 + 1, k * S2:(k + 1) * S2], context[:, k * P:(k + 1) * P], ident[0:S2, 0:S2])
                ins.then_inc(b[1].ready, 1)
                yield
                f.transpose_h(pe, s, i)
                free(pe, 1, i, "K")
                for m in range(KD):
                    for k in range(KD):
                        ins = pe.matmul(psum[:, c0 + 1, m * S2:(m + 1) * S2], wt["wk"][:, k, m * P:(m + 1) * P],
                                        contextT[:, k, :], start=k == 0, stop=k == KD - 1)
                ins.then_inc(b[1].ready, 1)
                yield
                f.need_hT(pe, s, i)
                free(pe, 0, i, "Q")
                for m in range(KD):
                    for k in range(KD):
                        ins = pe.matmul(psum[:, c0, m * TOK:(m + 1) * TOK], wt["wq"][:, k, m * P:(m + 1) * P],
                                        f.hT[:, k, :], start=k == 0, stop=k == KD - 1)
                ins.then_inc(b[0].ready, 1)
                free(pe, 1, i, "V")
                for k in range(KD):
                    ins = pe.matmul(psum[0:S2, c0 + 1, 0:D], contextT[:, k, :], wt["wv"][:, k, :], start=k == 0, stop=k == KD - 1)
                ins.then_inc(b[1].ready, 1)
                yield

            def pe_tail(pe, i):
                taken(pe, 0, i, "Q")
                free(pe, 2, i, "S")
                for j in range(NT):
                    for k in range(KD):
                        ins = pe.matmul(psum[:, c0 + 2, j * S2:(j + 1) * S2], QT[:, k, j * P:(j + 1) * P], KT[:, k, :],
                                        start=k == 0, stop=k == KD - 1)
                ins.then_inc(b[2].ready, 1)
                yield
                pe.wait_ge(El.ready, El.n(s, i) + 1)
                free(pe, 0, i, "t")
                for j in range(NT):
                    ins = pe.transpose(psum[0:S2, c0, j * P:(j + 1) * P], E[:, j, :], ident)
                ins.then_inc(b[0].ready, 1)
                yield
                taken(pe, 0, i, "t")
                taken(pe, 1, i, "V")
                free(pe, 2, i, "O")
                for j in range(NT):
                    ins = pe.matmul(psum[:, c0 + 2, j * D:(j + 1) * D], ET[:, j, :], V, start=True, stop=True)
                ins.then_inc(b[2].ready, 1)
                yield

            def act_head(act, i):
                ready(act, 1, i, "c")
                act.activation(contextT.rearrange("p a b -> p (a b)"), psum[:, c0 + 1, 0:KD * S2], ACT.Copy).then_inc(b[1].free, 1)
                yield
                f.copy_hT(act, s, i)
                ready(act, 1, i, "K")
                for m in range(KD):
                    ins = act.activation(KT[:, m, :], psum[:, c0 + 1, m * S2:(m + 1) * S2], ACT.Identity, bias=col(s + "_bk", m))
                ins.then_inc(b[1].free, 1)
                yield
                ready(act, 0, i, "Q")
                for m in range(KD):
                    ins = act.activation(QT[:, m, :], psum[:, c0, m * TOK:(m + 1) * TOK], ACT.Identity, bias=col(s + "_bq", m))
                ins.then_inc(b[0].free, 1)
                yield

            def act_tail(act, i):
                act.wait_ge(nl.ready, nl.n(s, i) + 1)
                for j in range(NT):
                    ins = act.activation(E[:, j, :], psum[:, c0 + 2, j * S2:(j + 1) * S2], ACT.Exp, scale=D ** -0.5,
                                         bias=nmax[:, j:j + 1], accum_out=den[:, j:j + 1])
                ins.then_inc(El.ready, 1)
                yield
                ready(act, 0, i, "t")
                act.activation(ET.rearrange("p a b -> p (a b)"), psum[0:S2, c0, 0:NT * P], ACT.Copy).then_inc(b[0].free, 1)
                yield
                yield

            def pool_head(pool, i):
                f.ln_power(pool, s, i)
                yield
                yield
                yield

            def pool_tail(pool, i):
                yield
                yield
                yield

            def dve_head(dve, i):
                f.ln_stats(dve, s, i, steps[0], XR[:, i, x])
                f.ln_apply(dve, s, i, XR[:, i, x])
                yield
                yield
                ready(dve, 1, i, "V")
                dve.tensor_tensor(V, psum[0:S2, c0 + 1, 0:D], rows[0:S2, slice(*ROW_AT[s + "_bv"])], ALU.add).then_inc(b[1].free, 1)
                yield

            def dve_tail(dve, i):
                step = steps[0]
                ready(dve, 2, i, "S")
                dve.tensor_reduce(mx, psum[:, c0 + 2, 0:NT * S2].rearrange("p (a b) -> p a b", a=NT), AXIS_X, ALU.max).then_inc(dve_steps, step.one())
                dve.wait_ge(dve_steps, step.done)
                dve.tensor_scalar(nmax, mx, -D ** -0.5, None, ALU.mult).then_inc(nl.ready, 1)
                yield
                dve.wait_ge(El.ready, El.n(s, i) + 1)
                dve.reciprocal(rden, den).then_inc(b[2].free, 1)
                yield
                taken(dve, 2, i, "S")
                ready(dve, 2, i, "O")
                for j in range(NT):
                    ins = dve.scalar_tensor_tensor(XR[:, i, x, j, :], psum[:, c0 + 2, j * D:(j + 1) * D], rden[:, j:j + 1],
                                                   XR[:, i, x, j, :], ALU.mult, ALU.add)
                ins.then_inc(b[2].free, 1)
                taken(dve, 2, i, "O")
                dve.memset(pad[:, x:x + 1], 0.0).then_inc(updated, 1)
                yield
            return dict(sync_first=sync_first, sync_next=sync_next, pe_head=pe_head, pe_tail=pe_tail,
                        act_head=act_head, act_tail=act_tail, pool_head=pool_head, pool_tail=pool_tail,
                        dve_head=dve_head, dve_tail=dve_tail)

        pair = [stream(x) for x in range(2)]

        def sp(sp):
            begin(sp, s)
            for p in pair:
                p["sync_first"](sp)
            load_weights(sp, s)
            if nb > 2:
                with sp.Fori(1, nb // 2) as i:
                    for p in pair:
                        p["sync_next"](sp, i)

        def pe(pe):
            begin(pe, s)
            pe.wait_ge(loaded["base"], LOADS["base"])
            pe.wait_ge(made, 1)
            pe.wait_ge(loaded[s], LOADS[s])
            halves_first(pair, "pe", pe)
            for i, more in rounds(pe):
                halves(pair, "pe", pe, i, more)

        def act(act):
            begin(act, s)
            halves_first(pair, "act", act)
            for i, more in rounds(act):
                halves(pair, "act", act, i, more)

        def pool(pool):
            begin(pool, s)
            halves_first(pair, "pool", pool)
            for i, more in rounds(pool):
                halves(pair, "pool", pool, i, more)

        def dve(dve):
            steps[0] = step = Steps()
            begin(dve, s)
            halves_first(pair, "dve", dve)
            dve.wait_ge(dve_steps, step.done)
            dve.sem_clear(dve_steps)
            for i, more in rounds(dve):
                steps[0] = step = Steps()
                halves(pair, "dve", dve, i, more)
                dve.wait_ge(dve_steps, step.done)
                dve.sem_clear(dve_steps)
        return dict(sync=sp, tensor=pe, scalar=act, gpsimd=pool, vector=dve)

    def ternary(s):
        wt = W[s]
        area = Area(WORK3)
        sm = Area(0, small)
        NF = FF2 // P
        steps = [Steps()]
        part, total, half, nhalf = sm.take(2, 16), sm.take(2), sm.take(2), sm.take(2)
        scratch = view(area.at, (KD * FF2,))
        ones = view(area.at + KD * FF2, (P,))
        sums, summed, ternaries = sem("weight_sums"), sem("weight_totals"), sem("ternary_weights")
        flat = [wt["fc"].rearrange("p a b -> p (a b)"), wt["proj"].rearrange("p a b -> p (a b)")]

        def stream(x):
            f = front[x]
            c0 = 4 * x
            b = B[c0:c0 + 4]
            G, CT = area.take(NT, FF2), area.take(NF, TOK)
            st, mo, var, rs = sm.take(NT, 2, 6), sm.take(NT, 2), sm.take(NT), sm.take(NT)
            f.plan(s, nb // 2)
            plan_uses(s, nb // 2, {c0: "f0 c0 Y", c0 + 1: "c1", c0 + 2: "f1 c2", c0 + 3: "T c3"},
                      **{f"inner_variance{x}": "f", f"inner_rstd{x}": "f", f"G{x}": "f"})
            vl, rl, Gl = (link(f"{n}{x}") for n in ("inner_variance", "inner_rstd", "G"))

            def pe_head(pe, i):
                yield
                f.transpose_h(pe, s, i)
                yield
                f.need_hT(pe, s, i)
                for j in range(NT):
                    pe.wait_ge(b[2 * j].free, b[2 * j].n(s, i, f"f{j}"))
                    if j == 0:
                        pe.wait_ge(b[1].free, b[1].n(s, i))
                    for m in range(FF2 // 512):
                        for k in range(KD):
                            ins = pe.matmul(bank(c0 + 2 * j + m), f.hT[:, k, j * P:(j + 1) * P], wt["fc"][:, k, m * 512:(m + 1) * 512],
                                            start=k == 0, stop=k == KD - 1)
                    ins.then_inc(b[2 * j].ready, 1)
                yield

            def pe_tail(pe, i):
                yield
                pe.wait_ge(Gl.ready, Gl.n(s, i) + 1)
                for q in range(NF // 2):
                    pe.wait_ge(b[q].free, b[q].n(s, i, f"c{q}"))
                    if q % 2:
                        pe.wait_ge(b[q - 1].free, b[q - 1].n(s, i, f"f{q // 2}") + 1)
                    for m in range(2):
                        for j in range(NT):
                            ins = pe.transpose(psum[:, c0 + q, m * TOK + j * P:m * TOK + (j + 1) * P],
                                               G[:, j, (2 * q + m) * P:(2 * q + m + 1) * P], ident)
                    ins.then_inc(b[q].ready, 1)
                yield
                pe.wait_ge(b[0].free, b[0].n(s, i, "Y"))
                for q in range(1, NF // 2):
                    pe.wait_ge(b[q].free, b[q].n(s, i, f"c{q}") + 1)
                for j in range(NT):
                    for m in range(NF):
                        ins = pe.matmul(psum[:, c0, j * D:(j + 1) * D], CT[:, m, j * P:(j + 1) * P], wt["proj"][:, m, :],
                                        start=m == 0, stop=m == NF - 1)
                ins.then_inc(b[0].ready, 1)
                yield

            def act_head(act, i):
                yield
                f.copy_hT(act, s, i)
                yield
                for j in range(NT):
                    act.wait_ge(b[2 * j].ready, b[2 * j].n(s, i, f"f{j}") + 1)
                    act.activation(G[:, j, :].rearrange("p (a b) -> p a b", a=2), psum[:, c0 + 2 * j:c0 + 2 * j + 2, :],
                                   ACT.Gelu).then_inc(b[2 * j].free, 1)
                yield

            def act_tail(act, i):
                yield
                for q in range(NF // 2):
                    act.wait_ge(b[q].ready, b[q].n(s, i, f"c{q}") + 1)
                    for m in range(2):
                        c = 2 * q + m
                        ins = act.activation(CT[:, c, :], psum[:, c0 + q, m * TOK:(m + 1) * TOK], ACT.Identity,
                                             scale=col("L2f_w", c), bias=col("L2f_b", c))
                    ins.then_inc(b[q].free, 1)
                yield
                yield

            def pool_head(pool, i):
                f.ln_power(pool, s, i)
                yield
                yield
                yield

            def pool_tail(pool, i):
                pool.wait_ge(vl.ready, vl.n(s, i) + 1)
                pool.tensor_tensor(rs, var, minus_half[:, 0:NT], ALU.pow).then_inc(rl.ready, 1)
                yield
                yield
                yield

            def dve_head(dve, i):
                f.ln_stats(dve, s, i, steps[0], XR[:, i, x])
                f.ln_apply(dve, s, i, XR[:, i, x])
                yield
                yield
                yield

            def dve_tail(dve, i):
                step = steps[0]
                for j in range(NT):
                    dve.wait_ge(b[2 * j].free, b[2 * j].n(s, i, f"f{j}") + 1)
                    dve.memset(pad[:, 4 * x + j:4 * x + j + 1], 0.0)
                    for m in range(2):
                        dve.bn_stats(st[:, j, m, :], G[:, j, m * 512:(m + 1) * 512]).then_inc(dve_steps, step.one())
                dve.wait_ge(dve_steps, step.done)
                for j in range(NT):
                    dve.bn_aggr(mo[:, j, :], st[:, j].rearrange("p a b -> p (a b)")).then_inc(dve_steps, step.one())
                dve.wait_ge(dve_steps, step.done)
                dve.tensor_scalar(var, mo[:, :, 1], EPS, None, ALU.add).then_inc(vl.ready, 1)
                dve.wait_ge(rl.ready, rl.n(s, i) + 1)
                for j in range(NT):
                    ins = dve.tensor_scalar(G[:, j, :], G[:, j, :], mo[:, j, 0:1], rs[:, j:j + 1], ALU.subtract, ALU.mult)
                ins.then_inc(Gl.ready, 1)
                yield
                yield
                dve.wait_ge(b[0].ready, b[0].n(s, i, "Y") + 1)
                xt = XR[:, i, x].rearrange("p a b -> p (a b)")
                dve.tensor_tensor(xt, bank(c0), xt, ALU.add).then_inc(b[0].free, 1)
                dve.wait_ge(b[0].free, b[0].n(s, i, "Y") + 1)
                dve.memset(pad[:, 4 * x + 2:4 * x + 3], 0.0).then_inc(updated, 1)
                yield
            return dict(pe_head=pe_head, pe_tail=pe_tail, act_head=act_head, act_tail=act_tail,
                        pool_head=pool_head, pool_tail=pool_tail, dve_head=dve_head, dve_tail=dve_tail)

        pair = [stream(x) for x in range(2)]

        def pe(pe):
            begin(pe, s)
            pe.wait_ge(loaded["base"], LOADS["base"])
            pe.wait_ge(sums, 1)
            pe.matmul(psum[:, 0, 0:2], ones, total, start=True, stop=True).then_inc(summed, 1)
            pe.wait_ge(ternaries, 2)
            halves_first(pair, "pe", pe)
            for i, more in rounds(pe):
                halves(pair, "pe", pe, i, more)

        def act(act):
            begin(act, s)
            act.wait_ge(ternaries, 2)
            halves_first(pair, "act", act)
            for i, more in rounds(act):
                halves(pair, "act", act, i, more)

        def pool(pool):
            begin(pool, s)
            halves_first(pair, "pool", pool)
            for i, more in rounds(pool):
                halves(pair, "pool", pool, i, more)

        def dve(dve):
            steps[0] = step = Steps()
            begin(dve, s)
            dve.wait_ge(loaded[s], LOADS[s])
            dve.memset(ones, 1.0).then_inc(dve_steps, step.one())
            for m in range(2):
                dve.tensor_reduce(part[:, m, :], flat[m].rearrange("p (a b) -> p a b", a=16), AXIS_X, ALU.add,
                                  apply_absolute_value=True).then_inc(dve_steps, step.one())
            dve.wait_ge(dve_steps, step.done)
            dve.tensor_reduce(total, part, AXIS_X, ALU.add).then_inc(sums, 1)
            dve.wait_ge(summed, 1)
            dve.tensor_scalar(total, psum[:, 0, 0:2], 1.0 / (D * FF2), 1e-6, ALU.mult, ALU.add).then_inc(dve_steps, step.one())
            dve.wait_ge(dve_steps, step.done)
            dve.tensor_scalar(half, total, 0.5, None, ALU.mult).then_inc(dve_steps, step.one())
            dve.tensor_scalar(nhalf, total, -0.5, None, ALU.mult).then_inc(dve_steps, step.one())
            dve.wait_ge(dve_steps, step.done)
            for m in range(2):
                if m:
                    dve.wait_ge(ternaries, 1)
                dve.tensor_scalar(scratch, flat[m], nhalf[:, m:m + 1], None, ALU.is_lt).then_inc(dve_steps, step.one())
                dve.wait_ge(dve_steps, step.done)
                dve.scalar_tensor_tensor(flat[m], flat[m], half[:, m:m + 1], scratch, ALU.is_gt, ALU.subtract).then_inc(ternaries, 1)
            halves_first(pair, "dve", dve)
            dve.wait_ge(dve_steps, step.done)
            dve.sem_clear(dve_steps)
            for i, more in rounds(dve):
                steps[0] = step = Steps()
                halves(pair, "dve", dve, i, more)
                dve.wait_ge(dve_steps, step.done)
                dve.sem_clear(dve_steps)
        return dict(tensor=pe, scalar=act, gpsimd=pool, vector=dve)

    def beside(s, sx, sf, cross, ffn, attended, steps, store=False):

        def alone(name, eng):
            for part in (cross[name + "_first"](eng), cross[name + "_scores"](eng, 0), cross[name + "_values"](eng, 0, True)):
                for _ in part:
                    pass

        def loops(eng):
            if nb > 2:
                with eng.Fori(0, nb - 2) as i:
                    yield i, True, True
            yield nb - 2, True, False
            yield nb - 1, False, False

        def both(name, eng, i, more, further):
            def attention():
                if more:
                    yield from cross[name + "_scores"](eng, i + 1)
                    yield from cross[name + "_values"](eng, i + 1, further)
            by_turns(attention(), ffn[name](eng, i, more))

        def sp(sp):
            begin(sp, s)
            y = out.rearrange("(b t p) d -> b p t d", p=P, t=NT)
            cross["sync_first"](sp)
            load_weights(sp, s)
            cross["sync_next"](sp, 1)
            for i, _, further in loops(sp):
                if further:
                    cross["sync_next"](sp, i + 2)
                if store:
                    sp.wait_ge(updated, number[s] * nb + i + 1)
                    sp.dma_start(y[i], X[:, i]).then_inc(stored, 16)

        def pe(pe):
            begin(pe, s)
            pe.wait_ge(loaded["base"], LOADS["base"])
            pe.wait_ge(made, 1)
            pe.wait_ge(loaded[sx], LOADS[sx])
            alone("pe", pe)
            pe.wait_ge(loaded[sf], LOADS[sf])
            transpose_h(pe, sf, 0)
            for args in loops(pe):
                both("pe", pe, *args)

        def act(act):
            begin(act, s)
            act.wait_ge(loaded["base"], LOADS["base"])
            alone("act", act)
            copy_hT(act, sf, 0)
            for args in loops(act):
                both("act", act, *args)

        def pool(pool):
            begin(pool, s)
            pool.wait_ge(loaded["base"], LOADS["base"])
            pool.wait_ge(made, 1)
            alone("pool", pool)
            ln_power(pool, sf, 0)
            for args in loops(pool):
                both("pool", pool, *args)

        def dve(dve):
            begin(dve, s)
            steps[0] = step = Steps()
            alone("dve", dve)
            dve.wait_ge(attended, 1)
            dve.wait_ge(loaded["rest"], LOADS["rest"])
            ln_stats(dve, sf, 0, step, X[:, 0])
            ln_apply(dve, sf, 0, X[:, 0])
            dve.wait_ge(dve_steps, step.done)
            dve.sem_clear(dve_steps)
            for args in loops(dve):
                steps[0] = step = Steps()
                both("dve", dve, *args)
                dve.wait_ge(dve_steps, step.done)
                dve.sem_clear(dve_steps)
        return dict(sync=sp, tensor=pe, scalar=act, gpsimd=pool, vector=dve)

    def experts(s):
        sx, sf = "L3x", "L3f"
        NC = FF3 // P
        area = Area(WORK_L3)
        sm = Area(0, small)
        steps = [Steps()]
        attended = sem("attended_L3")
        cross = cross_stream(sx, 0, area, sm, steps, nb, lambda i: X[:, i], lambda i: a["ctx"][i], attended)
        dead = Area(0, rows)
        hid = [area.take(NC, TOK), dead.take(NC, TOK)]
        sg = [dead.take(TOK) for _ in range(3)]
        assert dead.at <= ROW_AT["L3x_bv"][0]
        BANKS = (4, 5, 7)

        def bank_of(m):
            return BANKS[m % 3]

        logits, top, index, turn = sm.take(NT, NE), sm.take(NT, 8), sm.take(NT, 8), sm.take(NT)
        index_f, weight, share, combine = sm.take(NT, 2), sm.take(NT, 2), sm.take(NT, 2, NE), sm.take(NT, NE)
        index = index.bitcast(mybir.dt.uint32)
        whole.plan(sf, nb)
        chunks_of = [" ".join(f"m{m}" for m in range(r, (NE + 1) * NC, 3)) for r in range(3)]
        plan_uses(sf, nb, {4: chunks_of[0], 5: chunks_of[1], 6: " ".join(f"e{e}" for e in range(NE + 1)),
                           7: "T logits " + chunks_of[2]},
                  gates=" ".join(f"m{m}" for m in range((NE + 1) * NC)), turn="t", tanh="t")
        gates_l, turn_l, tanh_l = link("gates"), link("turn"), link("tanh")

        def pe_ffn(pe, i, more):
            need_hT(pe, sf, i)
            pe.wait_ge(B[7].free, B[7].n(sf, i, "logits"))
            for j in range(NT):
                for k in range(KD):
                    ins = pe.matmul(psum[:, 7, j * NE:(j + 1) * NE], hT[:, k, j * P:(j + 1) * P], router[:, k, :],
                                    start=k == 0, stop=k == KD - 1)
            ins.then_inc(B[7].ready, 1)

            def down(e):
                pe.wait_ge(B[6].free, B[6].n(sf, i, f"e{e}"))
                for m in range(e * NC + 1, e * NC + NC):
                    pe.wait_ge(B[bank_of(m)].free, B[bank_of(m)].n(sf, i, f"m{m}") + 1)
                for j in range(NT):
                    for c in range(NC):
                        ins = pe.matmul(psum[:, 6, j * D:(j + 1) * D], hid[e % 2][:, c, j * P:(j + 1) * P], W[sf][e]["d"][:, c, :],
                                        start=c == 0, stop=c == NC - 1)
                ins.then_inc(B[6].ready, 1)

            for e in range(NE + 1):
                if e >= EARLY:
                    pe.wait_ge(loaded[f"L3f_expert{e}"], LOADS[f"L3f_expert{e}"])
                for c in range(NC):
                    m = e * NC + c
                    b = bank_of(m)
                    pe.wait_ge(B[b].free, B[b].n(sf, i, f"m{m}"))
                    for q, n in enumerate("gu"):
                        for k in range(KD):
                            ins = pe.matmul(psum[:, b, q * TOK:(q + 1) * TOK], W[sf][e][n][:, k, c * P:(c + 1) * P], hT[:, k, :],
                                            start=k == 0, stop=k == KD - 1)
                    ins.then_inc(B[b].ready, 1)
                if e:
                    down(e - 1)
                if e < NE:
                    yield
            if more:
                transpose_h(pe, sf, i + 1)
            down(NE)
            yield

        def act_ffn(act, i, more):
            for m in range((NE + 1) * NC):
                b = bank_of(m)
                act.wait_ge(B[b].ready, B[b].n(sf, i, f"m{m}") + 1)
                act.activation(sg[m % 3], psum[:, b, 0:TOK], ACT.Silu).then_inc(gates_l.ready, 1)
                if m == 2 * NC - 1:
                    act.wait_ge(turn_l.ready, turn_l.n(sf, i) + 1)
                    act.activation(turn, turn, ACT.Tanh, scale=0.5).then_inc(tanh_l.ready, 1)
                if m % NC == NC - 1 and m < NE * NC:
                    yield
            if more:
                copy_hT(act, sf, i + 1)
            yield

        def pool_ffn(pool, i, more):
            for e in range(NE):
                yield
            if more:
                ln_power(pool, sf, i + 1)
            yield

        def take_logits(dve, i):
            dve.wait_ge(B[7].ready, B[7].n(sf, i, "logits") + 1)
            dve.tensor_copy(logits.rearrange("p a b -> p (a b)"), psum[:, 7, 0:NT * NE]).then_inc(B[7].free, 1)

        def route(dve, i, step):
            dve.wait_ge(B[7].free, B[7].n(sf, i, "logits") + 1)
            dve.memset(pad[:, 6:7], 0.0)
            for j in range(NT):
                dve.max(top[:, j, :], logits[:, j, :]).then_inc(dve_steps, step.one())
            dve.wait_ge(dve_steps, step.done)
            dve.tensor_tensor(turn, top[:, :, 0], top[:, :, 1], ALU.subtract).then_inc(turn_l.ready, 1)
            for j in range(NT):
                dve.max_index(index[:, j, :], top[:, j, :], logits[:, j, :]).then_inc(dve_steps, step.one())
            dve.wait_ge(dve_steps, step.done)
            dve.tensor_copy(index_f, index[:, :, 0:2]).then_inc(dve_steps, step.one())

        def weigh(dve, i, step):
            dve.wait_ge(tanh_l.ready, tanh_l.n(sf, i) + 1)
            dve.tensor_scalar(weight[:, :, 0], turn, 0.5, 0.5, ALU.mult, ALU.add).then_inc(dve_steps, step.one())
            dve.tensor_scalar(weight[:, :, 1], turn, -0.5, 0.5, ALU.mult, ALU.add).then_inc(dve_steps, step.one())
            dve.wait_ge(dve_steps, step.done)
            for j in range(NT):
                for q in range(2):
                    dve.tensor_scalar(share[:, j, q, :], const("iota"), index_f[:, j, q:q + 1], weight[:, j, q:q + 1],
                                      ALU.is_equal, ALU.mult).then_inc(dve_steps, step.one())
            dve.wait_ge(dve_steps, step.done)
            dve.tensor_tensor(combine, share[:, :, 0, :], share[:, :, 1, :], ALU.add).then_inc(dve_steps, step.one())
            dve.wait_ge(dve_steps, step.done)

        def add_expert(dve, i, e):
            if e:
                dve.wait_ge(B[6].free, B[6].n(sf, i, f"e{e - 1}") + 1)
            dve.wait_ge(B[6].ready, B[6].n(sf, i, f"e{e}") + 1)
            for j in range(NT):
                y = psum[:, 6, j * D:(j + 1) * D]
                if e == 0:
                    ins = dve.tensor_tensor(X[:, i, j, :], y, X[:, i, j, :], ALU.add)
                else:
                    ins = dve.scalar_tensor_tensor(X[:, i, j, :], y, combine[:, j, e - 1:e], X[:, i, j, :], ALU.mult, ALU.add)
            ins.then_inc(B[6].free, 1)

        def dve_ffn(dve, i, more):
            step = steps[0]
            take_logits(dve, i)
            for e in range(NE + 1):
                if e == NE and more:
                    dve.wait_ge(attended, i + 2)
                    dve.memset(pad[:, 5:6], 0.0)
                    ln_stats(dve, sf, i + 1, step, X[:, i + 1])
                for c in range(NC):
                    if e == NE and more and c == 1:
                        ln_apply(dve, sf, i + 1, X[:, i + 1])
                    m = e * NC + c
                    b = bank_of(m)
                    dve.wait_ge(gates_l.ready, gates_l.n(sf, i, f"m{m}") + 1)
                    dve.tensor_tensor(hid[e % 2][:, c, :], psum[:, b, TOK:2 * TOK], sg[m % 3], ALU.mult).then_inc(B[b].free, 1)
                if e == 0:
                    route(dve, i, step)
                if e == 2:
                    weigh(dve, i, step)
                if e:
                    add_expert(dve, i, e - 1)
                if e < NE:
                    yield
            add_expert(dve, i, NE)
            dve.wait_ge(B[6].free, B[6].n(sf, i, f"e{NE}") + 1)
            dve.memset(pad[:, 7:8], 0.0).then_inc(updated, 1)
            yield

        ffn = dict(pe=pe_ffn, act=act_ffn, pool=pool_ffn, dve=dve_ffn)
        return beside(s, sx, sf, cross, ffn, attended, steps, store=True)

    def memory(s):
        sx, sf = "L0x", "L0f"
        wt = W[sf]
        NC = FF0 // P
        area = Area(WORK1)
        sm = Area(0, small)
        steps = [Steps()]
        attended = sem("attended_L0")
        cross = cross_stream(sx, 0, area, sm, steps, nb, lambda i: X[:, i], lambda i: a["ctx"][i], attended)
        qT, sims = area.take(4, TOK), area.take(NT, 2, PH, NKEYS)
        below = Area(AT_L1A)
        S = [below.take(PROWS, NKEYS) for _ in range(PH)]
        at = below.at
        E = [below.take(NEXP) for _ in range(2)]
        CT = view(at, (NEXP // P, TOK))
        assert below.at <= AT_L1A + L1F_W
        G = [area.take(NEXP) for _ in range(NT)]
        C = [area.take(NEXP) for _ in range(NT)]
        hid = area.take(NC, TOK)
        sg = [area.take(TOK) for _ in range(2)]
        tx, ty, top = sm.take(PH, TOPK), sm.take(PH, TOPK), sm.take(PH, TOPK)
        grid = sm.take(PH, TOPK, TOPK)
        thr, ntop = sm.take(NT, PH), sm.take(NT, PH)
        shifted, e8 = sm.take(NT, PH, TOPK), sm.take(NT, PH, TOPK)
        z, rz, left = sm.take(NT, PH), sm.take(NT, PH), sm.take(NT, 2)
        heads = " ".join(f"{j}{h}" for j in range(NT) for h in range(PH))
        BANK = {0: 7, 1: 4, 2: 5, 3: 5, 4: 7, 5: 4, 6: 5, 7: 7}
        KEY_BANK = (7, 4)
        DOWN_BANKS = ((4, 5), (7, 4))
        TURN_BANKS = ((5, 7), (4, 5))
        whole.plan(sf, nb)
        plan_uses(sf, nb, {4: "q m1 s1 m5 w0 w1 c1", 5: "q m2 m3 m6 w0 c0 c1", 6: "Y", 7: "T m0 s0 m4 m7 w1 c0"},
                  gates=" ".join(f"m{m}" for m in range(NC)), shifted="t0 t1", e8="t0 t1", S=heads, exps=heads,
                  picked=heads, G=heads, C="t0 t1")
        gates_l, shifted_l, e8_l, S_l, E_l, picked_l, G_l, C_l = (link(n) for n in (
            "gates", "shifted", "e8", "S", "exps", "picked", "G", "C"))

        def pe_ffn(pe, i, more):
            def free(b, use):
                pe.wait_ge(B[b].free, B[b].n(sf, i, use))

            def taken(b, use):
                pe.wait_ge(B[b].free, B[b].n(sf, i, use) + 1)

            def gate_up(m):
                b = BANK[m]
                free(b, f"m{m}")
                for q, n in enumerate(("wg", "wu")):
                    for k in range(KD):
                        ins = pe.matmul(psum[:, b, q * TOK:(q + 1) * TOK], wt[n][:, k, m * P:(m + 1) * P], hT[:, k, :],
                                        start=k == 0, stop=k == KD - 1)
                ins.then_inc(B[b].ready, 1)

            def with_keys(j):
                b = KEY_BANK[j]
                for q in (4, 5):
                    taken(q, "q")
                free(b, f"s{j}")
                for c in range(4):
                    ins = pe.matmul(psum[:, b, c * P:(c + 1) * P], qT[:, c, j * P:(j + 1) * P], wt["keys"][:, c, :],
                                    start=True, stop=True)
                ins.then_inc(B[b].ready, 1)

            def with_down(j):
                for m, b in enumerate(DOWN_BANKS[j]):
                    free(b, f"w{j}")
                    for k in range(KD):
                        ins = pe.matmul(bank(b), hT[:, k, j * P:(j + 1) * P], wt["down"][:, k, m * 512:(m + 1) * 512],
                                        start=k == 0, stop=k == KD - 1)
                    ins.then_inc(B[b].ready, 1)

            need_hT(pe, sf, i)
            for b in (4, 5):
                free(b, "q")
                for x in range(2):
                    c = 2 * (b - 4) + x
                    for k in range(KD):
                        ins = pe.matmul(psum[:, b, x * TOK:(x + 1) * TOK], wt["wq"][:, k, c * P:(c + 1) * P], hT[:, k, :],
                                        start=k == 0, stop=k == KD - 1)
                ins.then_inc(B[b].ready, 1)
            gate_up(0)
            yield
            gate_up(1)
            gate_up(2)
            with_keys(0)
            yield
            with_keys(1)
            gate_up(3)
            gate_up(4)
            yield
            for m in (5, 6, 7):
                gate_up(m)
            yield
            with_down(0)
            yield
            with_down(1)
            yield
            free(6, "Y")
            for m in (5, 6, 7):
                taken(BANK[m], f"m{m}")
            for j in range(NT):
                y = psum[:, 6, j * D:(j + 1) * D]
                for m in range(NC):
                    pe.matmul(y, hid[:, m, j * P:(j + 1) * P], wt["wd"][:, m, :], start=m == 0, stop=False)
                pe.wait_ge(C_l.ready, C_l.n(sf, i, f"t{j}") + 1)
                for q, b in enumerate(TURN_BANKS[j]):
                    free(b, f"c{j}")
                    for m in range(4):
                        e = q * 4 + m
                        ins = pe.transpose(psum[:, b, m * P:(m + 1) * P], C[j][:, e * P:(e + 1) * P], ident)
                    ins.then_inc(B[b].ready, 1)
                for q, b in enumerate(TURN_BANKS[j]):
                    taken(b, f"c{j}")
                    for m in range(4):
                        e = q * 4 + m
                        ins = pe.matmul(y, CT[:, e, j * P:(j + 1) * P], wt["up"][:, e, :], start=False, stop=e == NEXP // P - 1)
                if j == 0:
                    yield
            ins.then_inc(B[6].ready, 1)
            if more:
                transpose_h(pe, sf, i + 1)
            yield

        def act_ffn(act, i, more):
            def silu(m):
                b = BANK[m]
                act.wait_ge(B[b].ready, B[b].n(sf, i, f"m{m}") + 1)
                if m > 1:
                    before = B[BANK[m - 2]]
                    act.wait_ge(before.free, before.n(sf, i, f"m{m - 2}") + 1)
                act.activation(sg[m % 2], psum[:, b, 0:TOK], ACT.Silu, bias=col("L0f_bg", m)).then_inc(gates_l.ready, 1)

            def take_sims(j):
                b = KEY_BANK[j]
                act.wait_ge(B[b].ready, B[b].n(sf, i, f"s{j}") + 1)
                act.activation(sims[:, j].rearrange("p a b c -> p (a b c)"), bank(b), ACT.Copy).then_inc(B[b].free, 1)

            def exps(j, pair):
                if pair == 0:
                    act.wait_ge(shifted_l.ready, shifted_l.n(sf, i, f"t{j}") + 1)
                    act.activation(e8[:, j], shifted[:, j], ACT.Exp).then_inc(e8_l.ready, 1)
                for hh in (2 * pair, 2 * pair + 1):
                    act.wait_ge(S_l.ready, S_l.n(sf, i, f"{j}{hh}") + 1)
                    if j or hh > 1:
                        act.wait_ge(G_l.ready, G_l.n(sf, i, f"{j}{hh}") - 1)
                    act.activation(E[hh % 2], S[hh].rearrange("p a b -> p (a b)"), ACT.Exp, bias=ntop[:, j, hh:hh + 1]).then_inc(E_l.ready, 1)

            def silu_w(j):
                for m, b in enumerate(DOWN_BANKS[j]):
                    act.wait_ge(B[b].ready, B[b].n(sf, i, f"w{j}") + 1)
                    act.activation(C[j][:, m * 512:(m + 1) * 512], bank(b), ACT.Silu).then_inc(B[b].free, 1)

            for b in (4, 5):
                act.wait_ge(B[b].ready, B[b].n(sf, i, "q") + 1)
                act.activation(qT[:, 2 * (b - 4):2 * (b - 4) + 2, :].rearrange("p a b -> p (a b)"), bank(b), ACT.Copy).then_inc(B[b].free, 1)
            silu(0)
            yield
            silu(1)
            silu(2)
            take_sims(0)
            yield
            take_sims(1)
            silu(3)
            silu(4)
            exps(0, 0)
            yield
            exps(0, 1)
            silu(5)
            silu(6)
            silu(7)
            yield
            silu_w(0)
            exps(1, 0)
            yield
            exps(1, 1)
            silu_w(1)
            yield
            for j in range(NT):
                for q, b in enumerate(TURN_BANKS[j]):
                    act.wait_ge(B[b].ready, B[b].n(sf, i, f"c{j}") + 1)
                    act.activation(CT[:, 4 * q:4 * q + 4, j * P:(j + 1) * P], bank(b).rearrange("p (a b) -> p a b", a=4),
                                   ACT.Copy).then_inc(B[b].free, 1)
                if j == 0:
                    yield
            if more:
                copy_hT(act, sf, i + 1)
            yield

        def pool_ffn(pool, i, more):
            def sums(j):
                b = KEY_BANK[j]
                pool.wait_ge(B[b].free, B[b].n(sf, i, f"s{j}") + 1)
                for hh in range(PH):
                    if j:
                        pool.wait_ge(picked_l.ready, picked_l.n(sf, i, f"{j - 1}{hh}") + 1)
                    x = sims[:, j, 0, hh, 0:PROWS].unsqueeze(2).broadcast_to([P, PROWS, NKEYS])
                    y = sims[:, j, 1, hh, :].unsqueeze(1).broadcast_to([P, PROWS, NKEYS])
                    pool.tensor_tensor(S[hh], x, y, ALU.add).then_inc(S_l.ready, 1)
            yield
            sums(0)
            yield
            yield
            sums(1)
            yield
            for _ in range(3):
                yield
            if more:
                ln_power(pool, sf, i + 1)
            yield

        def hidden(dve, i, m):
            b = BANK[m]
            dve.wait_ge(gates_l.ready, gates_l.n(sf, i, f"m{m}") + 1)
            dve.scalar_tensor_tensor(hid[:, m, :], psum[:, b, TOK:2 * TOK], col("L0f_bu", m), sg[m % 2], ALU.add, ALU.mult).then_inc(B[b].free, 1)

        def select(dve, i, j, step):
            dve.wait_ge(B[KEY_BANK[j]].free, B[KEY_BANK[j]].n(sf, i, f"s{j}") + 1)
            dve.memset(pad[:, 0:1], 0.0)
            for hh in range(PH):
                dve.max(tx[:, hh, :], sims[:, j, 0, hh, :]).then_inc(dve_steps, step.one())
                dve.max(ty[:, hh, :], sims[:, j, 1, hh, :]).then_inc(dve_steps, step.one())
            dve.wait_ge(dve_steps, step.done)
            dve.tensor_tensor(grid, tx.unsqueeze(3).broadcast_to([P, PH, TOPK, TOPK]),
                              ty.unsqueeze(2).broadcast_to([P, PH, TOPK, TOPK]), ALU.add).then_inc(dve_steps, step.one())
            dve.wait_ge(dve_steps, step.done)
            dve.memset(pad[:, 0:1], 0.0)
            for hh in range(PH):
                dve.max(top[:, hh, :], grid[:, hh].rearrange("p a b -> p (a b)")).then_inc(dve_steps, step.one())
            dve.wait_ge(dve_steps, step.done)
            dve.tensor_scalar(ntop[:, j, :], top[:, :, 0], -1.0, None, ALU.mult).then_inc(dve_steps, step.one())
            dve.tensor_copy(thr[:, j, :], top[:, :, TOPK - 1]).then_inc(dve_steps, step.one())
            dve.wait_ge(dve_steps, step.done)
            dve.tensor_tensor(shifted[:, j], top, ntop[:, j, :].unsqueeze(2).broadcast_to([P, PH, TOPK]),
                              ALU.add).then_inc(shifted_l.ready, 1)

        def normalise(dve, i, j, step):
            dve.wait_ge(e8_l.ready, e8_l.n(sf, i, f"t{j}") + 1)
            dve.tensor_reduce(z[:, j, :], e8[:, j], AXIS_X, ALU.add).then_inc(dve_steps, step.one())
            dve.wait_ge(dve_steps, step.done)
            dve.reciprocal(rz[:, j, :], z[:, j, :]).then_inc(dve_steps, step.one())

        def accumulate(dve, i, j, hh, step):
            at = f"{j}{hh}"
            dve.wait_ge(E_l.ready, E_l.n(sf, i, at) + 1)
            dve.scalar_tensor_tensor(E[hh % 2], S[hh].rearrange("p a b -> p (a b)"), thr[:, j, hh:hh + 1], E[hh % 2],
                                     ALU.is_ge, ALU.mult).then_inc(picked_l.ready, 1)
            dve.wait_ge(picked_l.ready, picked_l.n(sf, i, at) + 1)
            if hh == 0:
                dve.wait_ge(dve_steps, step.done)
                dve.tensor_scalar(G[j], E[hh % 2], rz[:, j, hh:hh + 1], None, ALU.mult).then_inc(G_l.ready, 1)
                return
            dve.wait_ge(G_l.ready, G_l.n(sf, i, at))
            last = hh == PH - 1
            dve.scalar_tensor_tensor(G[j], E[hh % 2], rz[:, j, hh:hh + 1], G[j], ALU.mult, ALU.add,
                                     accum_out=left[:, j, 0:1] if last else None).then_inc(G_l.ready, 1)
            if last:
                dve.wait_ge(G_l.ready, G_l.n(sf, i, at) + 1)
                dve.tensor_scalar(left[:, j, 1:2], left[:, j, 0:1], -1.0, float(PH), ALU.mult, ALU.add).then_inc(dve_steps, step.one())
                dve.wait_ge(dve_steps, step.done)
                dve.tensor_tensor(G[j][:, NEXP - 1:NEXP], G[j][:, NEXP - 1:NEXP], left[:, j, 1:2], ALU.add).then_inc(dve_steps, step.one())

        def combine(dve, i, j, step):
            for b in DOWN_BANKS[j]:
                dve.wait_ge(B[b].free, B[b].n(sf, i, f"w{j}") + 1)
            dve.wait_ge(dve_steps, step.done)
            dve.tensor_tensor(C[j], C[j], G[j], ALU.mult).then_inc(C_l.ready, 1)

        def dve_ffn(dve, i, more):
            step = steps[0]
            hidden(dve, i, 0)
            yield
            hidden(dve, i, 1)
            hidden(dve, i, 2)
            select(dve, i, 0, step)
            yield
            hidden(dve, i, 3)
            hidden(dve, i, 4)
            normalise(dve, i, 0, step)
            accumulate(dve, i, 0, 0, step)
            accumulate(dve, i, 0, 1, step)
            yield
            accumulate(dve, i, 0, 2, step)
            accumulate(dve, i, 0, 3, step)
            for m in (5, 6, 7):
                hidden(dve, i, m)
            select(dve, i, 1, step)
            yield
            normalise(dve, i, 1, step)
            accumulate(dve, i, 1, 0, step)
            accumulate(dve, i, 1, 1, step)
            yield
            accumulate(dve, i, 1, 2, step)
            accumulate(dve, i, 1, 3, step)
            combine(dve, i, 0, step)
            combine(dve, i, 1, step)
            yield
            yield
            if more:
                dve.wait_ge(attended, i + 2)
                dve.memset(pad[:, 5:6], 0.0)
                ln_stats(dve, sf, i + 1, step, X[:, i + 1])
                ln_apply(dve, sf, i + 1, X[:, i + 1])
            dve.wait_ge(B[6].ready, B[6].n(sf, i) + 1)
            x = X[:, i].rearrange("p a b -> p (a b)")
            dve.tensor_tensor(x, bank(6), x, ALU.add).then_inc(B[6].free, 1)
            dve.wait_ge(B[6].free, B[6].n(sf, i) + 1)
            dve.tensor_tensor(X[:, i], X[:, i], row("L0f_bd").unsqueeze(1).broadcast_to([P, NT, D]), ALU.add).then_inc(updated, 1)
            yield

        ffn = dict(pe=pe_ffn, act=act_ffn, pool=pool_ffn, dve=dve_ffn)
        return beside(s, sx, sf, cross, ffn, attended, steps)

    def local(s):
        NI = INNER // P
        HALF = WD // 2
        area = Area(WORK2)
        cos = [{n: area.take(NT, WD) for n in "qk"} for _ in range(2)]
        sin = [{n: area.take(NT, WD) for n in "qk"} for _ in range(2)]
        sm = Area(0, small)
        tables = sem("rotary_tables")
        steps = [Steps()]
        HEADS_OF = [[0, 1, 2, 3], [4, 5, 6, 7], [0, 1], [2, 3], [4, 5], [6, 7]]
        GROUP_BANK = [2, 3, 1, 2, 3, 1]

        def chunk(m):
            return P if m < NHC - 1 else HREM

        def both_layers(uses):
            return " ".join(u + l for l in "ab" for u in uses.split())

        def stream(x):
            f = front[x]
            c0 = 4 * x
            b = B[c0:c0 + 4]
            h, hT = f.h, f.hT
            at = area.at
            qk0, turned0, other0 = (area.take(2, WH, WD) for _ in range(3))
            mlp = Area(at)
            hid, gel, hs, hsT = mlp.take(NHC, TOK), mlp.take(2, TOK), mlp.take(NT, D), mlp.take(KD, TOK)
            assert mlp.at <= area.at
            v = area.take(NT, INNER)
            at = area.at
            qT, kT = area.take(NI, TOK), area.take(NI, TOK)
            PT = view(at, (2 * WH, P))
            at = area.at
            Pj = [area.take(WH, P), area.take(WH, 2 * P)]
            turned1, qk1, other1 = (view(at + k * WH * P, (2, WH, WD)) for k in range(3))
            qk, turned, other = (qk0, qk1), (turned0, turned1), (other0, other1)
            o, oT = view(at, (NT, INNER)), view(at + WH * P, (NI, TOK))
            z1 = area.take(NT, D)
            ssq, rn = sm.take(NT, 2 * WH), sm.take(NT, 2 * WH)
            mx, nmax, den, rden = sm.take(NT, WH), sm.take(NT, WH), sm.take(NT, WH), sm.take(NT, WH)
            st, mo, var, rs = sm.take(NT, 6), sm.take(NT, 2), sm.take(NT), sm.take(NT)
            f.plan(s, nb // 2, h_uses="ha hb")
            plan_uses(s, nb // 2, {
                c0: both_layers("q0 q1 S0 S1 O0 O1 sh g0 g2 g4 Y2"),
                c0 + 1: both_layers("k0 k1 S0 S1 p2 p5 o0 hf g1 g3 g5"),
                c0 + 2: both_layers("v0 v1 tq0 tq1 S1 p0 p3 o1 g0 g2 g4"),
                c0 + 3: both_layers("T tk0 tk1 S1 p1 p4 Y g1 g3 g5")},
                **{f"{n}{x}": both_layers("0 1") for n in ("squares", "norms", "inverse_norms", "other", "rotated", "scaled", "nmax", "E")},
                **{f"{n}{x}": "a b" for n in ("z1", "hs_variance", "hs_rstd", "hs")})
            sq_l, ssq_l, rn_l, other_l, rot_l, scaled_l, nmax_l, E_l, z1_l, var_l, rs_l, hs_l = (link(f"{n}{x}") for n in (
                "squares", "norms", "inverse_norms", "other", "rotated", "scaled", "nmax", "E", "z1",
                "hs_variance", "hs_rstd", "hs"))

            def free(eng, k, i, use):
                eng.wait_ge(b[k].free, b[k].n(s, i, use))

            def ready(eng, k, i, use):
                eng.wait_ge(b[k].ready, b[k].n(s, i, use) + 1)

            def taken(eng, k, i, use):
                eng.wait_ge(b[k].free, b[k].n(s, i, use) + 1)

            def pe_head(pe, i, l):
                wt, L = W["L1" + l], l
                yield
                free(pe, 3, i, "T" + L)
                pe.wait_ge(f.h_l.ready, f.h_l.n(s, i, "h" + L) + 1)
                for k in range(KD):
                    for j in range(NT):
                        ins = pe.transpose(psum[:, c0 + 3, k * TOK + j * P:k * TOK + (j + 1) * P], h[:, j, k * P:(k + 1) * P], ident)
                ins.then_inc(b[3].ready, 1)
                yield
                taken(pe, 3, i, "T" + L)
                for j in range(NT):
                    for c, n in enumerate("qkv"):
                        free(pe, c, i, f"{n}{j}{L}")
                        for k in range(KD):
                            ins = pe.matmul(bank(c0 + c), hT[:, k, j * P:(j + 1) * P], wt["wqkv"][:, k, c * INNER:(c + 1) * INNER],
                                            start=k == 0, stop=k == KD - 1)
                        ins.then_inc(b[c].ready, 1)
                    yield
                yield
                for j in range(NT):
                    pe.wait_ge(scaled_l.ready, scaled_l.n(s, i, f"{j}{L}") + 1)
                    for c, n in ((2, "tq"), (3, "tk")):
                        free(pe, c, i, f"{n}{j}{L}")
                        src = turned[j][:, c - 2].rearrange("p h d -> p (h d)")
                        for m in range(NI):
                            ins = pe.transpose(psum[:, c0 + c, m * P:(m + 1) * P], src[:, m * P:(m + 1) * P], ident)
                        ins.then_inc(b[c].ready, 1)
                    yield
                for odd in range(2):
                    free(pe, odd, i, "S0" + L)
                for c in (2, 3):
                    free(pe, c, i, "S1" + L)
                for odd in range(2):
                    r = slice(odd * WD, (odd + 1) * WD)
                    for m in range(NI):
                        ins = pe.matmul(psum[:, c0 + odd, m * P:(m + 1) * P], qT[r, m, 0:P], kT[r, m, 0:P], start=True, stop=True)
                    ins.then_inc(b[odd].ready, 1)

                def scores1(odd):
                    r = slice(odd * WD, (odd + 1) * WD)
                    for m in range(NI):
                        c = (0 if odd else 2) + m // 2
                        ins = pe.matmul(psum[:, c0 + c, (m % 2) * 2 * P:(m % 2 + 1) * 2 * P], qT[r, m, P:2 * P], kT[r, m, :], start=True, stop=True)
                        if m % 2:
                            ins.then_inc(b[c].ready, 1)
                scores1(0)
                yield
                for c in (0, 1):
                    free(pe, c, i, "S1" + L)
                scores1(1)
                yield

                def turn(g):
                    c = GROUP_BANK[g]
                    free(pe, c, i, f"p{g}{L}")
                    blocks = [Pj[0][:, hh, :] for hh in HEADS_OF[g]] if g < 2 else \
                        [Pj[1][:, hh, kb * P:(kb + 1) * P] for hh in HEADS_OF[g] for kb in range(2)]
                    for k, block in enumerate(blocks):
                        ins = pe.transpose(psum[:, c0 + c, k * P:(k + 1) * P], block, ident)
                    ins.then_inc(b[c].ready, 1)

                pe.wait_ge(E_l.ready, E_l.n(s, i, "0" + L) + 1)
                turn(0)
                turn(1)
                yield
                free(pe, 0, i, "O0" + L)
                for g in (0, 1):
                    taken(pe, GROUP_BANK[g], i, f"p{g}{L}")
                for hh in range(WH):
                    ins = pe.matmul(psum[:, c0, hh * WD:(hh + 1) * WD], PT[:, hh, :], v[:, 0, hh * WD:(hh + 1) * WD], start=True, stop=True)
                ins.then_inc(b[0].ready, 1)
                pe.wait_ge(E_l.ready, E_l.n(s, i, "1" + L) + 1)
                for g in (2, 3, 4, 5):
                    turn(g)
                yield
                free(pe, 0, i, "O1" + L)
                for g in (3, 4, 5):
                    taken(pe, GROUP_BANK[g], i, f"p{g}{L}")
                for hh in range(WH):
                    for kb in range(2):
                        ins = pe.matmul(psum[:, c0, hh * WD:(hh + 1) * WD], PT[:, 2 * hh + kb, :], v[:, kb, hh * WD:(hh + 1) * WD],
                                        start=kb == 0, stop=kb == 1)
                ins.then_inc(b[0].ready, 1)
                yield
                for j in range(NT):
                    taken(pe, 0, i, f"O{j}{L}")
                    free(pe, 1 + j, i, f"o{j}{L}")
                    for m in range(NI):
                        ins = pe.transpose(psum[:, c0 + 1 + j, m * P:(m + 1) * P], o[:, j, m * P:(m + 1) * P], ident)
                    ins.then_inc(b[1 + j].ready, 1)
                yield

            def pe_tail(pe, i, l):
                wt, L = W["L1" + l], l
                free(pe, 3, i, "Y" + L)
                for j in range(NT):
                    taken(pe, 1 + j, i, f"o{j}{L}")
                    for m in range(NI):
                        ins = pe.matmul(psum[:, c0 + 3, j * D:(j + 1) * D], oT[:, m, j * P:(j + 1) * P], wt["wo"][:, m, :],
                                        start=m == 0, stop=m == NI - 1)
                ins.then_inc(b[3].ready, 1)
                yield
                pe.wait_ge(z1_l.ready, z1_l.n(s, i, L) + 1)
                free(pe, 0, i, "sh" + L)
                for j in range(NT):
                    out_ = psum[:, c0, j * P:(j + 1) * P]
                    ins = pe.matmul(out_, const("shift"), z1[:, j, P:D], start=True, stop=j == 0)
                    if j:
                        ins = pe.matmul(out_, const("edge"), z1[:, j - 1, P:D], start=False, stop=True)
                ins.then_inc(b[0].ready, 1)
                yield
                pe.wait_ge(hs_l.ready, hs_l.n(s, i, L) + 1)
                free(pe, 1, i, "hf" + L)
                for k in range(KD):
                    for j in range(NT):
                        ins = pe.transpose(psum[:, c0 + 1, k * TOK + j * P:k * TOK + (j + 1) * P], hs[:, j, k * P:(k + 1) * P], ident)
                ins.then_inc(b[1].ready, 1)
                yield
                taken(pe, 1, i, "hf" + L)
                for m in range(NHC):
                    M = chunk(m)
                    for c, at in ((m % 2, HID), (2 + m % 2, 0)):
                        free(pe, c, i, f"g{m}{L}")
                        for k in range(KD):
                            ins = pe.matmul(psum[0:M, c0 + c, 0:TOK], wt["w1"][:, k, at + m * P:at + m * P + M], hsT[:, k, :],
                                            start=k == 0, stop=k == KD - 1)
                        ins.then_inc(b[c].ready, 1)
                    if m % 2:
                        yield
                free(pe, 0, i, "Y2" + L)
                for c in (2, 3):
                    taken(pe, c, i, f"g{c + 2}{L}")
                for j in range(NT):
                    for m in range(NHC):
                        M = chunk(m)
                        ins = pe.matmul(psum[:, c0, j * D:(j + 1) * D], hid[0:M, m, j * P:(j + 1) * P], wt["w2"][0:M, m, :],
                                        start=m == 0, stop=m == NHC - 1)
                ins.then_inc(b[0].ready, 1)
                yield

            def act_head(act, i, l):
                L = l
                yield
                ready(act, 3, i, "T" + L)
                act.activation(hT[:, 0, :], psum[:, c0 + 3, 0:TOK], ACT.Copy)
                act.activation(hT[:, 1, 1:TOK], psum[:, c0 + 3, TOK:2 * TOK - 1], ACT.Copy).then_inc(b[3].free, 1)
                yield
                for j in range(NT):
                    for c in range(2):
                        ready(act, c, i, f"{'qk'[c]}{j}{L}")
                        act.activation(qk[j][:, c].rearrange("p h d -> p (h d)"), bank(c0 + c), ACT.Copy).then_inc(b[c].free, 1)
                    ready(act, 2, i, f"v{j}{L}")
                    act.activation(v[:, j, :], bank(c0 + 2), ACT.Copy).then_inc(b[2].free, 1)
                    for c in range(2):
                        taken(act, c, i, f"{'qk'[c]}{j}{L}")
                    act.activation(other[j].rearrange("p a b c -> p (a b c)"), qk[j].rearrange("p a b c -> p (a b c)"),
                                   ACT.Square).then_inc(sq_l.ready, 1)
                    yield
                yield
                for j in range(NT):
                    for c, n, dst in ((2, "tq", qT), (3, "tk", kT)):
                        ready(act, c, i, f"{n}{j}{L}")
                        act.activation(dst[:, :, j * P:(j + 1) * P], bank(c0 + c).rearrange("p (a b) -> p a b", a=NI), ACT.Copy).then_inc(b[c].free, 1)
                    yield
                for j in range(NT):
                    act.wait_ge(nmax_l.ready, nmax_l.n(s, i, f"{j}{L}") + 1)
                    for hh in range(WH):
                        ins = act.activation(Pj[j][:, hh, :], Pj[j][:, hh, :], ACT.Exp, scale=QK_SCALE, bias=nmax[:, j, hh:hh + 1],
                                             accum_out=den[:, j, hh:hh + 1])
                    ins.then_inc(E_l.ready, 1)
                    yield
                for groups in ((0, 1), (2, 3, 4, 5)):
                    for g in groups:
                        c, to = GROUP_BANK[g], 4 * (g if g < 2 else g - 2)
                        ready(act, c, i, f"p{g}{L}")
                        act.activation(PT[:, to:to + 4, :].rearrange("p a b -> p (a b)"), bank(c0 + c), ACT.Copy).then_inc(b[c].free, 1)
                    yield
                yield
                for j in range(NT):
                    ready(act, 1 + j, i, f"o{j}{L}")
                    act.activation(oT[:, :, j * P:(j + 1) * P], bank(c0 + 1 + j).rearrange("p (a b) -> p a b", a=NI), ACT.Copy).then_inc(b[1 + j].free, 1)
                yield

            def act_tail(act, i, l):
                L, name = l, "L1" + l
                yield
                yield
                ready(act, 1, i, "hf" + L)
                for k in range(KD):
                    ins = act.activation(hsT[:, k, :], psum[:, c0 + 1, k * TOK:(k + 1) * TOK], ACT.Identity,
                                         scale=col(name + "_g", k), bias=col(name + "_b", k))
                ins.then_inc(b[1].free, 1)
                yield
                for m in range(NHC):
                    M, c = chunk(m), m % 2
                    k = COL_AT[name + "_b1g"][0] + m
                    ready(act, c, i, f"g{m}{L}")
                    free(act, 2 + c, i, f"g{m}{L}")
                    act.activation(gel[0:M, c, :], psum[0:M, c0 + c, 0:TOK], ACT.Gelu, bias=cols[0:M, k:k + 1]).then_inc(b[c].free, 1)
                    if m % 2:
                        yield
                yield

            def pool_head(pool, i, l):
                L = l
                if l == "a":
                    f.ln_power(pool, s, i)
                yield
                yield
                yield
                for j in range(NT):
                    pool.wait_ge(ssq_l.ready, ssq_l.n(s, i, f"{j}{L}") + 1)
                    pool.tensor_tensor(rn[:, j, :], ssq[:, j, :], minus_half[:, 0:2 * WH], ALU.pow).then_inc(rn_l.ready, 1)
                    for c in range(2):
                        taken(pool, c, i, f"{'qk'[c]}{j}{L}")
                        n = "qk"[c]
                        for a_, b_ in ((slice(0, HALF), slice(HALF, WD)), (slice(HALF, WD), slice(0, HALF))):
                            ins = pool.tensor_tensor(other[j][:, c, :, a_], qk[j][:, c, :, b_],
                                                     sin["ab".index(l)][n][:, j, a_].unsqueeze(1).broadcast_to([P, WH, HALF]), ALU.mult)
                    ins.then_inc(other_l.ready, 1)
                    yield
                for _ in range(8):
                    yield

            def pool_tail(pool, i, l):
                L = l
                yield
                pool.wait_ge(var_l.ready, var_l.n(s, i, L) + 1)
                pool.tensor_tensor(rs, var, minus_half[:, 0:NT], ALU.pow).then_inc(rs_l.ready, 1)
                for _ in range(6):
                    yield

            def dve_head(dve, i, l):
                L, step = l, steps[0]
                if l == "a":
                    f.ln_stats(dve, s, i, step, XR[:, i, x])
                    f.ln_apply(dve, s, i, XR[:, i, x], "Ta")
                yield
                yield
                yield

                def turn(j):
                    dve.wait_ge(sq_l.ready, sq_l.n(s, i, f"{j}{L}") + 1)
                    dve.tensor_reduce(ssq[:, j, :], other[j].rearrange("p a b c -> p (a b) c"), AXIS_X, ALU.add).then_inc(dve_steps, step.one())
                    dve.wait_ge(dve_steps, step.done)
                    dve.tensor_scalar(ssq[:, j, :], ssq[:, j, :], 1e-24, None, ALU.max).then_inc(ssq_l.ready, 1)
                    for c, n in enumerate("qk"):
                        dve.tensor_tensor(turned[j][:, c], qk[j][:, c],
                                          cos["ab".index(l)][n][:, j].unsqueeze(1).broadcast_to([P, WH, WD]), ALU.mult).then_inc(dve_steps, step.one())

                def scale(j):
                    dve.wait_ge(other_l.ready, other_l.n(s, i, f"{j}{L}") + 1)
                    dve.wait_ge(dve_steps, step.done)
                    flat = turned[j].rearrange("p a b c -> p (a b c)")
                    dve.tensor_tensor(flat, flat, other[j].rearrange("p a b c -> p (a b c)"), ALU.add).then_inc(rot_l.ready, 1)
                    dve.wait_ge(rot_l.ready, rot_l.n(s, i, f"{j}{L}") + 1)
                    dve.wait_ge(rn_l.ready, rn_l.n(s, i, f"{j}{L}") + 1)
                    t16 = turned[j].rearrange("p a b c -> p (a b) c")
                    dve.tensor_tensor(t16, t16, rn[:, j, :].unsqueeze(2).broadcast_to([P, 2 * WH, WD]), ALU.mult).then_inc(scaled_l.ready, 1)

                turn(0)
                yield
                turn(1)
                scale(0)
                yield
                scale(1)
                yield
                yield
                for j in range(NT):
                    held = [(0, [0, 2, 4, 6]), (1, [1, 3, 5, 7])] if j == 0 else \
                        [(2, [0, 2]), (3, [4, 6]), (0, [1, 3]), (1, [5, 7])]
                    mask, n = (const("band"), 2 * P) if j else (const("causal"), P)
                    for c, heads in held:
                        ready(dve, c, i, f"S{j}{L}")
                        dve.memset(pad[:, 4 * x + c:4 * x + c + 1], 0.0)
                        for k, hh in enumerate(heads):
                            ins = dve.tensor_tensor_reduce(out=Pj[j][:, hh, :], in0=psum[:, c0 + c, k * n:(k + 1) * n], in1=mask,
                                                           scale=1.0, scalar=MASKED, op0=ALU.add, op1=ALU.max,
                                                           accum_out=mx[:, j, hh:hh + 1])
                        ins.then_inc(b[c].free, 1)
                    for c, _ in held:
                        taken(dve, c, i, f"S{j}{L}")
                    dve.tensor_scalar(nmax[:, j, :], mx[:, j, :], -QK_SCALE, None, ALU.mult).then_inc(nmax_l.ready, 1)
                    yield
                yield
                for j in range(NT):
                    dve.wait_ge(E_l.ready, E_l.n(s, i, f"{j}{L}") + 1)
                    dve.reciprocal(rden[:, j, :], den[:, j, :]).then_inc(dve_steps, step.one())
                    dve.wait_ge(dve_steps, step.done)
                    ready(dve, 0, i, f"O{j}{L}")
                    dve.tensor_tensor(o[:, j, :].rearrange("p (h d) -> p h d", d=WD), bank(c0).rearrange("p (h d) -> p h d", d=WD),
                                      rden[:, j, :].unsqueeze(2).broadcast_to([P, WH, WD]), ALU.mult).then_inc(b[0].free, 1)
                    yield
                yield

            def dve_tail(dve, i, l):
                L, name, step = l, "L1" + l, steps[0]
                zf, hf = z1.rearrange("p a b -> p (a b)"), h[:].rearrange("p a b -> p (a b)")
                ready(dve, 3, i, "Y" + L)
                dve.tensor_tensor(zf, bank(c0 + 3), hf, ALU.add).then_inc(b[3].free, 1)
                taken(dve, 3, i, "Y" + L)
                dve.tensor_copy(hs[:, :, 0:P], z1[:, :, 0:P]).then_inc(z1_l.ready, 1)
                yield
                ready(dve, 0, i, "sh" + L)
                dve.tensor_copy(hs[:, :, P:D], psum[:, c0, 0:NT * P].rearrange("p (a b) -> p a b", a=NT)).then_inc(b[0].free, 1)
                taken(dve, 0, i, "sh" + L)
                dve.wait_ge(z1_l.ready, z1_l.n(s, i, L) + 1)
                for j in range(NT):
                    dve.bn_stats(st[:, j, :], hs[:, j, :]).then_inc(dve_steps, step.one())
                dve.wait_ge(dve_steps, step.done)
                for j in range(NT):
                    dve.bn_aggr(mo[:, j, :], st[:, j, :]).then_inc(dve_steps, step.one())
                dve.wait_ge(dve_steps, step.done)
                dve.tensor_scalar(var, mo[:, :, 1], EPS, None, ALU.add).then_inc(var_l.ready, 1)
                dve.wait_ge(rs_l.ready, rs_l.n(s, i, L) + 1)
                for j in range(NT):
                    ins = dve.tensor_scalar(hs[:, j, :], hs[:, j, :], mo[:, j, 0:1], rs[:, j:j + 1], ALU.subtract, ALU.mult)
                ins.then_inc(hs_l.ready, 1)
                yield
                yield
                for m in range(NHC):
                    M, c = chunk(m), 2 + m % 2
                    ready(dve, c, i, f"g{m}{L}")
                    taken(dve, c - 2, i, f"g{m}{L}")
                    k = COL_AT[name + "_b1a"][0] + m
                    dve.scalar_tensor_tensor(hid[0:M, m, :], psum[0:M, c0 + c, 0:TOK], cols[0:M, k:k + 1], gel[0:M, m % 2, :],
                                             ALU.add, ALU.mult).then_inc(b[c].free, 1)
                    if m % 2:
                        yield
                ready(dve, 0, i, "Y2" + L)
                dve.tensor_tensor(zf, bank(c0), zf, ALU.add).then_inc(b[0].free, 1)
                taken(dve, 0, i, "Y2" + L)
                b2 = row(name + "_b2").unsqueeze(1).broadcast_to([P, NT, D])
                if l == "a":
                    dve.tensor_tensor(h[:], z1, b2, ALU.add).then_inc(f.h_l.ready, 1)
                else:
                    dve.tensor_tensor(z1, z1, b2, ALU.add).then_inc(dve_steps, step.one())
                    dve.wait_ge(dve_steps, step.done)
                    dve.tensor_tensor(XR[:, i, x], z1, XR[:, i, x], ALU.add).then_inc(updated, 1)
                yield
            return dict(pe_head=pe_head, pe_tail=pe_tail, act_head=act_head, act_tail=act_tail,
                        pool_head=pool_head, pool_tail=pool_tail, dve_head=dve_head, dve_tail=dve_tail)

        pair = [stream(x) for x in range(2)]

        def first(name, eng):
            for _ in pair[1][name + "_head"](eng, 0, "a"):
                pass

        def both(name, eng, i, more):
            def leading():
                head, tail = pair[1][name + "_head"], pair[1][name + "_tail"]
                yield from tail(eng, i, "a")
                yield from head(eng, i, "b")
                yield from tail(eng, i, "b")
                if more:
                    yield from head(eng, i + 1, "a")

            def following():
                head, tail = pair[0][name + "_head"], pair[0][name + "_tail"]
                for l in "ab":
                    yield from head(eng, i, l)
                    yield from tail(eng, i, l)
            by_turns(following(), leading())

        def pe(pe):
            begin(pe, s)
            pe.wait_ge(loaded["base"], LOADS["base"])
            pe.wait_ge(loaded[s], LOADS[s])
            first("pe", pe)
            for i, more in rounds(pe):
                both("pe", pe, i, more)

        def act(act):
            begin(act, s)
            act.wait_ge(loaded["base"], LOADS["base"])
            for f in front:
                act.activation(f.hT[:, 1, 0:1], pad_act[:, 0:1], ACT.Copy)
            first("act", act)
            for i, more in rounds(act):
                both("act", act, i, more)

        def pool(pool):
            begin(pool, s)
            pool.wait_ge(tables, 1)
            first("pool", pool)
            for i, more in rounds(pool):
                both("pool", pool, i, more)

        def dve(dve):
            steps[0] = step = Steps()
            begin(dve, s)
            dve.wait_ge(loaded["base"], LOADS["base"])
            for l, name in enumerate(("L1a", "L1b")):
                for n in "qk":
                    scale = row(f"{name}_{n}s")
                    c, t = (const(f"{k}_{n}").rearrange("p (j d) -> p j d", j=NT) for k in ("cos", "sin"))
                    dve.tensor_tensor(cos[l][n], c, scale.unsqueeze(1).broadcast_to([P, NT, WD]), ALU.mult).then_inc(dve_steps, step.one())
                    for a_, b_ in ((slice(0, HALF), slice(HALF, WD)), (slice(HALF, WD), slice(0, HALF))):
                        ins = dve.tensor_tensor(sin[l][n][:, :, a_], t[:, :, a_], scale[:, b_].unsqueeze(1).broadcast_to([P, NT, HALF]), ALU.mult)
            ins.then_inc(tables, 1)
            first("dve", dve)
            dve.wait_ge(dve_steps, step.done)
            dve.sem_clear(dve_steps)
            for i, more in rounds(dve):
                steps[0] = step = Steps()
                both("dve", dve, i, more)
                dve.wait_ge(dve_steps, step.done)
                dve.sem_clear(dve_steps)
        return dict(tensor=pe, scalar=act, gpsimd=pool, vector=dve)

    parts = {"L0": memory("L0"), "L1x": single("L1x"), "L1f": local("L1f"), "L2x": cross("L2x"), "L2f": ternary("L2f"),
             "L3": experts("L3")}
    block = ctx.enter_context(nc.Block())

    @block.sync
    def _(sp):
        for l in B + list(links.values()):
            for counter in l.sems:
                sp.sem_inc(counter, 1)
        x = a["x"].rearrange("(b t p) d -> b p t d", p=P, t=NT)
        sp.dma_start(consts[:], a["consts"]).then_inc(loaded["base"], 16)
        sp.dma_start(cols[:], a["cols"]).then_inc(loaded["base"], 16)
        sp.dma_start(X[:, 0], x[0]).then_inc(loaded["base"], 16)
        sp.dma_start(X[:, 1], x[1]).then_inc(loaded["base"], 16)
        sp.dma_start(rows[:], a["rows"].partition_broadcast(P)).then_inc(loaded["base"], 16)
        sp.dma_start(mask_bytes[:], a["mask"].rearrange("(j p) k -> p j k", p=P)).then_inc(loaded["base"], 16)
        for s, part in parts.items():
            if "sync" in part:
                part["sync"](sp)
            else:
                load_weights(sp, s)
        sp.wait_ge(stored, 16 * nb)

    @block.gpsimd
    def _(pool):
        pool.memset(W["L0f"]["keys"], 0.0).then_inc(zeroed, 1)
        for part in parts.values():
            part["gpsimd"](pool)

    @block.scalar
    def _(act):
        for b in range(2, nb):
            act.dma_start(X[:, b], a["x"].rearrange("(b t p) d -> b p t d", p=P, t=NT)[b]).then_inc(loaded["rest"], 16)
        act.wait_ge(made, 1)
        for part in parts.values():
            part["scalar"](act)

    @block.tensor
    def _(pe):
        for part in parts.values():
            part["tensor"](pe)

    @block.vector
    def _(dve):
        dve.memset(minus_half[:], -0.5)
        dve.memset(pad_act[:], 0.0)
        dve.memset(pad[:], 0.0).then_inc(made, 1)
        dve.wait_ge(loaded["base"], LOADS["base"])
        for part in parts.values():
            part["vector"](dve)


def layout(inputs):
    import numpy as np

    g = {k: np.asarray(v) for k, v in inputs.items()}
    a = {"x": g["x"].reshape(-1, D), "ctx": g["ctx_1024"],
         "mask": g["mask_1x1xSxS2_bk0"].reshape(TOK, S2)}
    for s, names in (("L0x", ("L0_xattn_Wq", "L0_xattn_Wk", "L0_xattn_Wv", "L0_xattn_Wo")),
                     ("L2x", ("L2_xattn_W_q", "L2_xattn_W_k", "L2_xattn_W_v", "L2_xattn_W_o")),
                     ("L3x", ("L3_xattn_wq", "L3_xattn_wk", "L3_xattn_wv", "L3_xattn_wo"))):
        for n, name in zip(("wq", "wk", "wv", "wo"), names):
            a[f"{s}_{n}"] = g[name]
    for n in "qkv":
        a[f"L1x_w{n}"] = g[f"L1_xattn_W{n}"].T
    a["L0f_wg"], a["L0f_wu"], a["L0f_wd"], a["L0f_wq"] = (g[f"L0_ffn_{n}"] for n in ("Wg", "Wu", "Wd", "Wq"))
    a["L0f_keys"] = g["L0_ffn_keys"].transpose(2, 0, 3, 1).reshape(4, P, NKEYS)
    a["L0f_down"], a["L0f_up"] = g["L0_ffn_down_embed"].T, g["L0_ffn_up_embed"]
    for l, s in enumerate(("L1a", "L1b")):
        for n in ("wqkv", "wo", "w1", "w2"):
            a[f"{s}_{n}"] = g[f"L1_ffn_{n}"][l]
    a["L2f_fc"], a["L2f_proj"] = g["L2_ffn_W_fc"].T, g["L2_ffn_W_proj"].T
    a["L3f_router"] = g["L3_ffn_router_w"].T
    for n in "gud":
        shared, routed = g[f"L3_ffn_s{n}"], g[f"L3_ffn_e{n}"]
        a[f"L3f_{n}"] = np.concatenate([shared[None], routed]).transpose(0, 2, 1)

    def column(v, k):
        return np.concatenate([v, np.zeros(k * P - v.size, v.dtype)]).reshape(k, P).T

    c = {f"{s}_b{n}": g[f"{s[:2]}_xattn_b{n}"] for s in ("L0x", "L1x", "L3x") for n in "qk"}
    c.update(L0f_bg=g["L0_ffn_bg"], L0f_bu=g["L0_ffn_bu"], L2f_w=g["L2_ffn_ln_w"], L2f_b=g["L2_ffn_ln_b"])
    r = {f"{s}_b{n}": g[f"{s[:2]}_xattn_b{n}"] for s in ("L0x", "L3x") for n in "vo"}
    r.update(L0f_bd=g["L0_ffn_bd"], L1x_bv=g["L1_xattn_bv"])
    for l, s in enumerate(("L1a", "L1b")):
        b1 = g["L1_ffn_b1"][l]
        c.update({f"{s}_g": g["L1_ffn_ln_g"][l], f"{s}_b": g["L1_ffn_ln_b"][l], f"{s}_b1a": b1[:HID], f"{s}_b1g": b1[HID:]})
        r.update({f"{s}_b2": g["L1_ffn_b2"][l], f"{s}_qs": g["L1_ffn_q_scale"][l], f"{s}_ks": g["L1_ffn_k_scale"][l]})
    a["cols"] = np.concatenate([column(c[n], k) for n, k in COLS.items()], axis=1)
    a["rows"] = np.concatenate([r[n] for n in ROWS])
    a["consts"] = constants()
    return {k: np.ascontiguousarray(v) for k, v in a.items()}


def constants():
    import numpy as np

    p, f32 = np.arange(P)[:, None], np.float32
    q, j = p, np.arange(P)[None, :]
    j2 = np.arange(2 * P)[None, :]
    half = np.arange(0, WD, 2, dtype=f32)
    inv_freq = (f32(1.0) / f32(10000.0) ** (half / f32(WD))).astype(f32)
    t = np.arange(TOK, dtype=f32)
    freqs = t[:, None] * inv_freq[None, :]
    freqs = np.concatenate([freqs, freqs], axis=-1)
    base = (half + f32(0.4 * WD)) / f32(1.4 * WD)
    power = (t - f32(TOK // 2)) / f32(P // 2)
    scale = base[None, :] ** power[:, None]
    scale = np.concatenate([scale, scale], axis=-1)
    cos, sin = np.cos(freqs), np.sin(freqs)
    sin = sin * np.where(np.arange(WD) < WD // 2, -1, 1)

    def tokens(v):
        return v.reshape(NT, P, WD).transpose(1, 0, 2).reshape(P, NT * WD)

    c = dict(iota=np.broadcast_to(np.arange(NE), (P, NE)), ident=np.eye(P), headmask=p // HD == np.arange(P // HD)[None, :],
             causal=np.where(j > q, MASKED, 0), band=np.where((j2 > P + q) | (j2 < q), MASKED, 0),
             shift=j == p + 1, edge=(p == P - 1) & (j == 0),
             cos_q=tokens(cos * scale), sin_q=tokens(sin * scale),
             cos_k=tokens(cos / scale), sin_k=tokens(sin / scale))
    return np.concatenate([c[n].astype(f32) for n in CONSTS], axis=1)


def kernel(**inputs):
    import numpy as np
    import concourse.bacc as bacc
    from concourse.bass_utils import run_bass_kernel_spmd

    nc = bacc.Bacc("TRN2", target_bir_lowering=False, num_devices=1)
    arrays = layout(inputs)
    a = {n: nc.dram_tensor(f"in_{n}", v.shape, U8 if v.dtype == bool else F32, kind="ExternalInput").ap()
         for n, v in arrays.items()}
    out = nc.dram_tensor("out", (NB * TOK, D), F32, kind="ExternalOutput").ap()
    build(nc, a, out)
    r = run_bass_kernel_spmd(nc, [{f"in_{n}": v for n, v in arrays.items()}], core_ids=[0])
    return r.results[0]["out"].reshape(NB, TOK, D)
```
